# Optimizing a Trainium2 kernel written in Bass

```python
import numpy as np
import jax
import jax.numpy as jnp

def _softmax(x, axis=-1):
    return jax.nn.softmax(x, axis=axis)
def _gelu(x):
    return jax.nn.gelu(x, approximate=True)
def _silu(x):
    return jax.nn.silu(x)
def _sigmoid(x):
    return jax.nn.sigmoid(x)
def _layernorm(x, axis=-1, eps=1e-5):
    m = jnp.mean(x, axis=axis, keepdims=True)
    v = jnp.var(x, axis=axis, keepdims=True)
    return (x - m) / jnp.sqrt(v + eps)
def _scatter_add(tgt, idx, src, axis=0):
    return tgt.at[idx].add(src)
def _segment_sum(src, seg, n):
    return jax.ops.segment_sum(src, seg, n)

kernel_name = 'mk_dlrm_tower_d1_rec_fdc10d'

def setup_inputs(seed: int = 0):
    np.random.seed(seed)
    _w = jnp.asarray
    def _rec_inputs():
        import jax
        import jax.numpy as jnp
        _tk = jax.random.key(seed)
        ids = jnp.stack([jax.random.randint(jax.random.fold_in(_tk, 200 + f), (1024,), 0, v, jnp.int32) for f, v in enumerate([100000, 10000, 100000, 1000])], axis=1)
        tbl_0 = 0.05 * jax.random.normal(jax.random.fold_in(_tk, 500 + 0), (100000, 4), jnp.float32)
        tbl_1 = 0.05 * jax.random.normal(jax.random.fold_in(_tk, 500 + 1), (10000, 4), jnp.float32)
        tbl_2 = 0.05 * jax.random.normal(jax.random.fold_in(_tk, 500 + 2), (100000, 4), jnp.float32)
        tbl_3 = 0.05 * jax.random.normal(jax.random.fold_in(_tk, 500 + 3), (1000, 4), jnp.float32)
        _rk = jax.random.fold_in(_tk, 7)
        r_x = 7.22013e-05 + 1.00017 * jax.random.normal(jax.random.fold_in(_rk, 101), (1024, 2048), jnp.float32)
        W_top1 = 0.0197642 * jax.random.normal(jax.random.fold_in(_tk, 801), (2560, 512), jnp.float32)
        W_top2 = 0.0441942 * jax.random.normal(jax.random.fold_in(_tk, 802), (512, 256), jnp.float32)
        W_top3 = 0.0625 * jax.random.normal(jax.random.fold_in(_tk, 803), (256, 1), jnp.float32)
        b_top1 = jnp.zeros((512,), jnp.float32)
        b_top2 = jnp.zeros((256,), jnp.float32)
        return r_x, ids, tbl_0, tbl_1, tbl_2, tbl_3, W_top1, b_top1, W_top2, b_top2, W_top3
    r_x, ids, tbl_0, tbl_1, tbl_2, tbl_3, W_top1, b_top1, W_top2, b_top2, W_top3 = _rec_inputs()
    def _L0_rec_setup():
        import jax, jax.numpy as jnp
        import numpy as np
        B, IN, HID, D, N, OUT = (4096, 2048, 2048, 512, 4, 512)
        H = 8
        HD = D // H

        def _ln(x, g, b):
            m = x.mean(-1, keepdims=True)
            v = ((x - m) ** 2).mean(-1, keepdims=True)
            return (x - m) / jnp.sqrt(v + 1e-05) * g + b
        key = jax.random.key(seed)
        ks = jax.random.split(key, 32)

        def nrm(k, shape, scale=0.02):
            return jax.random.normal(k, shape, jnp.float32) * scale
        inp = {}
        inp['x'] = jax.random.normal(ks[0], (B, IN), jnp.float32)
        inp['strength'] = jax.random.uniform(ks[1], (B, N, N), jnp.float32)
        for t, i in (('er', 2), ('ei', 4)):
            inp[t + '_W1'] = nrm(ks[i], (HID, IN))
            inp[t + '_b1'] = jnp.zeros((HID,), jnp.float32)
            inp[t + '_g1'] = jnp.ones((HID,), jnp.float32)
            inp[t + '_be1'] = jnp.zeros((HID,), jnp.float32)
            inp[t + '_W2'] = nrm(ks[i + 1], (N * D, HID))
            inp[t + '_b2'] = jnp.zeros((N * D,), jnp.float32)
        names = ['Wq_r', 'Wq_i', 'Wk_r', 'Wk_i', 'Wv_r', 'Wv_i', 'Wo_r', 'Wo_i']
        for j, nm in enumerate(names):
            inp[nm] = nrm(ks[6 + j], (D, D))
            inp['b' + nm[1:]] = jnp.zeros((D,), jnp.float32)
        inp['int_Wr'] = jnp.tile(jnp.eye(D, dtype=jnp.float32)[None], (N, 1, 1))
        inp['int_Wi'] = jnp.zeros((N, D, D), jnp.float32)
        inp['meas_Mr'] = nrm(ks[20], (OUT, D), 1.0 / np.sqrt(D))
        inp['meas_Mi'] = nrm(ks[21], (OUT, D), 1.0 / np.sqrt(D))
        inp['post_W'] = nrm(ks[22], (OUT, OUT))
        inp['post_b'] = jnp.zeros((OUT,), jnp.float32)
        inp['post_g'] = jnp.ones((OUT,), jnp.float32)
        inp['post_be'] = jnp.zeros((OUT,), jnp.float32)
        return inp
    _L0_rec_all = _L0_rec_setup()
    _L0_rec_in = {k: v for k, v in _L0_rec_all.items() if k in ('er_W1', 'er_b1', 'er_g1', 'er_be1', 'er_W2', 'er_b2', 'ei_W1', 'ei_b1', 'ei_g1', 'ei_be1', 'ei_W2', 'ei_b2', 'Wq_r', 'bq_r', 'Wq_i', 'bq_i', 'Wk_r', 'bk_r', 'Wk_i', 'bk_i', 'Wv_r', 'bv_r', 'Wv_i', 'bv_i', 'Wo_r', 'bo_r', 'Wo_i', 'bo_i', 'int_Wr', 'int_Wi', 'meas_Mr', 'meas_Mi', 'post_W', 'post_b', 'post_g', 'post_be', )}
    del _L0_rec_all

    return {
        "r_x": r_x,
        "ids": ids,
        "tbl_0": tbl_0,
        "tbl_1": tbl_1,
        "tbl_2": tbl_2,
        "tbl_3": tbl_3,
        "W_top1": W_top1,
        "b_top1": b_top1,
        "W_top2": W_top2,
        "b_top2": b_top2,
        "W_top3": W_top3,
        "L0_rec_er_W1": _L0_rec_in["er_W1"],
        "L0_rec_er_b1": _L0_rec_in["er_b1"],
        "L0_rec_er_g1": _L0_rec_in["er_g1"],
        "L0_rec_er_be1": _L0_rec_in["er_be1"],
        "L0_rec_er_W2": _L0_rec_in["er_W2"],
        "L0_rec_er_b2": _L0_rec_in["er_b2"],
        "L0_rec_ei_W1": _L0_rec_in["ei_W1"],
        "L0_rec_ei_b1": _L0_rec_in["ei_b1"],
        "L0_rec_ei_g1": _L0_rec_in["ei_g1"],
        "L0_rec_ei_be1": _L0_rec_in["ei_be1"],
        "L0_rec_ei_W2": _L0_rec_in["ei_W2"],
        "L0_rec_ei_b2": _L0_rec_in["ei_b2"],
        "L0_rec_Wq_r": _L0_rec_in["Wq_r"],
        "L0_rec_bq_r": _L0_rec_in["bq_r"],
        "L0_rec_Wq_i": _L0_rec_in["Wq_i"],
        "L0_rec_bq_i": _L0_rec_in["bq_i"],
        "L0_rec_Wk_r": _L0_rec_in["Wk_r"],
        "L0_rec_bk_r": _L0_rec_in["bk_r"],
        "L0_rec_Wk_i": _L0_rec_in["Wk_i"],
        "L0_rec_bk_i": _L0_rec_in["bk_i"],
        "L0_rec_Wv_r": _L0_rec_in["Wv_r"],
        "L0_rec_bv_r": _L0_rec_in["bv_r"],
        "L0_rec_Wv_i": _L0_rec_in["Wv_i"],
        "L0_rec_bv_i": _L0_rec_in["bv_i"],
        "L0_rec_Wo_r": _L0_rec_in["Wo_r"],
        "L0_rec_bo_r": _L0_rec_in["bo_r"],
        "L0_rec_Wo_i": _L0_rec_in["Wo_i"],
        "L0_rec_bo_i": _L0_rec_in["bo_i"],
        "L0_rec_int_Wr": _L0_rec_in["int_Wr"],
        "L0_rec_int_Wi": _L0_rec_in["int_Wi"],
        "L0_rec_meas_Mr": _L0_rec_in["meas_Mr"],
        "L0_rec_meas_Mi": _L0_rec_in["meas_Mi"],
        "L0_rec_post_W": _L0_rec_in["post_W"],
        "L0_rec_post_b": _L0_rec_in["post_b"],
        "L0_rec_post_g": _L0_rec_in["post_g"],
        "L0_rec_post_be": _L0_rec_in["post_be"],
    }

def reference(r_x, ids, tbl_0, tbl_1, tbl_2, tbl_3, W_top1, b_top1, W_top2, b_top2, W_top3, L0_rec_er_W1, L0_rec_er_b1, L0_rec_er_g1, L0_rec_er_be1, L0_rec_er_W2, L0_rec_er_b2, L0_rec_ei_W1, L0_rec_ei_b1, L0_rec_ei_g1, L0_rec_ei_be1, L0_rec_ei_W2, L0_rec_ei_b2, L0_rec_Wq_r, L0_rec_bq_r, L0_rec_Wq_i, L0_rec_bq_i, L0_rec_Wk_r, L0_rec_bk_r, L0_rec_Wk_i, L0_rec_bk_i, L0_rec_Wv_r, L0_rec_bv_r, L0_rec_Wv_i, L0_rec_bv_i, L0_rec_Wo_r, L0_rec_bo_r, L0_rec_Wo_i, L0_rec_bo_i, L0_rec_int_Wr, L0_rec_int_Wi, L0_rec_meas_Mr, L0_rec_meas_Mi, L0_rec_post_W, L0_rec_post_b, L0_rec_post_g, L0_rec_post_be):
    import jax
    import jax.numpy as jnp
    def _L0_rec_ref(x, strength, er_W1, er_b1, er_g1, er_be1, er_W2, er_b2, ei_W1, ei_b1, ei_g1, ei_be1, ei_W2, ei_b2, Wq_r, bq_r, Wq_i, bq_i, Wk_r, bk_r, Wk_i, bk_i, Wv_r, bv_r, Wv_i, bv_i, Wo_r, bo_r, Wo_i, bo_i, int_Wr, int_Wi, meas_Mr, meas_Mi, post_W, post_b, post_g, post_be):
        import jax, jax.numpy as jnp
        import numpy as np
        B, IN, HID, D, N, OUT = (4096, 2048, 2048, 512, 4, 512)
        H = 8
        HD = D // H

        def _ln(x, g, b):
            m = x.mean(-1, keepdims=True)
            v = ((x - m) ** 2).mean(-1, keepdims=True)
            return (x - m) / jnp.sqrt(v + 1e-05) * g + b
        Bsz = x.shape[0]

        def enc(W1, b1, g, be, W2, b2):
            h = jax.nn.gelu(_ln(x @ W1.T + b1, g, be), approximate=False)
            return (h @ W2.T + b2).reshape(Bsz, N, D)
        sr = enc(er_W1, er_b1, er_g1, er_be1, er_W2, er_b2)
        si = enc(ei_W1, ei_b1, ei_g1, ei_be1, ei_W2, ei_b2)

        def heads(t):
            return t.reshape(Bsz, N, H, HD).transpose(0, 2, 1, 3)
        qr = heads(sr @ Wq_r.T + bq_r)
        qi = heads(si @ Wq_i.T + bq_i)
        kr = heads(sr @ Wk_r.T + bk_r)
        ki = heads(si @ Wk_i.T + bk_i)
        vr = heads(sr @ Wv_r.T + bv_r)
        vi = heads(si @ Wv_i.T + bv_i)
        ar = jnp.einsum('bhnd,bhmd->bhnm', qr, kr) + jnp.einsum('bhnd,bhmd->bhnm', qi, ki)
        ai = jnp.einsum('bhnd,bhmd->bhnm', qi, kr) - jnp.einsum('bhnd,bhmd->bhnm', qr, ki)
        mag = jnp.sqrt(ar ** 2 + ai ** 2 + 1e-08) * HD ** (-0.5)
        w = jax.nn.softmax(mag, axis=-1)
        out_r = jnp.einsum('bhnm,bhmd->bhnd', w, vr).transpose(0, 2, 1, 3).reshape(Bsz, N, D)
        out_i = jnp.einsum('bhnm,bhmd->bhnd', w, vi).transpose(0, 2, 1, 3).reshape(Bsz, N, D)
        attn_r = out_r @ Wo_r.T + bo_r
        attn_i = out_i @ Wo_i.T + bo_i
        R = jnp.einsum('bnd,ned->bne', attn_r, int_Wr) - jnp.einsum('bnd,ned->bne', attn_i, int_Wi)
        I = jnp.einsum('bnd,ned->bne', attn_r, int_Wi) + jnp.einsum('bnd,ned->bne', attn_i, int_Wr)
        Ri, Ii = (R[:, :, None, :], I[:, :, None, :])
        Rj, Ij = (R[:, None, :, :], I[:, None, :, :])
        phase = jnp.arctan2(Ii * Rj - Ri * Ij, Ri * Rj + Ii * Ij)
        f = jnp.cos(phase) * strength[..., None]
        sup_r = jnp.einsum('bijd,bjd->bd', f, R)
        sup_i = jnp.einsum('bijd,bjd->bd', f, I)
        norm = jnp.sqrt(jnp.sum(sup_r ** 2 + sup_i ** 2, axis=-1, keepdims=True) + 1e-08)
        sup_r = sup_r / norm
        sup_i = sup_i / norm
        mr = sup_r @ meas_Mr.T - sup_i @ meas_Mi.T
        mi = sup_r @ meas_Mi.T + sup_i @ meas_Mr.T
        amp = jnp.sqrt(mr ** 2 + mi ** 2)
        out = jax.nn.gelu(_ln(amp @ post_W.T + post_b, post_g, post_be), approximate=False)
        return out

    e = jnp.stack([tbl_0[ids[:, 0]], tbl_1[ids[:, 1]], tbl_2[ids[:, 2]], tbl_3[ids[:, 3]]], axis=1)
    z = _L0_rec_ref(r_x, e, L0_rec_er_W1, L0_rec_er_b1, L0_rec_er_g1, L0_rec_er_be1, L0_rec_er_W2, L0_rec_er_b2, L0_rec_ei_W1, L0_rec_ei_b1, L0_rec_ei_g1, L0_rec_ei_be1, L0_rec_ei_W2, L0_rec_ei_b2, L0_rec_Wq_r, L0_rec_bq_r, L0_rec_Wq_i, L0_rec_bq_i, L0_rec_Wk_r, L0_rec_bk_r, L0_rec_Wk_i, L0_rec_bk_i, L0_rec_Wv_r, L0_rec_bv_r, L0_rec_Wv_i, L0_rec_bv_i, L0_rec_Wo_r, L0_rec_bo_r, L0_rec_Wo_i, L0_rec_bo_i, L0_rec_int_Wr, L0_rec_int_Wi, L0_rec_meas_Mr, L0_rec_meas_Mi, L0_rec_post_W, L0_rec_post_b, L0_rec_post_g, L0_rec_post_be)
    z = z.reshape(z.shape[0], -1)
    h = jnp.concatenate([z, r_x], axis=1)
    h = jnp.maximum(h @ W_top1 + b_top1, 0.0)
    h = jnp.maximum(h @ W_top2 + b_top2, 0.0)
    y = h @ W_top3
    return y


_drawn_inputs = setup_inputs


def setup_inputs(seed=0):
    import zlib

    import numpy as np

    out = dict(_drawn_inputs(seed))
    spreads = {'b_top1': (0.0, 0.1),
     'b_top2': (0.0, 0.1),
     'L0_rec_er_b1': (0.0, 0.8),
     'L0_rec_er_g1': (1.0, 0.6),
     'L0_rec_er_be1': (0.0, 0.8),
     'L0_rec_er_b2': (0.0, 0.8),
     'L0_rec_ei_b1': (0.0, 0.8),
     'L0_rec_ei_g1': (1.0, 0.6),
     'L0_rec_ei_be1': (0.0, 0.8),
     'L0_rec_ei_b2': (0.0, 0.8),
     'L0_rec_bq_r': (0.0, 0.8),
     'L0_rec_bq_i': (0.0, 0.8),
     'L0_rec_bk_r': (0.0, 0.8),
     'L0_rec_bk_i': (0.0, 0.8),
     'L0_rec_bv_r': (0.0, 0.1),
     'L0_rec_bv_i': (0.0, 0.1),
     'L0_rec_bo_r': (0.0, 0.1),
     'L0_rec_bo_i': (0.0, 0.1),
     'L0_rec_int_Wi': (0.0, 0.1),
     'L0_rec_post_b': (0.0, 0.1),
     'L0_rec_post_g': (1.0, 0.2),
     'L0_rec_post_be': (0.0, 0.1)}
    factors = {'L0_rec_Wq_r': 8.0, 'L0_rec_Wq_i': 8.0, 'L0_rec_Wk_r': 8.0, 'L0_rec_Wk_i': 8.0}
    for name, (base, spread) in spreads.items():
        noise = np.random.default_rng([zlib.crc32(name.encode()), seed]).standard_normal(out[name].shape)
        drawn = base * np.exp(spread * noise) if base else spread * noise
        out[name] = jnp.asarray(drawn.astype(out[name].dtype))
    for name, factor in factors.items():
        out[name] = (out[name] * factor).astype(out[name].dtype)
    return out
```

```python
import concourse.bass as bass
from concourse import mybir
from contextlib import ExitStack

F32 = mybir.dt.float32
F32R = mybir.dt.float32r
U32 = mybir.dt.uint32
I32 = mybir.dt.int32
ALU = mybir.AluOpType
ACT = mybir.ActivationFunctionType
AX = mybir.AxisListType.X

P = 128
B = 1024
IN = 2048
HID = 2048
D = 512
N = 4
H = 8
HD = D // H
RT = B // P
KT = IN // P
DT = D // P
NB = 8
BLK = 64
NBLK = B // BLK
EPS = 1e-5


def mm3(pe, out, a_hi, a_lo, b_hi, b_lo, start, stop):
    pe.matmul(out, a_hi, b_hi, start=start, stop=False)
    pe.matmul(out, a_hi, b_lo, start=False, stop=False)
    return pe.matmul(out, a_lo, b_hi, start=False, stop=stop)


class Chip:

    def __init__(self, nc, ctx):
        self.nc = nc
        self.ctx = ctx
        self.psum = ctx.enter_context(nc.psum_tensor("psum", [P, NB, 512], F32))

    def sem(self, name):
        return self.ctx.enter_context(self.nc.semaphore(name))

    def keep(self, name, shape, dt=F32):
        return self.ctx.enter_context(self.nc.sbuf_tensor(name, shape, dt))

    def scratch(self, name, shape, dt=F32):
        return self.nc.dram_tensor(name, shape, dt, kind="Internal").ap()


def encoder_first_layer(nc, chip, t):
    CH = 9
    RING = 4
    with ExitStack() as mem:
        def sb(name, shape, dt=F32):
            return mem.enter_context(nc.sbuf_tensor(name, shape, dt))

        x_raw = sb("x_raw", [P, 2, B])
        x_hi = sb("x_hi", [P, KT, B], F32R)
        x_lo = sb("x_lo", [P, KT, B], F32R)
        w_raw = sb("w1_raw", [P, RING, 512])
        w_hi = sb("w1_hi", [P, RING, 512], F32R)
        w_lo = sb("w1_lo", [P, RING, 512], F32R)
        y = sb("y_rows", [P, RT, 512])
        bias = sb("bias1", [P, CH, 512])
        stats = sb("stats", [P, RT, CH, 6])
        ids = sb("ids_sb", [P, RT, N], I32)

        x_loaded = [chip.sem(f"a_x_loaded{i}") for i in range(2)]
        x_hi_done = chip.sem("a_x_hi_done")
        x_lo_done = chip.sem("a_x_lo_done")
        w_loaded = [chip.sem(f"a_w_loaded{i}") for i in range(RING)]
        w_hi_done = chip.sem("a_w_hi_done")
        w_lo_done = chip.sem("a_w_lo_done")
        w_used = chip.sem("a_w_used")
        acc_done = chip.sem("a_acc_done")
        y_copied = chip.sem("a_y_copied")
        y_biased = chip.sem("a_y_biased")
        y_stored = chip.sem("a_y_stored")
        stats_done = chip.sem("a_stats_done")
        var_ready = chip.sem("a_var_ready")
        std_ready = chip.sem("a_std_ready")
        bias_loaded = chip.sem("a_bias_loaded")
        ids_loaded = chip.sem("a_ids_loaded")
        gathered = chip.sem("a_gathered")
        ident_step = chip.sem("a_ident_step")

        block = mem.enter_context(nc.Block())

        @block.sync
        def _(sp):
            def load_w(c, k):
                if not (isinstance(c, int) and c == 0 and k < RING):
                    sp.wait_ge(w_lo_done, KT * c + k - RING + 1)
                sp.dma_start(w_raw[:, k % RING, :], t["w1"][c, k]).then_inc(w_loaded[k % RING], 16)

            def load_x(k):
                if k >= 2:
                    sp.wait_ge(x_lo_done, k - 1)
                sp.dma_start(x_raw[:, k % 2, :], t["xT"][k]).then_inc(x_loaded[k % 2], 16)

            for k in range(KT):
                load_x(k)
                load_w(0, k)
                if k == 1:
                    sp.dma_start(bias[:, :, :], t["b1"].partition_broadcast(P)).then_inc(bias_loaded, 16)
            with sp.Fori(1, CH) as c:
                for k in range(KT):
                    load_w(c, k)
            sp.wait_ge(gathered, 16 * RT * N)

        @block.gpsimd
        def _(pool):
            pool.memset(t["ident"][:, :], 0.0).then_inc(ident_step, 1)
            pool.wait_ge(ident_step, 1)
            pool.affine_select(out=t["ident"][:, :], in_=t["ident"][:, :], compare_op=ALU.not_equal,
                               fill=1.0, base=0, pattern=[[-1, P]], channel_multiplier=1)\
                .then_inc(ident_step, 1)
            pool.dma_start(ids[:, :, :], t["ids"].rearrange("(r p) i -> p r i", p=P)).then_inc(ids_loaded, 16)
            pool.wait_ge(ids_loaded, 16)
            for r in range(RT):
                for i in range(N):
                    pool.indirect_dma_start(
                        out=t["strength"][:, r, i * N:(i + 1) * N], out_offset=None,
                        in_=t["tables"][i],
                        in_offset=bass.IndirectOffsetOnAxis(ap=ids[:, r, i:i + 1].bitcast(U32), axis=0),
                    ).then_inc(gathered, 16)

            def store(c):
                for r in range(RT):
                    pool.wait_ge(y_biased, RT * c + r + 1)
                    pool.dma_start(t["y"][c, r], y[:, r, :]).then_inc(y_stored, 16)

            with pool.Fori(0, CH) as c:
                store(c)
            pool.wait_ge(y_stored, 16 * RT * CH)

        @block.scalar
        def _(act):
            def hi(c, k):
                act.wait_ge(w_loaded[k % RING], 16 * (KT // RING * c + k // RING + 1))
                if not (isinstance(c, int) and c == 0 and k < RING):
                    act.wait_ge(w_used, KT * c + k - RING + 1)
                act.activation(w_hi[:, k % RING, :], w_raw[:, k % RING, :], ACT.Copy).then_inc(w_hi_done, 1)

            def evacuate(c):
                act.wait_ge(y_stored, 16 * RT * c)
                for r in range(RT):
                    if r < RT - 1:
                        act.wait_ge(acc_done, (RT - 1) * c + r + 1)
                    else:
                        act.wait_ge(w_used, KT * (c + 1))
                    act.activation(y[:, r, :], chip.psum[:, r, :], ACT.Copy).then_inc(y_copied, 1)

            def chunk(c, is_first, is_last):
                for k in range(0 if is_first else 3, KT):
                    if is_first:
                        act.wait_ge(x_loaded[k % 2], 16 * (k // 2 + 1))
                        act.activation(x_hi[:, k, :], x_raw[:, k % 2, :], ACT.Copy).then_inc(x_hi_done, 1)
                    hi(c, k)
                if not is_last:
                    for k in range(3):
                        hi(c + 1, k)
                evacuate(c)

            chunk(0, True, False)
            with act.Fori(1, CH - 1) as c:
                chunk(c, False, False)
            chunk(CH - 1, False, True)
            act.wait_ge(var_ready, 1)
            act.activation(t["rstd"][:, :], t["rstd"][:, :], ACT.Sqrt).then_inc(std_ready, 1)

        @block.vector
        def _(dve):
            def lo(c, k):
                dve.wait_ge(w_hi_done, KT * c + k + 1)
                dve.tensor_tensor(w_lo[:, k % RING, :], w_raw[:, k % RING, :],
                                  w_hi[:, k % RING, :].bitcast(F32), ALU.subtract).then_inc(w_lo_done, 1)

            def add_bias(c, r):
                dve.wait_ge(y_copied, RT * c + r + 1)
                dve.tensor_tensor(y[:, r, :], y[:, r, :], bias[:, c, :], ALU.add).then_inc(y_biased, 1)

            def row_stats(c, r):
                dve.wait_ge(y_biased, RT * c + r + 1)
                dve.bn_stats(stats[:, r, c, :], y[:, r, :]).then_inc(stats_done, 1)

            def chunk(c, is_first, is_last):
                for k in range(0 if is_first else 3, KT):
                    if is_first:
                        dve.wait_ge(x_hi_done, k + 1)
                        dve.tensor_tensor(x_lo[:, k, :], x_raw[:, k % 2, :],
                                          x_hi[:, k, :].bitcast(F32), ALU.subtract).then_inc(x_lo_done, 1)
                    lo(c, k)
                if not is_last:
                    for k in range(3):
                        lo(c + 1, k)
                for r in range(RT):
                    add_bias(c, r)
                    if r:
                        row_stats(c, r - 1)
                row_stats(c, RT - 1)

            dve.wait_ge(bias_loaded, 16)
            chunk(0, True, False)
            with dve.Fori(1, CH - 1) as c:
                chunk(c, False, False)
            chunk(CH - 1, False, True)
            dve.wait_ge(stats_done, RT * CH)
            for e in range(2):
                for r in range(RT):
                    dve.bn_aggr(t["mean_var"][:, e * RT + r, :], stats[:, r, 4 * e:4 * e + 4, :]).then_inc(stats_done, 1)
            dve.wait_ge(stats_done, RT * CH + 2 * RT)
            dve.tensor_scalar(t["rstd"][:, :], t["mean_var"][:, :, 1], EPS, None, ALU.add).then_inc(var_ready, 1)
            dve.wait_ge(std_ready, 1)
            dve.reciprocal(t["rstd"][:, :], t["rstd"][:, :]).then_inc(var_ready, 1)
            dve.wait_ge(var_ready, 2)

        @block.tensor
        def _(pe):
            def chunk(c, is_first):
                for k in range(KT):
                    if is_first:
                        pe.wait_ge(x_lo_done, k + 1)
                    pe.wait_ge(w_lo_done, KT * c + k + 1)
                    for r in range(RT):
                        if k == 0 and not is_first:
                            pe.wait_ge(y_copied, RT * (c - 1) + r + 1)
                        rows = slice(r * P, (r + 1) * P)
                        mm = mm3(pe, chip.psum[:, r, :], x_hi[:, k, rows], x_lo[:, k, rows],
                                 w_hi[:, k % RING, :], w_lo[:, k % RING, :], k == 0, k == KT - 1)
                        if r == RT - 1:
                            mm.then_inc(w_used, 1)
                        elif k == KT - 1:
                            mm.then_inc(acc_done, 1)

            chunk(0, True)
            with pe.Fori(1, CH) as c:
                chunk(c, False)


def encoder_second_layer(nc, chip, t):
    RING = 4
    UNITS = 8
    with ExitStack() as mem:
        def sb(name, shape, dt=F32):
            return mem.enter_context(nc.sbuf_tensor(name, shape, dt))

        z = sb("z", [P, 2, 4, 512])
        h_raw = sb("h_raw", [P, 2, 512])
        h_hi = sb("h_hi", [P, KT, B], F32R)
        h_lo = sb("h_lo", [P, KT, B], F32R)
        w_raw = sb("w2_raw", [P, RING, 512])
        w_hi = sb("w2_hi", [P, RING, 512], F32R)
        w_lo = sb("w2_lo", [P, RING, 512], F32R)
        s_hi = sb("s_hi", [P, 4, 512], F32R)
        s_lo = sb("s_lo", [P, 4, 512], F32R)
        ln = sb("ln", [P, 2, 2, KT])
        b2 = sb("b2", [P, 2 * N * DT])
        b2_now = sb("b2_now", [P, DT])

        y_loaded = [chip.sem(f"b_y_loaded{i}") for i in range(2)]
        z_ready = chip.sem("b_z_ready")
        turned = chip.sem("b_turned")
        h_raw_done = chip.sem("b_h_raw_done")
        h_hi_done = chip.sem("b_h_hi_done")
        h_lo_done = chip.sem("b_h_lo_done")
        w_loaded = [chip.sem(f"b_w_loaded{i}") for i in range(RING)]
        w_hi_done = chip.sem("b_w_hi_done")
        w_lo_done = chip.sem("b_w_lo_done")
        w_used = chip.sem("b_w_used")
        acc_done = chip.sem("b_acc_done")
        s_hi_done = chip.sem("b_s_hi_done")
        s_lo_done = chip.sem("b_s_lo_done")
        s_stored = [chip.sem(f"b_s_stored{i}") for i in range(4)]
        consts_loaded = chip.sem("b_consts_loaded")
        b2_ready = chip.sem("b_b2_ready")

        block = mem.enter_context(nc.Block())

        @block.sync
        def _(sp):
            sp.dma_start(ln[:, :, :, :], t["ln1"]).then_inc(consts_loaded, 16)
            sp.dma_start(b2[:, :], t["b2"]).then_inc(consts_loaded, 16)

            def load_w(en, k):
                if not (isinstance(en, int) and en == 0 and k < RING):
                    sp.wait_ge(w_lo_done, KT * en + k - RING + 1)
                sp.dma_start(w_raw[:, k % RING, :], t["w2"][en, k]).then_inc(w_loaded[k % RING], 16)

            for k in range(KT):
                load_w(0, k)
            with sp.Fori(1, 2 * N) as en:
                for k in range(KT):
                    load_w(en, k)

        @block.gpsimd
        def _(pool):
            def load_y(e, u):
                if e or u >= 2:
                    pool.wait_ge(turned, 4 * (UNITS * e + u - 2) + 4)
                pool.dma_start(z[:, u % 2, :, :], t["y"][4 * e + u // 2, 4 * (u % 2):4 * (u % 2) + 4]
                               .rearrange("r p f -> p r f")).then_inc(y_loaded[u % 2], 16)

            def store(e, n):
                en = N * e + n
                for j in range(NB):
                    dt, half = j // 2, j % 2
                    pool.wait_ge(s_lo_done, NB * en + j + 1)
                    for part, src in ((0, s_hi), (1, s_lo)):
                        pool.dma_start(
                            t["sT"][part, e, half * 8:half * 8 + 8, :, dt, n, :].rearrange("b p q -> p b q"),
                            src[:, j % 4, :].rearrange("p (b q) -> p b q", q=BLK).bitcast(F32),
                        ).then_inc(s_stored[j % 4], 16)

            load_y(0, 0)
            load_y(0, 1)
            for e in range(2):
                for u in range(2, UNITS):
                    load_y(e, u)
                with pool.Fori(0, N - 1) as n:
                    store(e, n)
                if e == 0:
                    load_y(1, 0)
                    load_y(1, 1)
                store(e, N - 1)
            for slot in range(4):
                pool.wait_ge(s_stored[slot], 32 * 2 * 2 * N)

        @block.scalar
        def _(act):
            def hi(en, k):
                act.wait_ge(w_loaded[k % RING], 16 * (KT // RING * en + k // RING + 1))
                if not (isinstance(en, int) and en == 0 and k < RING):
                    act.wait_ge(w_used, KT * en + k - RING + 1)
                act.activation(w_hi[:, k % RING, :], w_raw[:, k % RING, :], ACT.Copy).then_inc(w_hi_done, 1)

            def gelu(e, u, j):
                n = 4 * (UNITS * e + u) + j
                k, half = 4 * (u // 2) + j, u % 2
                act.wait_ge(turned, n + 1)
                if n >= 2:
                    act.wait_ge(h_lo_done, n - 1)
                act.activation(h_raw[:, n % 2, :], chip.psum[:, n % NB, :], ACT.Gelu,
                               bias=ln[:, e, 1, k:k + 1], scale=ln[:, e, 0, k:k + 1]).then_inc(h_raw_done, 1)
                act.wait_ge(h_raw_done, n + 1)
                act.activation(h_hi[:, k, half * 512:(half + 1) * 512], h_raw[:, n % 2, :], ACT.Copy)\
                    .then_inc(h_hi_done, 1)

            def evacuate(en):
                act.wait_ge(b2_ready, en + 1)
                for j in range(NB):
                    if j < NB - 1:
                        act.wait_ge(acc_done, (NB - 1) * en + j + 1)
                    else:
                        act.wait_ge(w_used, KT * (en + 1))
                    act.wait_ge(s_stored[j % 4], 32 * (2 * en + j // 4))
                    act.activation(s_hi[:, j % 4, :], chip.psum[:, j, :], ACT.Identity,
                                   bias=b2_now[:, j // 2:j // 2 + 1]).then_inc(s_hi_done, 1)

            def token(en, is_last):
                for k in range(3, KT):
                    hi(en, k)
                if not is_last:
                    for k in range(3):
                        hi(en + 1, k)
                evacuate(en)

            for k in range(3):
                hi(0, k)
            act.wait_ge(consts_loaded, 32)
            for e in range(2):
                for u in range(UNITS):
                    for j in range(4):
                        gelu(e, u, j)
                with act.Fori(N * e, N * e + N - 1) as en:
                    token(en, False)
                token(N * e + N - 1, e == 1)

        @block.vector
        def _(dve):
            def lo(en, k):
                dve.wait_ge(w_hi_done, KT * en + k + 1)
                dve.tensor_tensor(w_lo[:, k % RING, :], w_raw[:, k % RING, :],
                                  w_hi[:, k % RING, :].bitcast(F32), ALU.subtract).then_inc(w_lo_done, 1)

            def normalise(e, u):
                n = UNITS * e + u
                dve.wait_ge(y_loaded[u % 2], 16 * (n // 2 + 1))
                for r in range(4):
                    row = e * RT + 4 * (u % 2) + r
                    v = dve.tensor_scalar(z[:, u % 2, r, :], z[:, u % 2, r, :], t["mean_var"][:, row, 0:1],
                                          t["rstd"][:, row:row + 1], ALU.subtract, ALU.mult)
                v.then_inc(z_ready, 1)

            def h_low(e, u, j):
                n = 4 * (UNITS * e + u) + j
                k, half = 4 * (u // 2) + j, u % 2
                cols = slice(half * 512, (half + 1) * 512)
                dve.wait_ge(h_hi_done, n + 1)
                dve.tensor_tensor(h_lo[:, k, cols], h_raw[:, n % 2, :],
                                  h_hi[:, k, cols].bitcast(F32), ALU.subtract).then_inc(h_lo_done, 1)

            def evacuate(en):
                for j in range(NB):
                    dve.wait_ge(s_hi_done, NB * en + j + 1)
                    dve.scalar_tensor_tensor(
                        out=s_lo[:, j % 4, :], in0=chip.psum[:, j, :],
                        scalar=b2_now[:, j // 2:j // 2 + 1],
                        in1=s_hi[:, j % 4, :].bitcast(F32), op0=ALU.add, op1=ALU.subtract).then_inc(s_lo_done, 1)

            def token(en, is_last):
                dve.wait_ge(s_lo_done, NB * en)
                dve.tensor_copy(b2_now[:, :], b2[:, bass.ds(DT * en, DT)]).then_inc(b2_ready, 1)
                for k in range(3, KT):
                    lo(en, k)
                if not is_last:
                    for k in range(3):
                        lo(en + 1, k)
                evacuate(en)

            for k in range(3):
                lo(0, k)
            dve.wait_ge(consts_loaded, 32)
            for e in range(2):
                normalise(e, 0)
                normalise(e, 1)
                for u in range(UNITS):
                    for j in range(4):
                        h_low(e, u, j)
                    if u + 2 < UNITS:
                        normalise(e, u + 2)
                with dve.Fori(N * e, N * e + N - 1) as en:
                    token(en, False)
                token(N * e + N - 1, e == 1)

        @block.tensor
        def _(pe):
            def turn(e, u):
                pe.wait_ge(z_ready, UNITS * e + u + 1)
                for j in range(4):
                    n = 4 * (UNITS * e + u) + j
                    if 4 * u + j >= NB:
                        pe.wait_ge(h_raw_done, n - NB + 1)
                    elif e:
                        pe.wait_ge(s_lo_done, NB * N * e)
                    for r in range(4):
                        mm = pe.transpose(chip.psum[:, n % NB, r * P:(r + 1) * P],
                                          z[:, u % 2, r, j * P:(j + 1) * P], t["ident"][:, :])
                    mm.then_inc(turned, 1)

            def token(e, en, is_first):
                for k in range(KT):
                    pe.wait_ge(w_lo_done, KT * en + k + 1)
                    if is_first:
                        if k == 0:
                            pe.wait_ge(h_raw_done, 4 * UNITS * (e + 1))
                        pe.wait_ge(h_lo_done, 4 * (UNITS * e + 2 * (k // 4) + 1) + k % 4 + 1)
                    for j in range(NB):
                        dt, half = j // 2, j % 2
                        if k == 0 and not is_first:
                            pe.wait_ge(s_lo_done, NB * (en - 1) + j + 1)
                        cols = slice(dt * P, (dt + 1) * P)
                        rows = slice(half * 512, (half + 1) * 512)
                        mm = mm3(pe, chip.psum[:, j, :], w_hi[:, k % RING, cols], w_lo[:, k % RING, cols],
                                 h_hi[:, k, rows], h_lo[:, k, rows], k == 0, k == KT - 1)
                        if j == NB - 1:
                            mm.then_inc(w_used, 1)
                        elif k == KT - 1:
                            mm.then_inc(acc_done, 1)

            for e in range(2):
                for u in range(UNITS):
                    turn(e, u)
                token(e, N * e, True)
                with pe.Fori(N * e + 1, N * e + N) as en:
                    token(e, en, False)


def split_weights(nc, chip, tag, pairs):
    SLOTS = 3
    with ExitStack() as mem:
        widest = max(n for _, _, _, n in pairs)
        raw = mem.enter_context(nc.sbuf_tensor(tag + "_raw", [P, SLOTS, widest], F32))
        loaded = [chip.sem(f"{tag}_loaded{i}") for i in range(SLOTS)]
        hi_done = chip.sem(tag + "_hi_done")
        lo_done = chip.sem(tag + "_lo_done")
        block = mem.enter_context(nc.Block())

        @block.sync
        def _(sp):
            for j, (src, _, _, n) in enumerate(pairs):
                if j >= SLOTS:
                    sp.wait_ge(lo_done, j - SLOTS + 1)
                sp.dma_start(raw[:, j % SLOTS, 0:n], src).then_inc(loaded[j % SLOTS], 16)

        @block.scalar
        def _(act):
            for j, (_, hi, _, n) in enumerate(pairs):
                act.wait_ge(loaded[j % SLOTS], 16 * (j // SLOTS + 1))
                act.activation(hi, raw[:, j % SLOTS, 0:n], ACT.Copy).then_inc(hi_done, 1)

        @block.vector
        def _(dve):
            for j, (_, hi, lo, n) in enumerate(pairs):
                dve.wait_ge(hi_done, j + 1)
                dve.tensor_tensor(lo, raw[:, j % SLOTS, 0:n], hi.bitcast(F32), ALU.subtract).then_inc(lo_done, 1)


def group(x, g):
    return x.rearrange("p n q -> p (n q)")[:, g::2]


def sum_pieces(psum, o, j):
    g, odd = j // 2, j % 2
    for half in range(2):
        lanes = slice(half * HD, (half + 1) * HD)
        src = psum[lanes, j, :].rearrange("p (d n q) -> p d n q", n=N, q=32)
        yield o[lanes, :, half ^ odd, :, g:BLK:2].rearrange("p n d q -> p d n q"), src


def attention(nc, chip, t):
    G = BLK // 32
    NV = 32
    QK = ("q_r", "k_r", "q_i", "k_i")
    with ExitStack() as mem:
        def sb(name, shape, dt=F32):
            return mem.enter_context(nc.sbuf_tensor(name, shape, dt))

        w_hi = sb("wc_hi", [P, 6, DT, 512], F32R)
        w_lo = sb("wc_lo", [P, 6, DT, 512], F32R)
        split_weights(nc, chip, "c_w", [
            (t["wqkv"][m, :, kt:kt + 2, :].rearrange("p k f -> p (k f)"),
             w_hi[:, m, kt:kt + 2, :].rearrange("p k f -> p (k f)"),
             w_lo[:, m, kt:kt + 2, :].rearrange("p k f -> p (k f)"), 1024)
            for m in range(6) for kt in (0, 2)])

        s = [[sb(f"s_{e}{part}", [P, DT, N, BLK], F32R) for part in ("hi", "lo")] for e in "ri"]
        q_r = [sb(f"q_r_{part}", [P, DT, N, BLK], F32R) for part in ("hi", "lo")]
        q_i = [sb(f"q_i_{part}", [P, DT, N, BLK], F32R) for part in ("hi", "lo")]
        k3 = [sb(f"k3_{part}", [P, DT, 3, N, BLK], F32R) for part in ("hi", "lo")]
        v = sb("v", [P, G, DT, 4, HD])
        wt = sb("wt", [P, 2 * G, DT, N * NV])
        o = [sb(f"o_{part}", [P, N, 2, DT, BLK], F32R) for part in ("hi", "lo")]
        picked = sb("picked", [P, 2, 16, NV])
        mask = sb("mask", [P, NV])
        A = G * H
        sc = sb("sc", [P, 2, A, N])
        sq = sb("sq", [P, 2, A * N])
        mag = sb("mag", [P, A, N])
        top = sb("top", [P, A])
        ex = sb("ex", [P, A, N])
        total = sb("total", [P, A])
        wgt = sb("wgt", [P, A, N])
        wgt_t = sb("wgt_t", [P, A, N])
        bqk = sb("bqk", [P, 4, DT])

        def dest(x, m, dt):
            return (q_r[x][:, dt], k3[x][:, dt, 1], q_i[x][:, dt], k3[x][:, dt, 0])[m].rearrange("p n q -> p (n q)")

        consts_loaded = chip.sem("c_consts_loaded")
        mask_done = chip.sem("c_mask_done")
        s_loaded = [chip.sem(f"c_s_loaded{e}") for e in "ri"]
        proj_done = chip.sem("c_proj_done")
        proj_hi = chip.sem("c_proj_hi")
        proj_lo = chip.sem("c_proj_lo")
        neg_done = chip.sem("c_neg_done")
        score_done = chip.sem("c_score_done")
        score_free = chip.sem("c_score_free")
        score_sum = chip.sem("c_score_sum")
        soft = chip.sem("c_soft")
        mag_ready = chip.sem("c_mag_ready")
        ex_ready = chip.sem("c_ex_ready")
        swapped = chip.sem("c_swapped")
        wt_ready = chip.sem("c_wt_ready")
        val_done = chip.sem("c_val_done")
        val_copied = chip.sem("c_val_copied")
        sum_done = chip.sem("c_sum_done")
        sum_hi = chip.sem("c_sum_hi")
        sum_lo = chip.sem("c_sum_lo")
        o_stored = chip.sem("c_o_stored")
        SOFT = 7

        block = mem.enter_context(nc.Block())

        @block.sync
        def _(sp):
            sp.dma_start(bqk[:, :, :], t["bqk"]).then_inc(consts_loaded, 16)

            def load_s(b):
                for e in range(2):
                    sp.wait_ge(val_done, 4 * b)
                    for part in range(2):
                        sp.dma_start(s[e][part][:, :, :, :].rearrange("p d n q -> p (d n q)").bitcast(F32),
                                     t["sT"][part, e, b].rearrange("p d n q -> p (d n q)"))\
                            .then_inc(s_loaded[e], 16)

            def store_o(i):
                sp.wait_ge(sum_lo, 4 + 4 * (i + 1))
                for part in range(2):
                    sp.dma_start(t["oT"][part, i].rearrange("p n e d q -> p (n e d q)"),
                                 o[part][:, :, :, :, :].rearrange("p n e d q -> p (n e d q)").bitcast(F32))\
                        .then_inc(o_stored, 16)

            load_s(0)
            with sp.Fori(0, NBLK - 1) as i:
                load_s(i + 1)
                store_o(i)
            store_o(NBLK - 1)
            sp.wait_ge(o_stored, 32 * NBLK)

        @block.tensor
        def _(pe):
            bank = chip.psum

            def projections(b, is_first):
                for j in range(8):
                    m, pair = j // 2, j % 2
                    e = m // 2
                    if j % 4 == 0:
                        pe.wait_ge(s_loaded[e], 32 * (b + 1))
                    if not is_first:
                        pe.wait_ge(score_free, 8 * (b - 1) + j + 1)
                    for d in range(2):
                        dt = 2 * pair + d
                        cols = slice(dt * P, (dt + 1) * P)
                        for kt in range(DT):
                            mm = mm3(pe, bank[:, j, d * 256:(d + 1) * 256],
                                     w_hi[:, m, kt, cols], w_lo[:, m, kt, cols],
                                     s[e][0][:, kt, :, :].rearrange("p n q -> p (n q)"),
                                     s[e][1][:, kt, :, :].rearrange("p n q -> p (n q)"), kt == 0, kt == DT - 1)
                    mm.then_inc(proj_done, 1)

            def values(b):
                for j in range(4):
                    e, g = j // 2, j % 2
                    pe.wait_ge(proj_lo, 8 * b + 4 + j + 1)
                    for kt in range(DT):
                        mm = mm3(pe, bank[:, 4 + j, :], group(s[e][0][:, kt, :, :], g), group(s[e][1][:, kt, :, :], g),
                                 w_hi[:, 4 + e, kt, :], w_lo[:, 4 + e, kt, :], kt == 0, kt == DT - 1)
                    mm.then_inc(val_done, 1)

            def scores(i):
                pe.wait_ge(neg_done, 4 * (i + 1))
                for jj in range(4):
                    g, dtp = jj // 2, jj % 2
                    for j in (2 * jj, 2 * jj + 1):
                        if j < 4:
                            pe.wait_ge(sum_lo, 4 * i + j + 1)
                        else:
                            pe.wait_ge(val_copied, 4 * i + j - 4 + 1)
                    for d in range(2):
                        dt = 2 * dtp + d
                        for n, (q, first) in enumerate(((q_r, 1), (q_i, 0))):
                            for x, y in ((0, 0), (0, 1), (1, 0)):
                                for odd in range(2):
                                    lanes = slice(odd * HD, (odd + 1) * HD)
                                    ks = k3[y][lanes, dt, first:first + 2].rearrange("p c n q -> p c (n q)")[:, :, g::2]
                                    mm = pe.matmul(bank[:, 2 * jj + odd, 256 * d:256 * d + 256],
                                                   group(q[x][lanes, dt], g), ks,
                                                   start=(n, x, y) == (0, 0, 0), stop=(n, x) == (1, 1))
                                    if (d, n, x) == (1, 1, 1):
                                        mm.then_inc(score_done, 1)

            def sums(i, has_next):
                pe.wait_ge(val_copied, 4 * (i + 1))
                for j in range(4):
                    g, odd = j // 2, j % 2
                    pe.wait_ge(wt_ready, 4 * i + j + 1)
                    if has_next:
                        pe.wait_ge(proj_lo, 8 * (i + 1) + j + 1)
                    for dt in range(DT):
                        mm = pe.matmul(bank[:, j, dt * P:(dt + 1) * P],
                                       v[:, g, dt, 2 * odd:2 * odd + 2, :].rearrange("p a d -> p (a d)"),
                                       wt[:, j, dt, :], start=True, stop=True)
                    mm.then_inc(sum_done, 1)

            projections(0, True)
            values(0)
            with pe.Fori(0, NBLK - 1) as i:
                scores(i)
                projections(i + 1, False)
                sums(i, True)
                values(i + 1)
            scores(NBLK - 1)
            sums(NBLK - 1, False)

        @block.scalar
        def _(act):
            bank = chip.psum

            def projections_hi(b):
                for j in range(8):
                    m, pair = j // 2, j % 2
                    act.wait_ge(proj_done, 8 * b + j + 1)
                    for d in range(2):
                        dt = 2 * pair + d
                        a = act.activation(dest(0, m, dt), bank[:, j, d * 256:(d + 1) * 256], ACT.Identity,
                                           bias=bqk[:, m, dt:dt + 1])
                    a.then_inc(proj_hi, 1)

            def values_copy(b):
                for j in range(4):
                    e, g = j // 2, j % 2
                    act.wait_ge(val_done, 4 * b + j + 1)
                    dst = v[:, g, :, 0:4:3, :] if e == 0 else v[:, g, :, 1:3, :]
                    act.activation(dst, bank[:, 4 + j, :].rearrange("p (h a d) -> p h a d", a=2, d=HD), ACT.Copy)\
                        .then_inc(val_copied, 1)

            def sums_hi(i):
                act.wait_ge(o_stored, 32 * i)
                for j in range(4):
                    act.wait_ge(sum_done, 4 * i + j + 1)
                    for dst, src in sum_pieces(bank, o[0], j):
                        a = act.activation(dst, src, ACT.Copy)
                    a.then_inc(sum_hi, 1)

            def softmax(i):
                act.wait_ge(soft, SOFT * i + 2)
                act.activation(mag[:, :, :], mag[:, :, :], ACT.Sqrt).then_inc(mag_ready, 1)
                act.wait_ge(soft, SOFT * i + 4)
                act.activation(ex[:, :, :], mag[:, :, :], ACT.Exp, scale=HD ** -0.5).then_inc(ex_ready, 1)

            act.wait_ge(consts_loaded, 16)
            projections_hi(0)
            values_copy(0)
            with act.Fori(0, NBLK - 1) as i:
                softmax(i)
                projections_hi(i + 1)
                sums_hi(i)
                values_copy(i + 1)
            softmax(NBLK - 1)
            sums_hi(NBLK - 1)

        @block.vector
        def _(dve):
            bank = chip.psum

            def projections_lo(b):
                for j in range(8):
                    m, pair = j // 2, j % 2
                    dve.wait_ge(proj_hi, 8 * b + j + 1)
                    for d in range(2):
                        dt = 2 * pair + d
                        a = dve.scalar_tensor_tensor(out=dest(1, m, dt), in0=bank[:, j, d * 256:(d + 1) * 256],
                                                     scalar=bqk[:, m, dt:dt + 1], in1=dest(0, m, dt).bitcast(F32),
                                                     op0=ALU.add, op1=ALU.subtract)
                    a.then_inc(proj_lo, 1)
                    if m == 3:
                        dve.wait_ge(proj_lo, 8 * b + j + 1)
                        for x in range(2):
                            k_i, k_n = (k3[x][:, 2 * pair:2 * pair + 2, c].rearrange("p d n q -> p d (n q)") for c in (0, 2))
                            dve.tensor_scalar(k_n, k_i.bitcast(F32), -1.0, None, ALU.mult).then_inc(neg_done, 1)

            def pick_scores(i):
                for j in range(9):
                    if j < 8:
                        dve.wait_ge(score_done, 8 * i + j + 1)
                        if j >= 2:
                            dve.wait_ge(score_sum, 8 * i + j - 1)
                        dve.tensor_tensor(picked[:, j % 2, :, :],
                                          bank[:, j, :].rearrange("p (m b) -> p m b", b=NV),
                                          mask[:, :].unsqueeze(1).broadcast_to((P, 16, NV)), ALU.mult)\
                            .then_inc(score_free, 1)
                    if j >= 1:
                        g, dtp, odd = (j - 1) // 4, ((j - 1) // 2) % 2, (j - 1) % 2
                        first = (g * 2 + odd) * DT + 2 * dtp
                        dve.wait_ge(score_free, 8 * i + j)
                        dve.tensor_reduce(sc[:, :, first:first + 2, :].rearrange("p c a m -> p a c m"),
                                          picked[:, (j - 1) % 2, :, :].rearrange("p (a c m) b -> p a c m b", a=2, c=2),
                                          AX, ALU.add).then_inc(score_sum, 1)

            def softmax(i):
                def flat(x):
                    return x.rearrange("p a m -> p (a m)")

                wide = (P, A, N)
                dve.wait_ge(score_sum, 8 * (i + 1))
                dve.tensor_tensor(sq[:, :, :], sc[:, :, :, :].rearrange("p c a m -> p c (a m)"),
                                  sc[:, :, :, :].rearrange("p c a m -> p c (a m)"), ALU.mult).then_inc(soft, 1)
                dve.wait_ge(soft, SOFT * i + 1)
                dve.scalar_tensor_tensor(out=flat(mag[:, :, :]), in0=sq[:, 0, :], scalar=1e-8, in1=sq[:, 1, :],
                                         op0=ALU.add, op1=ALU.add).then_inc(soft, 1)
                dve.wait_ge(mag_ready, i + 1)
                dve.tensor_reduce(top[:, :], mag[:, :, :], AX, ALU.max).then_inc(soft, 1)
                dve.wait_ge(soft, SOFT * i + 3)
                dve.tensor_tensor(mag[:, :, :], mag[:, :, :], top[:, :].unsqueeze(2).broadcast_to(wide),
                                  ALU.subtract).then_inc(soft, 1)
                dve.wait_ge(ex_ready, i + 1)
                dve.tensor_reduce(total[:, :], ex[:, :, :], AX, ALU.add).then_inc(soft, 1)
                dve.wait_ge(soft, SOFT * i + 5)
                dve.reciprocal(total[:, :], total[:, :]).then_inc(soft, 1)
                dve.wait_ge(soft, SOFT * i + 6)
                dve.tensor_tensor(wgt[:, :, :], ex[:, :, :], total[:, :].unsqueeze(2).broadcast_to(wide),
                                  ALU.mult).then_inc(soft, 1)
                dve.wait_ge(soft, SOFT * i + 7)

            def spread_weights(i):
                for n in range(N):
                    for m in range(N):
                        c = dve.tensor_copy(wgt_t[m * NV:(m + 1) * NV, :, n], wgt[n * NV:(n + 1) * NV, :, m])
                c.then_inc(swapped, 1)
                dve.wait_ge(swapped, i + 1)
                for j in range(4):
                    dve.tensor_tensor(wt[:, j, :, :].rearrange("p d (n b) -> p (d n) b", b=NV),
                                      wgt_t[:, 4 * j:4 * j + 4, :].rearrange("p a n -> p (a n)").unsqueeze(2)
                                      .broadcast_to((P, 16, NV)),
                                      mask[:, :].unsqueeze(1).broadcast_to((P, 16, NV)), ALU.mult)\
                        .then_inc(wt_ready, 1)

            def sums_lo(i):
                for j in range(4):
                    dve.wait_ge(sum_hi, 4 * i + j + 1)
                    for (lo, src), (hi, _) in zip(sum_pieces(bank, o[1], j), sum_pieces(bank, o[0], j)):
                        a = dve.tensor_tensor(lo, src, hi.bitcast(F32), ALU.subtract)
                    a.then_inc(sum_lo, 1)

            dve.sem_inc(sum_lo, 4)
            dve.tensor_reduce(mask[:, :], t["ident"][:, :].rearrange("p (m b) -> p b m", b=NV), AX, ALU.add)\
                .then_inc(mask_done, 1)
            dve.wait_ge(mask_done, 1)
            dve.wait_ge(consts_loaded, 16)
            projections_lo(0)
            with dve.Fori(0, NBLK - 1) as i:
                pick_scores(i)
                softmax(i)
                spread_weights(i)
                projections_lo(i + 1)
                sums_lo(i)
            pick_scores(NBLK - 1)
            softmax(NBLK - 1)
            spread_weights(NBLK - 1)
            sums_lo(NBLK - 1)


def interaction_products(nc, chip, t):
    HALF = B // 2
    with ExitStack() as mem:
        def sb(name, shape, dt=F32):
            return mem.enter_context(nc.sbuf_tensor(name, shape, dt))

        wo = [sb(f"wo_{part}", [P, 2, DT, 512], F32R) for part in ("hi", "lo")]
        bv = [sb(f"bv_{part}", [P, 2, DT, 2], F32R) for part in ("hi", "lo")]
        split_weights(nc, chip, "d_w", [
            (t["bv"].rearrange("p e d c -> p (e d c)"),
             bv[0][:, :, :, :].rearrange("p e d c -> p (e d c)"), bv[1][:, :, :, :].rearrange("p e d c -> p (e d c)"), 16)
        ] + [
            (t["wo"][e, :, kt:kt + 2, :].rearrange("p k f -> p (k f)"),
             wo[0][:, e, kt:kt + 2, :].rearrange("p k f -> p (k f)"),
             wo[1][:, e, kt:kt + 2, :].rearrange("p k f -> p (k f)"), 1024) for e in range(2) for kt in (0, 2)])

        o = [[sb(f"oT_{half}{part}", [P, HALF // BLK, 2, DT, BLK], F32R) for part in ("hi", "lo")] for half in range(2)]
        attn = [sb(f"attn_{part}", [P, 2, DT, HALF], F32R) for part in ("hi", "lo")]
        w_raw = sb("wi_raw", [P, 2, DT, 512])
        w = [sb(f"wi_{part}", [P, 2, DT, 512], F32R) for part in ("hi", "lo")]
        ri = sb("ri", [P, 4, 2, 512])
        rr = sb("rr", [P, 2, 512])
        bo = sb("bo", [P, 2, DT])

        consts_loaded = chip.sem("d_consts_loaded")
        bias_done = chip.sem("d_bias_done")
        bias_ready = chip.sem("d_bias_ready")
        o_loaded = [chip.sem(f"d_o_loaded{half}") for half in range(2)]
        w_loaded = chip.sem("d_w_loaded")
        w_hi = chip.sem("d_w_hi")
        w_lo = chip.sem("d_w_lo")
        attn_done = chip.sem("d_attn_done")
        attn_hi = chip.sem("d_attn_hi")
        attn_lo = chip.sem("d_attn_lo")
        ri_done = chip.sem("d_ri_done")
        rr_copied = chip.sem("d_rr_copied")
        r_done = chip.sem("d_r_done")
        i_done = chip.sem("d_i_done")
        ri_stored = [chip.sem(f"d_ri_stored{i}") for i in range(4)]

        block = mem.enter_context(nc.Block())

        @block.sync
        def _(sp):
            sp.dma_start(bo[:, :, :], t["bo"]).then_inc(consts_loaded, 16)

            def load_w(n):
                sp.wait_ge(w_lo, 8 * n)
                sp.dma_start(w_raw[:, :, :, :].rearrange("p m k f -> p (m k f)"),
                             t["wint"][n].rearrange("p m k f -> p (m k f)")).then_inc(w_loaded, 16)

            def load_o(n, half, is_first):
                if not is_first:
                    sp.wait_ge(attn_done, 8 * (2 * n + half - 1))
                for part in range(2):
                    sp.dma_start(o[half][part][:, :, :, :, :].rearrange("p b e d q -> p b (e d q)").bitcast(F32),
                                 t["oT"][part, half * 8:half * 8 + 8, :, n].rearrange("b p e d q -> p b (e d q)"))\
                        .then_inc(o_loaded[half], 16)

            load_o(0, 0, True)
            load_w(0)
            load_o(0, 1, True)
            with sp.Fori(1, N) as n:
                load_o(n, 0, False)
                load_w(n)
                load_o(n, 1, False)

        @block.gpsimd
        def _(pool):
            def store(n, half):
                u = 2 * n + half
                for r in range(4):
                    pool.wait_ge(r_done, 4 * u + r + 5)
                    pool.wait_ge(i_done, 4 * u + r + 5)
                    pool.dma_start(t["RI"][4 * half + r, :, n], ri[:, r, :, :]).then_inc(ri_stored[r], 16)

            with pool.Fori(0, N) as n:
                store(n, 0)
                store(n, 1)
            for r in range(4):
                pool.wait_ge(ri_stored[r], 16 * 2 * N)

        @block.tensor
        def _(pe):
            bank = chip.psum

            def attn_products(n, half):
                u = 2 * n + half
                pe.wait_ge(o_loaded[half], 32 * (n + 1))
                for j in range(8):
                    e, dt = j // 4, j % 4
                    pe.wait_ge(r_done, 4 * u + 3 + j // 4)
                    pe.wait_ge(i_done, 4 * u + 3 + j // 4)
                    for kt in range(DT):
                        cols = slice(dt * P, (dt + 1) * P)
                        mm = mm3(pe, bank[:, j, :], wo[0][:, e, kt, cols], wo[1][:, e, kt, cols],
                                 o[half][0][:, :, e, kt, :], o[half][1][:, :, e, kt, :], kt == 0, kt == DT - 1)
                    mm.then_inc(attn_done, 1)

            def ri_products(n, half):
                u = 2 * n + half
                pe.wait_ge(attn_lo, 8 * (u + 1))
                pe.wait_ge(w_lo, 8 * (n + 1))
                for r in range(4):
                    if r >= 2:
                        pe.wait_ge(r_done, 4 * u + r - 2 + 5)
                        pe.wait_ge(i_done, 4 * u + r - 2 + 5)
                    rows = slice(r * P, (r + 1) * P)
                    first = 4 * (r % 2)
                    for j, terms in enumerate((((0, 0),), ((1, 1),), ((0, 1), (1, 0)))):
                        for a, (e, m) in enumerate(terms):
                            for kt in range(DT):
                                mm = mm3(pe, bank[:, first + j, :], attn[0][:, e, kt, rows], attn[1][:, e, kt, rows],
                                         w[0][:, m, kt, :], w[1][:, m, kt, :],
                                         (a, kt) == (0, 0), (a, kt) == (len(terms) - 1, DT - 1))
                        mm.then_inc(ri_done, 1)

            for e in range(2):
                for dt in range(DT):
                    for kt in range(DT):
                        cols = slice(dt * P, (dt + 1) * P)
                        mm = mm3(pe, bank[:, 3, (e * DT + dt) * 2:(e * DT + dt) * 2 + 2],
                                 wo[0][:, e, kt, cols], wo[1][:, e, kt, cols],
                                 bv[0][:, e, kt, :], bv[1][:, e, kt, :], kt == 0, kt == DT - 1)
            mm.then_inc(bias_done, 1)
            pe.wait_ge(bias_ready, 1)
            with pe.Fori(0, N) as n:
                for half in range(2):
                    attn_products(n, half)
                    ri_products(n, half)

        @block.scalar
        def _(act):
            bank = chip.psum

            def unit(n, half):
                u = 2 * n + half
                if half == 0:
                    act.wait_ge(w_loaded, 16 * (n + 1))
                    act.wait_ge(ri_done, 24 * n)
                for j in range(8):
                    e, dt = j // 4, j % 4
                    if half == 0:
                        act.activation(w[0][:, e, dt, :], w_raw[:, e, dt, :], ACT.Copy).then_inc(w_hi, 1)
                    act.wait_ge(attn_done, 8 * u + j + 1)
                    act.activation(attn[0][:, e, dt, :], bank[:, j, :], ACT.Identity,
                                   bias=bo[:, e, dt:dt + 1]).then_inc(attn_hi, 1)
                for r in range(4):
                    first = 4 * (r % 2)
                    act.wait_ge(ri_done, 12 * u + 3 * r + 1)
                    act.wait_ge(r_done, 4 * u + r + 3)
                    act.activation(rr[:, r % 2, :], bank[:, first, :], ACT.Copy).then_inc(rr_copied, 1)
                    act.wait_ge(ri_stored[r], 16 * u)
                    act.wait_ge(ri_done, 12 * u + 3 * r + 3)
                    act.activation(ri[:, r, 1, :], bank[:, first + 2, :], ACT.Copy).then_inc(i_done, 1)

            act.sem_inc(i_done, 4)
            act.wait_ge(bias_ready, 1)
            with act.Fori(0, N) as n:
                unit(n, 0)
                unit(n, 1)

        @block.vector
        def _(dve):
            bank = chip.psum

            def unit(n, half):
                u = 2 * n + half
                for j in range(8):
                    e, dt = j // 4, j % 4
                    if half == 0:
                        dve.wait_ge(w_hi, 8 * n + j + 1)
                        dve.tensor_tensor(w[1][:, e, dt, :], w_raw[:, e, dt, :], w[0][:, e, dt, :].bitcast(F32),
                                          ALU.subtract).then_inc(w_lo, 1)
                    dve.wait_ge(attn_hi, 8 * u + j + 1)
                    dve.scalar_tensor_tensor(out=attn[1][:, e, dt, :], in0=bank[:, j, :],
                                             scalar=bo[:, e, dt:dt + 1], in1=attn[0][:, e, dt, :].bitcast(F32),
                                             op0=ALU.add, op1=ALU.subtract).then_inc(attn_lo, 1)
                for r in range(4):
                    first = 4 * (r % 2)
                    dve.wait_ge(rr_copied, 4 * u + r + 1)
                    dve.wait_ge(ri_stored[r], 16 * u)
                    dve.wait_ge(ri_done, 12 * u + 3 * r + 2)
                    dve.tensor_tensor(ri[:, r, 0, :], rr[:, r % 2, :], bank[:, first + 1, :],
                                      ALU.subtract).then_inc(r_done, 1)

            dve.sem_inc(r_done, 4)
            dve.wait_ge(consts_loaded, 16)
            dve.wait_ge(bias_done, 1)
            dve.tensor_tensor(bo[:, :, :].rearrange("p e d -> p (e d)"), bo[:, :, :].rearrange("p e d -> p (e d)"),
                              bank[:, 3, 0:16:2], ALU.add).then_inc(bias_ready, 1)
            dve.wait_ge(bias_ready, 1)
            with dve.Fori(0, N) as n:
                unit(n, 0)
                unit(n, 1)


def interference_and_top(nc, chip, t, out):
    PAIRS = ((0, 1), (0, 2), (0, 3), (1, 2), (1, 3), (2, 3))
    OFF = [(i, j) for i in range(N) for j in range(N) if i != j]
    with ExitStack() as mem:
        def sb(name, shape, dt=F32):
            return mem.enter_context(nc.sbuf_tensor(name, shape, dt))

        def parts(name, shape):
            return [sb(f"{name}_{part}", shape, F32R) for part in ("hi", "lo")]

        wm = parts("wm", [P, 2, DT, 512])
        wp = parts("wp", [P, DT, 512])
        w1 = parts("wt1", [P, DT, 512])
        w2 = parts("wt2", [P, DT, 256])
        pieces = []
        for m in range(2):
            for kt in (0, 2):
                pieces.append((t["wm"][m, :, kt:kt + 2, :], [x[:, m, kt:kt + 2, :] for x in wm]))
        for src, dst in ((t["wp"], wp), (t["wt1"], w1)):
            for kt in (0, 2):
                pieces.append((src[:, kt:kt + 2, :], [x[:, kt:kt + 2, :] for x in dst]))
        pieces.append((t["wt2"], [x[:, :, :] for x in w2]))
        split_weights(nc, chip, "e_w", [tuple(x.rearrange("p k f -> p (k f)") for x in (src, *dst)) + (1024,)
                                        for src, dst in pieces])

        ri = sb("ri_in", [P, 2, N, 2, 512])
        u = sb("u", [P, N, 2, 512])
        mf = sb("mf", [P, 6, 512])
        zero = sb("zero", [P, N, 512])
        prod = sb("prod", [P, 8, 512])
        sup = sb("sup", [P, 2, 512])
        sumsq = sb("sumsq", [P, 1])
        strength = sb("strength_now", [P, N * N])
        diag = sb("diag", [P, len(OFF), P])
        sup_t = [parts(f"sup_t{c}", [P, DT, P]) for c in ("r", "i", "n")]
        act_t = parts("act_t", [P, DT, P])
        raw_t = sb("raw_t", [P, DT, P])
        msq = sb("msq", [P, 2, 512])
        v = sb("v_rows", [P, 512])
        vstats = sb("vstats", [P, 6])
        vmean = sb("vmean", [P, 2])
        vstd = sb("vstd", [P, 1])
        h_x = sb("h_x", [P, 2, 512])
        h = sb("h_rows", [P, 512])
        h2 = sb("h2_rows", [P, 256])
        y = sb("y_out", [P, RT])
        y_t = sb("y_t", [RT, P])
        post_b = sb("post_b", [P, 512])
        post_ln = sb("post_ln", [P, 2, DT])
        top_b2 = sb("top_b2", [P, 256])
        top_w3 = sb("top_w3", [P, 256])

        consts_loaded = chip.sem("e_consts_loaded")
        ri_loaded = [chip.sem(f"e_ri_loaded{i}") for i in range(2)]
        hx_loaded = chip.sem("e_hx_loaded")
        strength_ready = chip.sem("e_strength_ready")
        diag_ready = chip.sem("e_diag_ready")
        squared = chip.sem("e_squared")
        norm2_ready = chip.sem("e_norm2_ready")
        root_ready = chip.sem("e_root_ready")
        unit_ready = chip.sem("e_unit_ready")
        prod_ready = chip.sem("e_prod_ready")
        cos_ready = chip.sem("e_cos_ready")
        weight_done = chip.sem("e_weight_done")
        zero_used = chip.sem("e_zero_used")
        part_ready = chip.sem("e_part_ready")
        sup_step = chip.sem("e_sup_step")
        sumsq_ready = chip.sem("e_sumsq_ready")
        norm_step = chip.sem("e_norm_step")
        norm_root = chip.sem("e_norm_root")
        sup_turned = chip.sem("e_sup_turned")
        sup_hi = chip.sem("e_sup_hi")
        sup_lo = chip.sem("e_sup_lo")
        meas_done = chip.sem("e_meas_done")
        meas_sq = chip.sem("e_meas_sq")
        amp2_ready = chip.sem("e_amp2_ready")
        amp_ready = chip.sem("e_amp_ready")
        amp_turned = chip.sem("e_amp_turned")
        amp_hi = chip.sem("e_amp_hi")
        amp_lo = chip.sem("e_amp_lo")
        post_done = chip.sem("e_post_done")
        post_step = chip.sem("e_post_step")
        std_ready = chip.sem("e_std_ready")
        z_turned = chip.sem("e_z_turned")
        z_raw = chip.sem("e_z_raw")
        z_hi = chip.sem("e_z_hi")
        z_lo = chip.sem("e_z_lo")
        top1_done = chip.sem("e_top1_done")
        h_ready = chip.sem("e_h_ready")
        h_turned = chip.sem("e_h_turned")
        h_raw = chip.sem("e_h_raw")
        h_hi = chip.sem("e_h_hi")
        h_lo = chip.sem("e_h_lo")
        top2_done = chip.sem("e_top2_done")
        out_step = chip.sem("e_out_step")
        y_turned = chip.sem("e_y_turned")
        y_ready = chip.sem("e_y_ready")
        stored = chip.sem("e_stored")

        block = mem.enter_context(nc.Block())

        @block.sync
        def _(sp):
            sp.dma_start(post_b[:, :], t["post_b"].partition_broadcast(P)).then_inc(consts_loaded, 16)
            sp.dma_start(top_b2[:, :], t["top_b2"].partition_broadcast(P)).then_inc(consts_loaded, 16)
            sp.dma_start(top_w3[:, :], t["top_w3"].partition_broadcast(P)).then_inc(consts_loaded, 16)
            sp.dma_start(post_ln[:, :, :], t["post_ln"]).then_inc(consts_loaded, 16)

            def load(r, par, is_first):
                if not is_first:
                    sp.wait_ge(part_ready, 4 * (r - 1))
                sp.dma_start(ri[:, par, :, :, :], t["RI"][r]).then_inc(ri_loaded[par], 16)

            load(0, 0, True)
            load(1, 1, True)
            with sp.Fori(1, RT // 2) as rr:
                load(2 * rr, 0, False)
                load(2 * rr + 1, 1, False)
            sp.wait_ge(y_ready, 1)
            sp.dma_start(out.rearrange("(r p) c -> r (p c)", p=P), y_t[:, :]).then_inc(stored, 16)
            sp.wait_ge(stored, 16)

        @block.gpsimd
        def _(pool):
            def load_h(r):
                pool.wait_ge(h_ready, r)
                pool.dma_start(h_x[:, 0, :], t["y"][8, r]).then_inc(hx_loaded, 16)

            with pool.Fori(0, RT) as r:
                load_h(r)

        @block.tensor
        def _(pe):
            bank = chip.psum
            ident = t["ident"]

            def spread(r, which, first):
                for n, (i, j, x) in enumerate(which):
                    last_of_all = (not first) and n == len(which) - 1
                    mm = pe.matmul(bank[:, j, :], diag[:, OFF.index((i, j)), :], x,
                                   start=first and i == min(a for a, b in OFF if b == j), stop=last_of_all,
                                   skip_group_check=True)
                return mm

            def weights_zero(r):
                pe.wait_ge(diag_ready, r + 1)
                pe.wait_ge(norm2_ready, 3 * r + 2)
                pe.wait_ge(part_ready, 4 * r)
                spread(r, [(i, j, zero[:, i, :]) for i, j in OFF], True).then_inc(zero_used, 1)

            def weights_cos(r, i):
                pe.wait_ge(cos_ready, 3 * r + i + 1)
                terms = []
                for n, (a, b) in enumerate(PAIRS):
                    if a == i:
                        terms += [(a, b, mf[:, n, :]), (b, a, mf[:, n, :])]
                mm = spread(r, terms, False)
                if i == 2:
                    mm.then_inc(weight_done, 1)

            def turn(dst, src, signal):
                for d in range(DT):
                    mm = pe.transpose(bank[:, dst, d * P:(d + 1) * P], src[:, d * P:(d + 1) * P], ident[:, :])
                mm.then_inc(signal, 1)

            def rows(dst, a, w_hi, w_lo, width, first, last):
                for kt in range(DT):
                    mm = mm3(pe, bank[:, dst, 0:width], a[0][:, kt, :], a[1][:, kt, :], w_hi[:, kt, :], w_lo[:, kt, :],
                             first and kt == 0, last and kt == DT - 1)
                return mm

            def tail_sup(r):
                pe.wait_ge(norm_step, 3 * (r + 1))
                pe.wait_ge(out_step, 3 * r)
                turn(4, sup[:, 0, :], sup_turned)
                turn(5, sup[:, 1, :], sup_turned)

            def tail_measure(r):
                pe.wait_ge(sup_lo, 3 * (r + 1))
                rows(6, sup_t[0], wm[0][:, 0], wm[1][:, 0], 512, True, False)
                rows(6, sup_t[2], wm[0][:, 1], wm[1][:, 1], 512, False, True).then_inc(meas_done, 1)
                rows(7, sup_t[0], wm[0][:, 1], wm[1][:, 1], 512, True, False)
                rows(7, sup_t[1], wm[0][:, 0], wm[1][:, 0], 512, False, True).then_inc(meas_done, 1)

            def tail_amp(r):
                pe.wait_ge(amp_ready, r + 1)
                turn(4, msq[:, 0, :], amp_turned)

            def tail_post(r):
                pe.wait_ge(amp_lo, r + 1)
                rows(5, act_t, wp[0], wp[1], 512, True, True).then_inc(post_done, 1)

            def tail_z(r):
                pe.wait_ge(post_step, 6 * (r + 1))
                turn(6, v[:, :], z_turned)

            def tail_top1(r):
                pe.wait_ge(z_lo, r + 1)
                rows(7, act_t, w1[0], w1[1], 512, True, True).then_inc(top1_done, 1)

            def tail_h(r):
                pe.wait_ge(h_ready, r + 1)
                turn(4, h[:, :], h_turned)

            def tail_top2(r):
                pe.wait_ge(h_lo, r + 1)
                rows(5, act_t, w2[0], w2[1], 256, True, True).then_inc(top2_done, 1)

            def step(r, has_head, has_tail):
                if has_tail:
                    tail_sup(r - 1)
                if has_head:
                    weights_zero(r)
                if has_tail:
                    tail_measure(r - 1)
                if has_head:
                    weights_cos(r, 0)
                if has_tail:
                    tail_amp(r - 1)
                if has_head:
                    weights_cos(r, 1)
                if has_tail:
                    tail_post(r - 1)
                if has_head:
                    weights_cos(r, 2)
                if has_tail:
                    tail_z(r - 1)
                    tail_top1(r - 1)
                    tail_h(r - 1)
                    tail_top2(r - 1)

            step(0, True, False)
            with pe.Fori(1, RT) as r:
                step(r, True, True)
            step(RT, False, True)
            pe.wait_ge(out_step, 3 * RT)
            pe.transpose(bank[0:RT, 4, 0:P], y[:, :], ident[:, :]).then_inc(y_turned, 1)

        @block.scalar
        def _(act):
            bank = chip.psum

            def head_diag(r):
                act.wait_ge(strength_ready, r + 1)
                act.wait_ge(weight_done, r)
                for n, (i, j) in enumerate(OFF):
                    a = act.activation(diag[:, n, :], t["ident"][:, :], ACT.Copy,
                                       scale=strength[:, i * N + j:i * N + j + 1])
                a.then_inc(diag_ready, 1)

            def head_squares(r, par):
                act.wait_ge(ri_loaded[par], 16 * ((r - par) // 2 + 1) if isinstance(r, int) else 8 * (r - par) + 16)
                act.wait_ge(cos_ready, 3 * r)
                act.activation(u[:, :, :, :].rearrange("p n c f -> p (n c f)"),
                               ri[:, par, :, :, :].rearrange("p n c f -> p (n c f)"), ACT.Square).then_inc(squared, 1)

            def head_root(r):
                act.wait_ge(norm2_ready, 3 * (r + 1))
                m = mf[:, 0:4, :].rearrange("p n f -> p (n f)")
                act.activation(m, m, ACT.Sqrt).then_inc(root_ready, 1)

            def tail_sumsq(r):
                act.wait_ge(sup_step, 2 * (r + 1))
                act.activation(msq[:, :, :].rearrange("p c f -> p (c f)"), sup[:, :, :].rearrange("p c f -> p (c f)"),
                               ACT.Square, accum_out=sumsq[:, :]).then_inc(sumsq_ready, 1)

            def tail_norm(r):
                act.wait_ge(norm_step, 3 * r + 1)
                act.activation(sumsq[:, :], sumsq[:, :], ACT.Sqrt).then_inc(norm_root, 1)

            def tail_sup(r):
                for c in range(2):
                    act.wait_ge(sup_turned, 2 * r + c + 1)
                    act.activation(sup_t[c][0][:, :, :].rearrange("p d q -> p (d q)"), bank[:, 4 + c, :], ACT.Copy)\
                        .then_inc(sup_hi, 1)

            def tail_measure(r):
                for c in range(2):
                    act.wait_ge(meas_done, 2 * r + c + 1)
                    act.activation(msq[:, c, :], bank[:, 6 + c, :], ACT.Square).then_inc(meas_sq, 1)

            def tail_amp(r):
                act.wait_ge(amp2_ready, r + 1)
                act.activation(msq[:, 0, :], msq[:, 0, :], ACT.Sqrt).then_inc(amp_ready, 1)
                act.wait_ge(amp_turned, r + 1)
                act.activation(act_t[0][:, :, :].rearrange("p d q -> p (d q)"), bank[:, 4, :], ACT.Copy).then_inc(amp_hi, 1)

            def tail_std(r):
                act.wait_ge(post_step, 6 * r + 4)
                act.activation(vstd[:, :], vstd[:, :], ACT.Sqrt).then_inc(std_ready, 1)

            def tail_z(r):
                act.wait_ge(z_turned, r + 1)
                for d in range(DT):
                    a = act.activation(raw_t[:, d, :], bank[:, 6, d * P:(d + 1) * P], ACT.Gelu,
                                       bias=post_ln[:, 1, d:d + 1], scale=post_ln[:, 0, d:d + 1])
                a.then_inc(z_raw, 1)
                act.wait_ge(z_raw, r + 1)
                act.activation(act_t[0][:, :, :], raw_t[:, :, :], ACT.Copy).then_inc(z_hi, 1)

            def tail_h(r):
                act.wait_ge(h_turned, r + 1)
                act.activation(raw_t[:, :, :].rearrange("p d q -> p (d q)"), bank[:, 4, :], ACT.Relu).then_inc(h_raw, 1)
                act.wait_ge(h_raw, r + 1)
                act.activation(act_t[0][:, :, :], raw_t[:, :, :], ACT.Copy).then_inc(h_hi, 1)

            def step(r, par, has_head, has_tail):
                if has_tail:
                    tail_sumsq(r - 1)
                if has_head:
                    head_diag(r)
                if has_tail:
                    tail_norm(r - 1)
                if has_head:
                    head_squares(r, par)
                if has_tail:
                    tail_sup(r - 1)
                if has_head:
                    head_root(r)
                if has_tail:
                    tail_measure(r - 1)
                    tail_amp(r - 1)
                    tail_std(r - 1)
                    tail_z(r - 1)
                    tail_h(r - 1)

            act.wait_ge(consts_loaded, 64)
            step(0, 0, True, False)
            step(1, 1, True, True)
            with act.Fori(1, RT // 2) as rr:
                step(2 * rr, 0, True, True)
                step(2 * rr + 1, 1, True, True)
            step(RT, 0, False, True)

        @block.vector
        def _(dve):
            bank = chip.psum

            def flat(x):
                return x.rearrange("p a b -> p (a b)")

            def head_strength(r):
                dve.wait_ge(part_ready, 4 * r)
                dve.wait_ge(diag_ready, r)
                dve.tensor_copy(strength[:, :], t["strength"][:, r, :]).then_inc(strength_ready, 1)

            def head_norm2(r):
                m = mf[:, 0:4, :]
                dve.wait_ge(squared, r + 1)
                dve.wait_ge(weight_done, r)
                dve.tensor_tensor(m, u[:, :, 0, :], u[:, :, 1, :], ALU.add).then_inc(norm2_ready, 1)
                dve.wait_ge(norm2_ready, 3 * r + 1)
                dve.tensor_scalar(flat(zero[:, :, :]), flat(m), 0.0, None, ALU.is_equal).then_inc(norm2_ready, 1)
                dve.wait_ge(norm2_ready, 3 * r + 2)
                dve.tensor_scalar(flat(m), flat(m), 1e-37, None, ALU.max).then_inc(norm2_ready, 1)

            def head_unit(r, par):
                m = mf[:, 0:4, :]
                dve.wait_ge(root_ready, r + 1)
                dve.reciprocal(flat(m), flat(m)).then_inc(unit_ready, 1)
                dve.wait_ge(unit_ready, 2 * r + 1)
                dve.tensor_tensor(u[:, :, :, :], ri[:, par, :, :, :], m.unsqueeze(2).broadcast_to((P, N, 2, 512)),
                                  ALU.mult).then_inc(unit_ready, 1)

            def head_cos(r, i):
                first = (0, 3, 5)[i]
                n = 3 - i
                both = prod[:, 0:2 * n, :].rearrange("p (j c) f -> p j c f", c=2)
                if i == 0:
                    dve.wait_ge(unit_ready, 2 * (r + 1))
                    dve.wait_ge(sup_step, 2 * r)
                else:
                    dve.wait_ge(cos_ready, 3 * r + i)
                dve.tensor_tensor(both, u[:, i + 1:N, :, :], u[:, i:i + 1, :, :].broadcast_to((P, n, 2, 512)),
                                  ALU.mult).then_inc(prod_ready, 1)
                dve.wait_ge(prod_ready, 3 * r + i + 1)
                dve.tensor_tensor(mf[:, first:first + n, :], both[:, :, 0, :], both[:, :, 1, :], ALU.add)\
                    .then_inc(cos_ready, 1)

            def head_part(r, par, j):
                if j == 0:
                    dve.wait_ge(weight_done, r + 1)
                    dve.wait_ge(cos_ready, 3 * (r + 1))
                for c in range(2):
                    a = dve.scalar_tensor_tensor(out=prod[:, 2 * j + c, :], in0=bank[:, j, :],
                                                 scalar=strength[:, j * N + j:j * N + j + 1],
                                                 in1=ri[:, par, j, c, :], op0=ALU.add, op1=ALU.mult)
                a.then_inc(part_ready, 1)

            def head_sup(r):
                dve.wait_ge(part_ready, 4 * (r + 1))
                dve.tensor_tensor(flat(prod[:, 0:4, :]), flat(prod[:, 0:4, :]), flat(prod[:, 4:8, :]), ALU.add)\
                    .then_inc(sup_step, 1)
                dve.wait_ge(sup_step, 2 * r + 1)
                dve.wait_ge(sup_turned, 2 * r)
                dve.tensor_tensor(flat(sup[:, :, :]), flat(prod[:, 0:2, :]), flat(prod[:, 2:4, :]), ALU.add)\
                    .then_inc(sup_step, 1)

            def tail_eps(r):
                dve.wait_ge(sumsq_ready, r + 1)
                dve.tensor_scalar(sumsq[:, :], sumsq[:, :], 1e-8, None, ALU.add).then_inc(norm_step, 1)

            def tail_scale(r):
                dve.wait_ge(norm_root, r + 1)
                dve.reciprocal(sumsq[:, :], sumsq[:, :]).then_inc(norm_step, 1)
                dve.wait_ge(norm_step, 3 * r + 2)
                dve.tensor_scalar(flat(sup[:, :, :]), flat(sup[:, :, :]), sumsq[:, :], None, ALU.mult)\
                    .then_inc(norm_step, 1)

            def tail_sup(r):
                for c in range(2):
                    dve.wait_ge(sup_hi, 2 * r + c + 1)
                    dve.tensor_tensor(flat(sup_t[c][1][:, :, :]), bank[:, 4 + c, :],
                                      flat(sup_t[c][0][:, :, :]).bitcast(F32), ALU.subtract).then_inc(sup_lo, 1)
                dve.wait_ge(sup_lo, 3 * r + 2)
                for x in range(2):
                    a = dve.tensor_scalar(flat(sup_t[2][x][:, :, :]), flat(sup_t[1][x][:, :, :]).bitcast(F32),
                                          -1.0, None, ALU.mult)
                a.then_inc(sup_lo, 1)

            def tail_amp2(r):
                dve.wait_ge(meas_sq, 2 * (r + 1))
                dve.tensor_tensor(msq[:, 0, :], msq[:, 0, :], msq[:, 1, :], ALU.add).then_inc(amp2_ready, 1)

            def tail_amp(r):
                dve.wait_ge(amp_hi, r + 1)
                dve.tensor_tensor(flat(act_t[1][:, :, :]), bank[:, 4, :], flat(act_t[0][:, :, :]).bitcast(F32),
                                  ALU.subtract).then_inc(amp_lo, 1)

            def tail_post(r):
                dve.wait_ge(post_done, r + 1)
                dve.wait_ge(z_turned, r)
                dve.tensor_tensor(v[:, :], bank[:, 5, :], post_b[:, :], ALU.add).then_inc(post_step, 1)
                dve.wait_ge(post_step, 6 * r + 1)
                dve.bn_stats(vstats[:, :], v[:, :]).then_inc(post_step, 1)

            def tail_variance(r):
                dve.bn_aggr(vmean[:, :], vstats[:, :]).then_inc(post_step, 1)
                dve.wait_ge(post_step, 6 * r + 3)
                dve.tensor_scalar(vstd[:, :], vmean[:, 1:2], EPS, None, ALU.add).then_inc(post_step, 1)

            def tail_z(r):
                dve.wait_ge(std_ready, r + 1)
                dve.reciprocal(vstd[:, :], vstd[:, :]).then_inc(post_step, 1)
                dve.wait_ge(post_step, 6 * r + 5)
                dve.tensor_scalar(v[:, :], v[:, :], vmean[:, 0:1], vstd[:, :], ALU.subtract, ALU.mult)\
                    .then_inc(post_step, 1)

            def tail_z_lo(r):
                dve.wait_ge(z_hi, r + 1)
                dve.tensor_tensor(act_t[1][:, :, :], raw_t[:, :, :], act_t[0][:, :, :].bitcast(F32),
                                  ALU.subtract).then_inc(z_lo, 1)

            def tail_h(r):
                dve.wait_ge(top1_done, r + 1)
                dve.wait_ge(hx_loaded, 16 * (r + 1))
                dve.wait_ge(h_turned, r)
                dve.tensor_tensor(h[:, :], bank[:, 7, :], h_x[:, 0, :], ALU.add).then_inc(h_ready, 1)

            def tail_h_lo(r):
                dve.wait_ge(h_hi, r + 1)
                dve.tensor_tensor(act_t[1][:, :, :], raw_t[:, :, :], act_t[0][:, :, :].bitcast(F32),
                                  ALU.subtract).then_inc(h_lo, 1)

            def tail_out(r):
                dve.wait_ge(top2_done, r + 1)
                dve.wait_ge(out_step, 3 * r)
                dve.tensor_tensor(h2[:, :], bank[:, 5, 0:256], top_b2[:, :], ALU.add).then_inc(out_step, 1)
                dve.wait_ge(out_step, 3 * r + 1)
                dve.scalar_tensor_tensor(out=h2[:, :], in0=h2[:, :], scalar=0.0, in1=top_w3[:, :],
                                         op0=ALU.max, op1=ALU.mult).then_inc(out_step, 1)
                dve.wait_ge(out_step, 3 * r + 2)
                dve.reduce_sum(y[:, bass.ds(r, 1)], h2[:, :], AX).then_inc(out_step, 1)

            def step(r, par, has_head, has_tail):
                if has_head:
                    head_strength(r)
                if has_tail:
                    tail_eps(r - 1)
                if has_tail:
                    tail_scale(r - 1)
                if has_head:
                    head_norm2(r)
                if has_tail:
                    tail_sup(r - 1)
                if has_head:
                    head_unit(r, par)
                    head_cos(r, 0)
                if has_tail:
                    tail_amp2(r - 1)
                if has_head:
                    head_cos(r, 1)
                if has_tail:
                    tail_amp(r - 1)
                if has_head:
                    head_cos(r, 2)
                if has_tail:
                    tail_post(r - 1)
                    dve.wait_ge(post_step, 6 * (r - 1) + 2)
                if has_head:
                    head_part(r, par, 0)
                if has_tail:
                    tail_variance(r - 1)
                    tail_z(r - 1)
                if has_head:
                    head_part(r, par, 1)
                    head_part(r, par, 2)
                if has_tail:
                    tail_z_lo(r - 1)
                if has_head:
                    head_part(r, par, 3)
                if has_tail:
                    tail_h(r - 1)
                if has_head:
                    head_sup(r)
                if has_tail:
                    tail_h_lo(r - 1)
                    tail_out(r - 1)

            dve.wait_ge(consts_loaded, 64)
            step(0, 0, True, False)
            step(1, 1, True, True)
            with dve.Fori(1, RT // 2) as rr:
                step(2 * rr, 0, True, True)
                step(2 * rr + 1, 1, True, True)
            step(RT, 0, False, True)
            dve.wait_ge(y_turned, 1)
            dve.tensor_copy(y_t[:, :], bank[0:RT, 4, 0:P]).then_inc(y_ready, 1)


def build(nc, d, outs, upto=9):
    with ExitStack() as ctx:
        chip = Chip(nc, ctx)
        t = dict(d)
        t["tables"] = [d["tbl_0"], d["tbl_1"], d["tbl_2"], d["tbl_3"]]
        t["ident"] = chip.keep("ident", [P, P])
        t["strength"] = chip.keep("strength", [P, RT, N * N])
        t["mean_var"] = chip.keep("mean_var", [P, 2 * RT, 2])
        t["rstd"] = chip.keep("rstd", [P, 2 * RT])
        t["y"] = chip.scratch("y_scratch", (9, RT, P, 512))
        t["sT"] = chip.scratch("sT_scratch", (2, 2, NBLK, P, DT, N, BLK))
        encoder_first_layer(nc, chip, t)
        if upto >= 2:
            encoder_second_layer(nc, chip, t)
        t["oT"] = chip.scratch("oT_scratch", (2, NBLK, P, N, 2, DT, BLK))
        if upto >= 3:
            attention(nc, chip, t)
        t["RI"] = chip.scratch("RI_scratch", (RT, P, N, 2, 512))
        if upto >= 4:
            interaction_products(nc, chip, t)
        if upto >= 5:
            interference_and_top(nc, chip, t, outs)
        return t


def host_layout(x):
    import numpy as np

    def tiles(w):
        return w.reshape(w.shape[0] // 128, 128, w.shape[1])

    def chunks(w):
        return w.reshape(w.shape[0] // 128, 128, w.shape[1] // 512, 512).transpose(2, 0, 1, 3)

    def column(v):
        return v.reshape(-1, 128).T

    L = {k[7:]: np.asarray(v) for k, v in x.items() if k.startswith("L0_rec_")}
    d = {"ids": np.asarray(x["ids"])}
    for i in range(4):
        d[f"tbl_{i}"] = np.asarray(x[f"tbl_{i}"])
    d["xT"] = tiles(np.asarray(x["r_x"]).T)
    top1 = np.asarray(x["W_top1"])
    d["w1"] = np.concatenate([chunks(L["er_W1"].T), chunks(L["ei_W1"].T), chunks(top1[512:])])
    d["b1"] = np.concatenate([L["er_b1"], L["ei_b1"], np.asarray(x["b_top1"])]).reshape(9, 512)
    d["ln1"] = np.stack([np.stack([column(L[e + "_g1"]), column(L[e + "_be1"])], 1) for e in ("er", "ei")], 1)
    d["w2"] = np.concatenate([chunks(L["er_W2"].T), chunks(L["ei_W2"].T)])
    d["b2"] = np.concatenate([column(L["er_b2"]), column(L["ei_b2"])], 1)

    def rows(w):
        return w.reshape(w.shape[0] // 128, 128, w.shape[1]).transpose(1, 0, 2)

    names = ("q_r", "k_r", "q_i", "k_i", "v_r", "v_i")
    d["wqkv"] = np.stack([rows(L["W" + m].T) for m in names])
    d["bqk"] = np.stack([column(L["b" + m]) for m in names[:4]], 1)


    def crossed(w):
        return w.reshape(4, 2, 64, -1)[:, ::-1].reshape(w.shape)

    d["wo"] = np.stack([rows(L["Wo_r"].T), rows(crossed(L["Wo_i"].T))])
    bv = np.stack([column(L["bv_r"]), column(crossed(L["bv_i"]))], 1)
    d["bv"] = np.repeat(bv[..., None], 2, -1)
    d["bo"] = np.stack([column(L["bo_r"]), column(L["bo_i"])], 1)
    wint = np.stack([L["int_Wr"], L["int_Wi"]], 1).transpose(0, 1, 3, 2)
    d["wint"] = wint.reshape(4, 2, 4, 128, 512).transpose(0, 3, 1, 2, 4)
    d["wm"] = np.stack([rows(L["meas_Mr"].T), rows(L["meas_Mi"].T)])
    d["wp"] = rows(L["post_W"].T)
    d["wt1"] = rows(top1[:512])
    d["wt2"] = rows(np.asarray(x["W_top2"]))
    d["post_b"] = L["post_b"]
    d["post_ln"] = np.stack([column(L["post_g"]), column(L["post_be"])], 1)
    d["top_b2"] = np.asarray(x["b_top2"])
    d["top_w3"] = np.asarray(x["W_top3"]).reshape(256)
    return {k: np.ascontiguousarray(v) for k, v in d.items()}


def kernel(**inputs):
    import concourse.bacc as bacc
    from concourse.bass_utils import run_bass_kernel_spmd

    arrays = host_layout(inputs)
    nc = bacc.Bacc("TRN2", target_bir_lowering=False, num_devices=1)
    d = {n: nc.dram_tensor("in_" + n, a.shape, mybir.dt.from_np(a.dtype), kind="ExternalInput").ap()
         for n, a in arrays.items()}
    out = nc.dram_tensor("out_0_dram", (B, 1), F32, kind="ExternalOutput").ap()
    build(nc, d, out)
    r = run_bass_kernel_spmd(nc, [{"in_" + n: a for n, a in arrays.items()}], core_ids=[0])
    return r.results[0]["out_0_dram"]
```

```python
import concourse.bass as bass
from concourse import mybir
from contextlib import ExitStack

F32 = mybir.dt.float32
F32R = mybir.dt.float32r
U32 = mybir.dt.uint32
I32 = mybir.dt.int32
ALU = mybir.AluOpType
ACT = mybir.ActivationFunctionType
AX = mybir.AxisListType.X

P = 128
B = 1024
IN = 2048
HID = 2048
D = 512
N = 4
H = 8
HD = D // H
RT = B // P
KT = IN // P
DT = D // P
NB = 8
BLK = 64
NBLK = B // BLK
EPS = 1e-5


def mm3(pe, out, a_hi, a_lo, b_hi, b_lo, start, stop):
    pe.matmul(out, a_hi, b_hi, start=start, stop=False)
    pe.matmul(out, a_hi, b_lo, start=False, stop=False)
    return pe.matmul(out, a_lo, b_hi, start=False, stop=stop)


class Chip:

    def __init__(self, nc, ctx):
        self.nc = nc
        self.ctx = ctx
        self.psum = ctx.enter_context(nc.psum_tensor("psum", [P, NB, 512], F32))

    def sem(self, name):
        return self.ctx.enter_context(self.nc.semaphore(name))

    def keep(self, name, shape, dt=F32):
        return self.ctx.enter_context(self.nc.sbuf_tensor(name, shape, dt))

    def scratch(self, name, shape, dt=F32):
        return self.nc.dram_tensor(name, shape, dt, kind="Internal").ap()


def encoder_first_layer(nc, chip, t):
    CH = 9
    RING = 4
    with ExitStack() as mem:
        def sb(name, shape, dt=F32):
            return mem.enter_context(nc.sbuf_tensor(name, shape, dt))

        x_raw = sb("x_raw", [P, 2, B])
        x_hi = sb("x_hi", [P, KT, B], F32R)
        x_lo = sb("x_lo", [P, KT, B], F32R)
        w_raw = sb("w1_raw", [P, RING, 512])
        w_hi = sb("w1_hi", [P, RING, 512], F32R)
        w_lo = sb("w1_lo", [P, RING, 512], F32R)
        y = sb("y_rows", [P, RT, 512])
        bias = sb("bias1", [P, CH, 512])
        stats = sb("stats", [P, RT, CH, 6])
        ids = sb("ids_sb", [P, RT, N], I32)

        x_loaded = [chip.sem(f"a_x_loaded{i}") for i in range(2)]
        x_hi_done = chip.sem("a_x_hi_done")
        x_lo_done = chip.sem("a_x_lo_done")
        w_loaded = [chip.sem(f"a_w_loaded{i}") for i in range(RING)]
        w_hi_done = chip.sem("a_w_hi_done")
        w_lo_done = chip.sem("a_w_lo_done")
        w_used = chip.sem("a_w_used")
        acc_done = chip.sem("a_acc_done")
        y_copied = chip.sem("a_y_copied")
        y_biased = chip.sem("a_y_biased")
        y_stored = chip.sem("a_y_stored")
        stats_done = chip.sem("a_stats_done")
        var_ready = chip.sem("a_var_ready")
        std_ready = chip.sem("a_std_ready")
        bias_loaded = chip.sem("a_bias_loaded")
        ids_loaded = chip.sem("a_ids_loaded")
        gathered = chip.sem("a_gathered")
        ident_step = chip.sem("a_ident_step")

        block = mem.enter_context(nc.Block())

        @block.sync
        def _(sp):
            def load_w(c, k):
                if not (isinstance(c, int) and c == 0 and k < RING):
                    sp.wait_ge(w_lo_done, KT * c + k - RING + 1)
                sp.dma_start(w_raw[:, k % RING, :], t["w1"][c, k]).then_inc(w_loaded[k % RING], 16)

            def load_x(k):
                if k >= 2:
                    sp.wait_ge(x_lo_done, k - 1)
                sp.dma_start(x_raw[:, k % 2, :], t["xT"][k]).then_inc(x_loaded[k % 2], 16)

            for k in range(KT):
                load_x(k)
                load_w(0, k)
                if k == 1:
                    sp.dma_start(bias[:, :, :], t["b1"].partition_broadcast(P)).then_inc(bias_loaded, 16)
            with sp.Fori(1, CH) as c:
                for k in range(KT):
                    load_w(c, k)
            sp.wait_ge(gathered, 16 * RT * N)

        @block.gpsimd
        def _(pool):
            pool.memset(t["ident"][:, :], 0.0).then_inc(ident_step, 1)
            pool.wait_ge(ident_step, 1)
            pool.affine_select(out=t["ident"][:, :], in_=t["ident"][:, :], compare_op=ALU.not_equal,
                               fill=1.0, base=0, pattern=[[-1, P]], channel_multiplier=1)\
                .then_inc(ident_step, 1)
            pool.dma_start(ids[:, :, :], t["ids"].rearrange("(r p) i -> p r i", p=P)).then_inc(ids_loaded, 16)
            pool.wait_ge(ids_loaded, 16)
            for r in range(RT):
                for i in range(N):
                    pool.indirect_dma_start(
                        out=t["strength"][:, r, i * N:(i + 1) * N], out_offset=None,
                        in_=t["tables"][i],
                        in_offset=bass.IndirectOffsetOnAxis(ap=ids[:, r, i:i + 1].bitcast(U32), axis=0),
                    ).then_inc(gathered, 16)

            def store(c):
                for r in range(RT):
                    pool.wait_ge(y_biased, RT * c + r + 1)
                    pool.dma_start(t["y"][c, r], y[:, r, :]).then_inc(y_stored, 16)

            with pool.Fori(0, CH) as c:
                store(c)
            pool.wait_ge(y_stored, 16 * RT * CH)

        @block.scalar
        def _(act):
            def hi(c, k):
                act.wait_ge(w_loaded[k % RING], 16 * (KT // RING * c + k // RING + 1))
                if not (isinstance(c, int) and c == 0 and k < RING):
                    act.wait_ge(w_used, KT * c + k - RING + 1)
                act.activation(w_hi[:, k % RING, :], w_raw[:, k % RING, :], ACT.Copy).then_inc(w_hi_done, 1)

            def evacuate(c):
                if not (isinstance(c, int) and c == 0):
                    act.wait_ge(y_stored, 16 * RT * c)
                for r in range(RT):
                    if r < RT - 1:
                        act.wait_ge(acc_done, (RT - 1) * c + r + 1)
                    else:
                        act.wait_ge(w_used, KT * (c + 1))
                    act.activation(y[:, r, :], chip.psum[:, r, :], ACT.Copy).then_inc(y_copied, 1)

            def chunk(c, is_first, is_last):
                for k in range(0 if is_first else 3, KT):
                    if is_first:
                        act.wait_ge(x_loaded[k % 2], 16 * (k // 2 + 1))
                        act.activation(x_hi[:, k, :], x_raw[:, k % 2, :], ACT.Copy).then_inc(x_hi_done, 1)
                    hi(c, k)
                if not is_last:
                    for k in range(3):
                        hi(c + 1, k)
                evacuate(c)

            chunk(0, True, False)
            with act.Fori(1, CH - 1) as c:
                chunk(c, False, False)
            chunk(CH - 1, False, True)
            act.wait_ge(var_ready, 1)
            act.activation(t["rstd"][:, :], t["rstd"][:, :], ACT.Sqrt).then_inc(std_ready, 1)

        @block.vector
        def _(dve):
            def lo(c, k):
                dve.wait_ge(w_hi_done, KT * c + k + 1)
                dve.tensor_tensor(w_lo[:, k % RING, :], w_raw[:, k % RING, :],
                                  w_hi[:, k % RING, :].bitcast(F32), ALU.subtract).then_inc(w_lo_done, 1)

            def add_bias(c, r):
                dve.wait_ge(y_copied, RT * c + r + 1)
                dve.tensor_tensor(y[:, r, :], y[:, r, :], bias[:, c, :], ALU.add).then_inc(y_biased, 1)

            def row_stats(c, r):
                dve.wait_ge(y_biased, RT * c + r + 1)
                dve.bn_stats(stats[:, r, c, :], y[:, r, :]).then_inc(stats_done, 1)

            def chunk(c, is_first, is_last):
                for k in range(0 if is_first else 3, KT):
                    if is_first:
                        dve.wait_ge(x_hi_done, k + 1)
                        dve.tensor_tensor(x_lo[:, k, :], x_raw[:, k % 2, :],
                                          x_hi[:, k, :].bitcast(F32), ALU.subtract).then_inc(x_lo_done, 1)
                    lo(c, k)
                if not is_last:
                    for k in range(3):
                        lo(c + 1, k)
                for r in range(RT):
                    add_bias(c, r)
                    if r:
                        row_stats(c, r - 1)
                row_stats(c, RT - 1)

            dve.wait_ge(bias_loaded, 16)
            chunk(0, True, False)
            with dve.Fori(1, CH - 1) as c:
                chunk(c, False, False)
            chunk(CH - 1, False, True)
            dve.wait_ge(stats_done, RT * CH)
            for e in range(2):
                for r in range(RT):
                    dve.bn_aggr(t["mean_var"][:, e * RT + r, :], stats[:, r, 4 * e:4 * e + 4, :]).then_inc(stats_done, 1)
            dve.wait_ge(stats_done, RT * CH + 2 * RT)
            dve.tensor_scalar(t["rstd"][:, :], t["mean_var"][:, :, 1], EPS, None, ALU.add).then_inc(var_ready, 1)
            dve.wait_ge(std_ready, 1)
            dve.reciprocal(t["rstd"][:, :], t["rstd"][:, :]).then_inc(var_ready, 1)
            dve.wait_ge(var_ready, 2)

        @block.tensor
        def _(pe):
            def chunk(c, is_first):
                for k in range(KT):
                    if is_first:
                        pe.wait_ge(x_lo_done, k + 1)
                    pe.wait_ge(w_lo_done, KT * c + k + 1)
                    for r in range(RT):
                        if k == 0 and not is_first:
                            pe.wait_ge(y_copied, RT * (c - 1) + r + 1)
                        rows = slice(r * P, (r + 1) * P)
                        mm = mm3(pe, chip.psum[:, r, :], x_hi[:, k, rows], x_lo[:, k, rows],
                                 w_hi[:, k % RING, :], w_lo[:, k % RING, :], k == 0, k == KT - 1)
                        if r == RT - 1:
                            mm.then_inc(w_used, 1)
                        elif k == KT - 1:
                            mm.then_inc(acc_done, 1)

            chunk(0, True)
            with pe.Fori(1, CH) as c:
                chunk(c, False)


def encoder_second_layer(nc, chip, t):
    RING = 4
    UNITS = 8
    PASSES = N + 1
    ACCS = 3 + 3 + 7 * (N - 1)
    with ExitStack() as mem:
        def sb(name, shape, dt=F32):
            return mem.enter_context(nc.sbuf_tensor(name, shape, dt))

        z = sb("z", [P, 2, 4, 512])
        h_raw = sb("h_raw", [P, 2, 512])
        h_hi = sb("h_hi", [P, KT, B], F32R)
        h_lo = sb("h_lo", [P, KT, B], F32R)
        w_raw = sb("w2_raw", [P, RING, 512])
        w_hi = sb("w2_hi", [P, RING, 512], F32R)
        w_lo = sb("w2_lo", [P, RING, 512], F32R)
        s_hi = sb("s_hi", [P, 4, 512], F32R)
        s_lo = sb("s_lo", [P, 4, 512], F32R)
        ln = sb("ln", [P, 2, 2, KT])
        b2 = sb("b2", [P, 2 * N * DT])
        b2_now = sb("b2_now", [P, DT])

        y_loaded = [chip.sem(f"b_y_loaded{i}") for i in range(2)]
        z_ready = chip.sem("b_z_ready")
        turned = chip.sem("b_turned")
        h_raw_done = chip.sem("b_h_raw_done")
        h_hi_done = chip.sem("b_h_hi_done")
        h_lo_done = chip.sem("b_h_lo_done")
        w_loaded = [chip.sem(f"b_w_loaded{i}") for i in range(RING)]
        w_hi_done = chip.sem("b_w_hi_done")
        w_lo_done = chip.sem("b_w_lo_done")
        w_used = chip.sem("b_w_used")
        acc_done = chip.sem("b_acc_done")
        s_hi_done = chip.sem("b_s_hi_done")
        s_lo_done = chip.sem("b_s_lo_done")
        s_stored = [chip.sem(f"b_s_stored{i}") for i in range(4)]
        consts_loaded = chip.sem("b_consts_loaded")
        b2_ready = chip.sem("b_b2_ready")

        def half_piece(h, dt):
            return 4 * h + dt, dt, dt, h

        def full_piece(i):
            return i, (i + 4) % NB, i // 2, i % 2

        def half_pieces(h):
            return [half_piece(h, dt) for dt in range(DT)]

        FULL = [full_piece(i) for i in range(NB)]

        block = mem.enter_context(nc.Block())

        @block.sync
        def _(sp):
            sp.dma_start(ln[:, :, :, :], t["ln1"]).then_inc(consts_loaded, 16)
            sp.dma_start(b2[:, :], t["b2"]).then_inc(consts_loaded, 16)

            def load_w(e, a, en, k):
                if not (isinstance(a, int) and (e, a) == (0, 0) and k < RING):
                    sp.wait_ge(w_lo_done, KT * (PASSES * e + a) + k - RING + 1)
                sp.dma_start(w_raw[:, k % RING, :], t["w2"][en, k]).then_inc(w_loaded[k % RING], 16)

            for e in range(2):
                for a in range(2):
                    for k in range(KT):
                        load_w(e, a, N * e, k)
                with sp.Fori(1, N) as n:
                    for k in range(KT):
                        load_w(e, n + 1, N * e + n, k)

        @block.gpsimd
        def _(pool):
            def load_y(e, u):
                if e or u >= 2:
                    pool.wait_ge(turned, 4 * (UNITS * e + u - 2) + 4)
                pool.dma_start(z[:, u % 2, :, :], t["y"][4 * e + u % 4, 4 * (u // 4):4 * (u // 4) + 4]
                               .rearrange("r p f -> p r f")).then_inc(y_loaded[u % 2], 16)

            def store(e, n, pieces):
                for i, _, dt, half in pieces:
                    pool.wait_ge(s_lo_done, NB * (N * e + n) + i + 1)
                    for part, src in ((0, s_hi), (1, s_lo)):
                        pool.dma_start(
                            t["sT"][part, e, half * 8:half * 8 + 8, :, dt, n, :].rearrange("b p q -> p b q"),
                            src[:, i % 4, :].rearrange("p (b q) -> p b q", q=BLK).bitcast(F32),
                        ).then_inc(s_stored[i % 4], 16)

            load_y(0, 0)
            load_y(0, 1)
            for e in range(2):
                for u in range(2, UNITS):
                    load_y(e, u)
                    if u == 6:
                        store(e, 0, half_pieces(0))
                if e == 0:
                    load_y(1, 0)
                    load_y(1, 1)
                store(e, 0, half_pieces(1))
                with pool.Fori(1, N) as n:
                    store(e, n, FULL)
            for slot in range(4):
                pool.wait_ge(s_stored[slot], 32 * 2 * 2 * N)

        @block.scalar
        def _(act):
            def hi(e, a, k):
                tile = KT * (PASSES * e + a) + k
                act.wait_ge(w_loaded[k % RING], 4 * (tile - k % RING) + 16)
                if not (isinstance(a, int) and tile < RING):
                    act.wait_ge(w_used, tile - RING + 2)
                act.activation(w_hi[:, k % RING, :], w_raw[:, k % RING, :], ACT.Copy).then_inc(w_hi_done, 1)

            def gelu(e, u, j):
                n = 4 * (UNITS * e + u) + j
                k, half = 4 * (u % 4) + j, u // 4
                act.wait_ge(turned, n + 1)
                if n >= 2:
                    act.wait_ge(h_lo_done, n - 1)
                act.activation(h_raw[:, n % 2, :], chip.psum[:, 4 + n % 4, :], ACT.Gelu,
                               bias=ln[:, e, 1, k:k + 1], scale=ln[:, e, 0, k:k + 1]).then_inc(h_raw_done, 1)
                act.wait_ge(h_raw_done, n + 1)
                act.activation(h_hi[:, k, half * 512:(half + 1) * 512], h_raw[:, n % 2, :], ACT.Copy)\
                    .then_inc(h_hi_done, 1)

            def evacuate(e, a, en, pieces, accs):
                act.wait_ge(b2_ready, en + 1)
                for x, (i, b, dt, _) in enumerate(pieces):
                    if x < len(pieces) - 1:
                        act.wait_ge(acc_done, accs + x + 1)
                    else:
                        act.wait_ge(w_used, KT * (PASSES * e + a + 1) + 1)
                    if not (isinstance(en, int) and en == 0 and i < 4):
                        act.wait_ge(s_stored[i % 4], 32 * (2 * en + i // 4))
                    act.activation(s_hi[:, i % 4, :], chip.psum[:, b, :], ACT.Identity,
                                   bias=b2_now[:, dt:dt + 1]).then_inc(s_hi_done, 1)

            def token(e, n, is_last):
                for k in range(3, KT if is_last else KT + 3):
                    hi(e, n + 1, k)
                evacuate(e, n + 1, N * e + n, FULL, ACCS * e + 7 * (n - 1) + 6)

            for k in range(3):
                hi(0, 0, k)
            act.wait_ge(consts_loaded, 32)
            for e in range(2):
                for j in range(4):
                    gelu(e, 0, j)
                for u in range(UNITS):
                    if u == 4:
                        evacuate(e, 0, N * e, half_pieces(0), ACCS * e)
                    for j in range(4):
                        if u + 1 < UNITS:
                            gelu(e, u + 1, j)
                        hi(e, 0, 4 * u + j + 3)
                evacuate(e, 1, N * e, half_pieces(1), ACCS * e + 3)
                with act.Fori(1, N - e) as n:
                    token(e, n, False)
                if e:
                    token(e, N - 1, True)

        @block.vector
        def _(dve):
            def lo(tile, k):
                dve.wait_ge(w_hi_done, tile + 1)
                dve.tensor_tensor(w_lo[:, k % RING, :], w_raw[:, k % RING, :],
                                  w_hi[:, k % RING, :].bitcast(F32), ALU.subtract).then_inc(w_lo_done, 1)

            def normalise(e, u):
                n = UNITS * e + u
                dve.wait_ge(y_loaded[u % 2], 16 * (n // 2 + 1))
                for r in range(4):
                    row = e * RT + 4 * (u // 4) + r
                    v = dve.tensor_scalar(z[:, u % 2, r, :], z[:, u % 2, r, :], t["mean_var"][:, row, 0:1],
                                          t["rstd"][:, row:row + 1], ALU.subtract, ALU.mult)
                v.then_inc(z_ready, 1)

            def h_low(e, u, j):
                n = 4 * (UNITS * e + u) + j
                k, half = 4 * (u % 4) + j, u // 4
                cols = slice(half * 512, (half + 1) * 512)
                dve.wait_ge(h_hi_done, n + 1)
                dve.tensor_tensor(h_lo[:, k, cols], h_raw[:, n % 2, :],
                                  h_hi[:, k, cols].bitcast(F32), ALU.subtract).then_inc(h_lo_done, 1)

            def take_bias(en):
                dve.tensor_copy(b2_now[:, :], b2[:, bass.ds(DT * en, DT)]).then_inc(b2_ready, 1)
                dve.wait_ge(b2_ready, en + 1)

            def evacuate(en, pieces):
                for i, b, dt, _ in pieces:
                    dve.wait_ge(s_hi_done, NB * en + i + 1)
                    dve.scalar_tensor_tensor(
                        out=s_lo[:, i % 4, :], in0=chip.psum[:, b, :],
                        scalar=b2_now[:, dt:dt + 1],
                        in1=s_hi[:, i % 4, :].bitcast(F32), op0=ALU.add, op1=ALU.subtract).then_inc(s_lo_done, 1)

            def token(e, n, is_last):
                en = N * e + n
                take_bias(en)
                for k in range(3, KT if is_last else KT + 3):
                    lo(KT * (PASSES * e + n + 1) + k, k)
                evacuate(en, FULL)
                dve.wait_ge(s_lo_done, NB * (en + 1))

            for k in range(3):
                lo(k, k)
            dve.wait_ge(consts_loaded, 32)
            normalise(0, 0)
            normalise(0, 1)
            for e in range(2):
                take_bias(N * e)
                for j in range(4):
                    h_low(e, 0, j)
                normalise(e, 2)
                for u in range(UNITS):
                    if u == 4:
                        evacuate(N * e, half_pieces(0))
                    for j in range(4):
                        if u + 1 < UNITS:
                            h_low(e, u + 1, j)
                        lo(KT * PASSES * e + 4 * u + j + 3, 4 * u + j + 3)
                    if u + 3 < UNITS:
                        normalise(e, u + 3)
                evacuate(N * e, half_pieces(1))
                dve.wait_ge(s_lo_done, NB * (N * e + 1))
                if e == 0:
                    normalise(1, 0)
                    normalise(1, 1)
                with dve.Fori(1, N - e) as n:
                    token(e, n, False)
                if e:
                    token(e, N - 1, True)

        @block.tensor
        def _(pe):
            def turn(e, u):
                pe.wait_ge(z_ready, UNITS * e + u + 1)
                for j in range(4):
                    n = 4 * (UNITS * e + u) + j
                    if u:
                        pe.wait_ge(h_raw_done, n - 4 + 1)
                    elif e:
                        pe.wait_ge(s_lo_done, NB * N * e - NB + j + 1)
                    for r in range(4):
                        mm = pe.transpose(chip.psum[:, 4 + j, r * P:(r + 1) * P],
                                          z[:, u % 2, r, j * P:(j + 1) * P], t["ident"][:, :])
                    mm.then_inc(turned, 1)

            def products(k, pieces, wait_for_bank=None):
                for x, (i, b, dt, half) in enumerate(pieces):
                    if k == 0 and wait_for_bank:
                        wait_for_bank(i, b)
                    cols = slice(dt * P, (dt + 1) * P)
                    rows = slice(half * 512, (half + 1) * 512)
                    mm = mm3(pe, chip.psum[:, b, :], w_hi[:, k % RING, cols], w_lo[:, k % RING, cols],
                             h_hi[:, k, rows], h_lo[:, k, rows], k == 0, k == KT - 1)
                    if x == len(pieces) - 1:
                        mm.then_inc(w_used, 1)
                    elif k == KT - 1:
                        mm.then_inc(acc_done, 1)

            def half_products(e, u):
                h = u // 4
                for j in range(4):
                    k = 4 * (u % 4) + j
                    pe.wait_ge(w_lo_done, KT * (PASSES * e + h) + k + 1)
                    pe.wait_ge(h_lo_done, 4 * (UNITS * e + u) + j + 1)
                    if k == 0 and (e or h):
                        pe.wait_ge(s_lo_done, NB * N * e + 4 * h)
                    products(k, half_pieces(h))

            def token(e, n, is_first):
                def bank_free(i, b):
                    if not is_first:
                        pe.wait_ge(s_lo_done, NB * (N * e + n - 1) + i + 1)
                    elif b < 4:
                        pe.wait_ge(s_lo_done, NB * N * e + 4 + b + 1)
                    else:
                        pe.wait_ge(h_raw_done, 4 * UNITS * (e + 1))

                for k in range(KT):
                    pe.wait_ge(w_lo_done, KT * (PASSES * e + n + 1) + k + 1)
                    products(k, FULL, bank_free)

            pe.sem_inc(w_used, 1)
            for e in range(2):
                turn(e, 0)
                for u in range(UNITS):
                    if u + 1 < UNITS:
                        turn(e, u + 1)
                    half_products(e, u)
                token(e, 1, True)
                with pe.Fori(2, N) as n:
                    token(e, n, False)


def split_weights(nc, chip, tag, pairs):
    SLOTS = 3
    with ExitStack() as mem:
        widest = max(n for _, _, _, n in pairs)
        raw = mem.enter_context(nc.sbuf_tensor(tag + "_raw", [P, SLOTS, widest], F32))
        loaded = [chip.sem(f"{tag}_loaded{i}") for i in range(SLOTS)]
        hi_done = chip.sem(tag + "_hi_done")
        lo_done = chip.sem(tag + "_lo_done")
        block = mem.enter_context(nc.Block())

        @block.sync
        def _(sp):
            for j, (src, _, _, n) in enumerate(pairs):
                if j >= SLOTS:
                    sp.wait_ge(lo_done, j - SLOTS + 1)
                sp.dma_start(raw[:, j % SLOTS, 0:n], src).then_inc(loaded[j % SLOTS], 16)

        @block.scalar
        def _(act):
            for j, (_, hi, _, n) in enumerate(pairs):
                act.wait_ge(loaded[j % SLOTS], 16 * (j // SLOTS + 1))
                act.activation(hi, raw[:, j % SLOTS, 0:n], ACT.Copy).then_inc(hi_done, 1)

        @block.vector
        def _(dve):
            for j, (_, hi, lo, n) in enumerate(pairs):
                dve.wait_ge(hi_done, j + 1)
                dve.tensor_tensor(lo, raw[:, j % SLOTS, 0:n], hi.bitcast(F32), ALU.subtract).then_inc(lo_done, 1)


def group(x, g):
    return x.rearrange("p n q -> p (n q)")[:, g::2]


def sum_pieces(psum, o, j):
    g, odd = j // 2, j % 2
    for half in range(2):
        lanes = slice(half * HD, (half + 1) * HD)
        src = psum[lanes, j, :].rearrange("p (d n q) -> p d n q", n=N, q=32)
        yield o[lanes, :, half ^ odd, :, g:BLK:2].rearrange("p n d q -> p d n q"), src


def attention(nc, chip, t):
    G = BLK // 32
    NV = 32
    QK = ("q_r", "k_r", "q_i", "k_i")
    with ExitStack() as mem:
        def sb(name, shape, dt=F32):
            return mem.enter_context(nc.sbuf_tensor(name, shape, dt))

        w_hi = sb("wc_hi", [P, 6, DT, 512], F32R)
        w_lo = sb("wc_lo", [P, 6, DT, 512], F32R)
        split_weights(nc, chip, "c_w", [
            (t["wqkv"][m, :, kt:kt + 2, :].rearrange("p k f -> p (k f)"),
             w_hi[:, m, kt:kt + 2, :].rearrange("p k f -> p (k f)"),
             w_lo[:, m, kt:kt + 2, :].rearrange("p k f -> p (k f)"), 1024)
            for m in range(6) for kt in (0, 2)])

        s = [[sb(f"s_{e}{part}", [P, DT, N, BLK], F32R) for part in ("hi", "lo")] for e in "ri"]
        q_r = [sb(f"q_r_{part}", [P, DT, N, BLK], F32R) for part in ("hi", "lo")]
        q_i = [sb(f"q_i_{part}", [P, DT, N, BLK], F32R) for part in ("hi", "lo")]
        k3 = [sb(f"k3_{part}", [P, DT, 3, N, BLK], F32R) for part in ("hi", "lo")]
        v = sb("v", [P, G, DT, 4, HD])
        wt = sb("wt", [P, 2 * G, DT, N * NV])
        o = [sb(f"o_{part}", [P, N, 2, DT, BLK], F32R) for part in ("hi", "lo")]
        picked = sb("picked", [P, 2, 16, NV])
        mask = sb("mask", [P, NV])
        A = G * H
        sc = sb("sc", [P, 2, A, N])
        sq = sb("sq", [P, 2, A * N])
        mag = sb("mag", [P, A, N])
        top = sb("top", [P, A])
        ex = sb("ex", [P, A, N])
        total = sb("total", [P, A])
        wgt = sb("wgt", [P, A, N])
        wgt_t = sb("wgt_t", [P, A, N])
        bqk = sb("bqk", [P, 4, DT])

        def dest(x, m, dt):
            return (q_r[x][:, dt], k3[x][:, dt, 1], q_i[x][:, dt], k3[x][:, dt, 0])[m].rearrange("p n q -> p (n q)")

        consts_loaded = chip.sem("c_consts_loaded")
        mask_done = chip.sem("c_mask_done")
        s_loaded = [chip.sem(f"c_s_loaded{e}") for e in "ri"]
        proj_done = chip.sem("c_proj_done")
        proj_hi = chip.sem("c_proj_hi")
        proj_lo = chip.sem("c_proj_lo")
        neg_done = chip.sem("c_neg_done")
        score_done = chip.sem("c_score_done")
        score_free = chip.sem("c_score_free")
        score_sum = chip.sem("c_score_sum")
        soft = chip.sem("c_soft")
        mag_ready = chip.sem("c_mag_ready")
        ex_ready = chip.sem("c_ex_ready")
        swapped = chip.sem("c_swapped")
        wt_ready = chip.sem("c_wt_ready")
        val_done = chip.sem("c_val_done")
        val_copied = chip.sem("c_val_copied")
        sum_done = chip.sem("c_sum_done")
        sum_hi = chip.sem("c_sum_hi")
        sum_lo = chip.sem("c_sum_lo")
        o_stored = chip.sem("c_o_stored")
        SOFT = 7

        block = mem.enter_context(nc.Block())

        @block.sync
        def _(sp):
            sp.dma_start(bqk[:, :, :], t["bqk"]).then_inc(consts_loaded, 16)

            def load_s(b):
                for e in range(2):
                    if not (isinstance(b, int) and b == 0):
                        sp.wait_ge(val_done, 4 * b)
                    for part in range(2):
                        sp.dma_start(s[e][part][:, :, :, :].rearrange("p d n q -> p (d n q)").bitcast(F32),
                                     t["sT"][part, e, b].rearrange("p d n q -> p (d n q)"))\
                            .then_inc(s_loaded[e], 16)

            def store_o(i):
                sp.wait_ge(sum_lo, 4 + 4 * (i + 1))
                for part in range(2):
                    sp.dma_start(t["oT"][part, i].rearrange("p n e d q -> p (n e d q)"),
                                 o[part][:, :, :, :, :].rearrange("p n e d q -> p (n e d q)").bitcast(F32))\
                        .then_inc(o_stored, 16)

            sp.sem_inc(o_stored, 32)
            load_s(0)
            with sp.Fori(0, NBLK - 1) as i:
                load_s(i + 1)
                store_o(i)
            store_o(NBLK - 1)
            sp.wait_ge(o_stored, 32 * (NBLK + 1))

        @block.tensor
        def _(pe):
            bank = chip.psum

            def projections(b, is_first):
                for j in range(8):
                    m, pair = j // 2, j % 2
                    e = m // 2
                    if j % 4 == 0:
                        pe.wait_ge(s_loaded[e], 32 * (b + 1))
                    if not is_first:
                        pe.wait_ge(score_free, 8 * (b - 1) + j + 1)
                    for d in range(2):
                        dt = 2 * pair + d
                        cols = slice(dt * P, (dt + 1) * P)
                        for kt in range(DT):
                            mm = mm3(pe, bank[:, j, d * 256:(d + 1) * 256],
                                     w_hi[:, m, kt, cols], w_lo[:, m, kt, cols],
                                     s[e][0][:, kt, :, :].rearrange("p n q -> p (n q)"),
                                     s[e][1][:, kt, :, :].rearrange("p n q -> p (n q)"), kt == 0, kt == DT - 1)
                    mm.then_inc(proj_done, 1)

            def values(b):
                for j in range(4):
                    e, g = j // 2, j % 2
                    pe.wait_ge(proj_lo, 8 * b + 4 + j + 1)
                    for kt in range(DT):
                        mm = mm3(pe, bank[:, 4 + j, :], group(s[e][0][:, kt, :, :], g), group(s[e][1][:, kt, :, :], g),
                                 w_hi[:, 4 + e, kt, :], w_lo[:, 4 + e, kt, :], kt == 0, kt == DT - 1)
                    mm.then_inc(val_done, 1)

            def scores(i):
                pe.wait_ge(neg_done, 4 * (i + 1))
                for jj in range(4):
                    g, dtp = jj // 2, jj % 2
                    for j in (2 * jj, 2 * jj + 1):
                        if j < 4:
                            pe.wait_ge(sum_lo, 4 * i + j + 1)
                        else:
                            pe.wait_ge(val_copied, 4 * i + j - 4 + 1)
                    for d in range(2):
                        dt = 2 * dtp + d
                        for n, (q, first) in enumerate(((q_r, 1), (q_i, 0))):
                            for x, y in ((0, 0), (0, 1), (1, 0)):
                                for odd in range(2):
                                    lanes = slice(odd * HD, (odd + 1) * HD)
                                    ks = k3[y][lanes, dt, first:first + 2].rearrange("p c n q -> p c (n q)")[:, :, g::2]
                                    mm = pe.matmul(bank[:, 2 * jj + odd, 256 * d:256 * d + 256],
                                                   group(q[x][lanes, dt], g), ks,
                                                   start=(n, x, y) == (0, 0, 0), stop=(n, x) == (1, 1))
                                    if (d, n, x) == (1, 1, 1):
                                        mm.then_inc(score_done, 1)

            def sums(i, has_next):
                pe.wait_ge(val_copied, 4 * (i + 1))
                for j in range(4):
                    g, odd = j // 2, j % 2
                    pe.wait_ge(wt_ready, 4 * i + j + 1)
                    if has_next:
                        pe.wait_ge(proj_lo, 8 * (i + 1) + j + 1)
                    for dt in range(DT):
                        mm = pe.matmul(bank[:, j, dt * P:(dt + 1) * P],
                                       v[:, g, dt, 2 * odd:2 * odd + 2, :].rearrange("p a d -> p (a d)"),
                                       wt[:, j, dt, :], start=True, stop=True)
                    mm.then_inc(sum_done, 1)

            projections(0, True)
            values(0)
            with pe.Fori(0, NBLK - 1) as i:
                scores(i)
                projections(i + 1, False)
                sums(i, True)
                values(i + 1)
            scores(NBLK - 1)
            sums(NBLK - 1, False)

        @block.scalar
        def _(act):
            bank = chip.psum

            def projections_hi(b):
                for j in range(8):
                    m, pair = j // 2, j % 2
                    act.wait_ge(proj_done, 8 * b + j + 1)
                    for d in range(2):
                        dt = 2 * pair + d
                        a = act.activation(dest(0, m, dt), bank[:, j, d * 256:(d + 1) * 256], ACT.Identity,
                                           bias=bqk[:, m, dt:dt + 1])
                    a.then_inc(proj_hi, 1)

            def values_copy(b):
                for j in range(4):
                    e, g = j // 2, j % 2
                    act.wait_ge(val_done, 4 * b + j + 1)
                    dst = v[:, g, :, 0:4:3, :] if e == 0 else v[:, g, :, 1:3, :]
                    act.activation(dst, bank[:, 4 + j, :].rearrange("p (h a d) -> p h a d", a=2, d=HD), ACT.Copy)\
                        .then_inc(val_copied, 1)

            def sums_hi(i):
                act.wait_ge(o_stored, 32 * (i + 1))
                for j in range(4):
                    act.wait_ge(sum_done, 4 * i + j + 1)
                    for dst, src in sum_pieces(bank, o[0], j):
                        a = act.activation(dst, src, ACT.Copy)
                    a.then_inc(sum_hi, 1)

            def softmax(i):
                act.wait_ge(soft, SOFT * i + 2)
                act.activation(mag[:, :, :], mag[:, :, :], ACT.Sqrt).then_inc(mag_ready, 1)
                act.wait_ge(soft, SOFT * i + 4)
                act.activation(ex[:, :, :], mag[:, :, :], ACT.Exp, scale=HD ** -0.5).then_inc(ex_ready, 1)

            act.wait_ge(consts_loaded, 16)
            projections_hi(0)
            values_copy(0)
            with act.Fori(0, NBLK - 1) as i:
                softmax(i)
                projections_hi(i + 1)
                sums_hi(i)
                values_copy(i + 1)
            softmax(NBLK - 1)
            sums_hi(NBLK - 1)

        @block.vector
        def _(dve):
            bank = chip.psum

            def projections_lo(b):
                for j in range(8):
                    m, pair = j // 2, j % 2
                    dve.wait_ge(proj_hi, 8 * b + j + 1)
                    for d in range(2):
                        dt = 2 * pair + d
                        a = dve.scalar_tensor_tensor(out=dest(1, m, dt), in0=bank[:, j, d * 256:(d + 1) * 256],
                                                     scalar=bqk[:, m, dt:dt + 1], in1=dest(0, m, dt).bitcast(F32),
                                                     op0=ALU.add, op1=ALU.subtract)
                    a.then_inc(proj_lo, 1)
                    if m == 3:
                        dve.wait_ge(proj_lo, 8 * b + j + 1)
                        for x in range(2):
                            k_i, k_n = (k3[x][:, 2 * pair:2 * pair + 2, c].rearrange("p d n q -> p d (n q)") for c in (0, 2))
                            dve.tensor_scalar(k_n, k_i.bitcast(F32), -1.0, None, ALU.mult).then_inc(neg_done, 1)

            def pick_scores(i):
                for j in range(9):
                    if j < 8:
                        dve.wait_ge(score_done, 8 * i + j + 1)
                        if j >= 2:
                            dve.wait_ge(score_sum, 8 * i + j - 1)
                        dve.tensor_tensor(picked[:, j % 2, :, :],
                                          bank[:, j, :].rearrange("p (m b) -> p m b", b=NV),
                                          mask[:, :].unsqueeze(1).broadcast_to((P, 16, NV)), ALU.mult)\
                            .then_inc(score_free, 1)
                    if j >= 1:
                        g, dtp, odd = (j - 1) // 4, ((j - 1) // 2) % 2, (j - 1) % 2
                        first = (g * 2 + odd) * DT + 2 * dtp
                        dve.wait_ge(score_free, 8 * i + j)
                        dve.tensor_reduce(sc[:, :, first:first + 2, :].rearrange("p c a m -> p a c m"),
                                          picked[:, (j - 1) % 2, :, :].rearrange("p (a c m) b -> p a c m b", a=2, c=2),
                                          AX, ALU.add).then_inc(score_sum, 1)

            def softmax(i):
                def flat(x):
                    return x.rearrange("p a m -> p (a m)")

                wide = (P, A, N)
                dve.wait_ge(score_sum, 8 * (i + 1))
                dve.tensor_tensor(sq[:, :, :], sc[:, :, :, :].rearrange("p c a m -> p c (a m)"),
                                  sc[:, :, :, :].rearrange("p c a m -> p c (a m)"), ALU.mult).then_inc(soft, 1)
                dve.wait_ge(soft, SOFT * i + 1)
                dve.scalar_tensor_tensor(out=flat(mag[:, :, :]), in0=sq[:, 0, :], scalar=1e-8, in1=sq[:, 1, :],
                                         op0=ALU.add, op1=ALU.add).then_inc(soft, 1)
                dve.wait_ge(mag_ready, i + 1)
                dve.tensor_reduce(top[:, :], mag[:, :, :], AX, ALU.max).then_inc(soft, 1)
                dve.wait_ge(soft, SOFT * i + 3)
                dve.tensor_tensor(mag[:, :, :], mag[:, :, :], top[:, :].unsqueeze(2).broadcast_to(wide),
                                  ALU.subtract).then_inc(soft, 1)
                dve.wait_ge(ex_ready, i + 1)
                dve.tensor_reduce(total[:, :], ex[:, :, :], AX, ALU.add).then_inc(soft, 1)
                dve.wait_ge(soft, SOFT * i + 5)
                dve.reciprocal(total[:, :], total[:, :]).then_inc(soft, 1)
                dve.wait_ge(soft, SOFT * i + 6)
                dve.tensor_tensor(wgt[:, :, :], ex[:, :, :], total[:, :].unsqueeze(2).broadcast_to(wide),
                                  ALU.mult).then_inc(soft, 1)
                dve.wait_ge(soft, SOFT * i + 7)

            def spread_weights(i):
                for n in range(N):
                    for m in range(N):
                        c = dve.tensor_copy(wgt_t[m * NV:(m + 1) * NV, :, n], wgt[n * NV:(n + 1) * NV, :, m])
                c.then_inc(swapped, 1)
                dve.wait_ge(swapped, i + 1)
                for j in range(4):
                    dve.tensor_tensor(wt[:, j, :, :].rearrange("p d (n b) -> p (d n) b", b=NV),
                                      wgt_t[:, 4 * j:4 * j + 4, :].rearrange("p a n -> p (a n)").unsqueeze(2)
                                      .broadcast_to((P, 16, NV)),
                                      mask[:, :].unsqueeze(1).broadcast_to((P, 16, NV)), ALU.mult)\
                        .then_inc(wt_ready, 1)

            def sums_lo(i):
                for j in range(4):
                    dve.wait_ge(sum_hi, 4 * i + j + 1)
                    for (lo, src), (hi, _) in zip(sum_pieces(bank, o[1], j), sum_pieces(bank, o[0], j)):
                        a = dve.tensor_tensor(lo, src, hi.bitcast(F32), ALU.subtract)
                    a.then_inc(sum_lo, 1)

            dve.sem_inc(sum_lo, 4)
            dve.tensor_reduce(mask[:, :], t["ident"][:, :].rearrange("p (m b) -> p b m", b=NV), AX, ALU.add)\
                .then_inc(mask_done, 1)
            dve.wait_ge(mask_done, 1)
            dve.wait_ge(consts_loaded, 16)
            projections_lo(0)
            with dve.Fori(0, NBLK - 1) as i:
                pick_scores(i)
                softmax(i)
                spread_weights(i)
                projections_lo(i + 1)
                sums_lo(i)
            pick_scores(NBLK - 1)
            softmax(NBLK - 1)
            spread_weights(NBLK - 1)
            sums_lo(NBLK - 1)


def interaction_products(nc, chip, t):
    HALF = B // 2
    with ExitStack() as mem:
        def sb(name, shape, dt=F32):
            return mem.enter_context(nc.sbuf_tensor(name, shape, dt))

        wo = [sb(f"wo_{part}", [P, 2, DT, 512], F32R) for part in ("hi", "lo")]
        bv = [sb(f"bv_{part}", [P, 2, DT, 2], F32R) for part in ("hi", "lo")]
        split_weights(nc, chip, "d_w", [
            (t["bv"].rearrange("p e d c -> p (e d c)"),
             bv[0][:, :, :, :].rearrange("p e d c -> p (e d c)"), bv[1][:, :, :, :].rearrange("p e d c -> p (e d c)"), 16)
        ] + [
            (t["wo"][e, :, kt:kt + 2, :].rearrange("p k f -> p (k f)"),
             wo[0][:, e, kt:kt + 2, :].rearrange("p k f -> p (k f)"),
             wo[1][:, e, kt:kt + 2, :].rearrange("p k f -> p (k f)"), 1024) for e in range(2) for kt in (0, 2)])

        o = [[sb(f"oT_{half}{part}", [P, HALF // BLK, 2, DT, BLK], F32R) for part in ("hi", "lo")] for half in range(2)]
        attn = [sb(f"attn_{part}", [P, 2, DT, HALF], F32R) for part in ("hi", "lo")]
        w_raw = sb("wi_raw", [P, 2, DT, 512])
        w = [sb(f"wi_{part}", [P, 2, DT, 512], F32R) for part in ("hi", "lo")]
        ri = sb("ri", [P, 4, 2, 512])
        rr = sb("rr", [P, 2, 512])
        bo = sb("bo", [P, 2, DT])

        consts_loaded = chip.sem("d_consts_loaded")
        bias_done = chip.sem("d_bias_done")
        bias_ready = chip.sem("d_bias_ready")
        o_loaded = [chip.sem(f"d_o_loaded{half}") for half in range(2)]
        w_loaded = chip.sem("d_w_loaded")
        w_hi = chip.sem("d_w_hi")
        w_lo = chip.sem("d_w_lo")
        attn_done = chip.sem("d_attn_done")
        attn_hi = chip.sem("d_attn_hi")
        attn_lo = chip.sem("d_attn_lo")
        ri_done = chip.sem("d_ri_done")
        rr_copied = chip.sem("d_rr_copied")
        r_done = chip.sem("d_r_done")
        i_done = chip.sem("d_i_done")
        ri_stored = [chip.sem(f"d_ri_stored{i}") for i in range(4)]

        block = mem.enter_context(nc.Block())

        @block.sync
        def _(sp):
            sp.dma_start(bo[:, :, :], t["bo"]).then_inc(consts_loaded, 16)

            def load_w(n):
                if not (isinstance(n, int) and n == 0):
                    sp.wait_ge(w_lo, 8 * n)
                sp.dma_start(w_raw[:, :, :, :].rearrange("p m k f -> p (m k f)"),
                             t["wint"][n].rearrange("p m k f -> p (m k f)")).then_inc(w_loaded, 16)

            def load_o(n, half, is_first):
                if not is_first:
                    sp.wait_ge(attn_done, 8 * (2 * n + half - 1))
                for part in range(2):
                    sp.dma_start(o[half][part][:, :, :, :, :].rearrange("p b e d q -> p b (e d q)").bitcast(F32),
                                 t["oT"][part, half * 8:half * 8 + 8, :, n].rearrange("b p e d q -> p b (e d q)"))\
                        .then_inc(o_loaded[half], 16)

            load_o(0, 0, True)
            load_w(0)
            load_o(0, 1, True)
            with sp.Fori(1, N) as n:
                load_o(n, 0, False)
                load_w(n)
                load_o(n, 1, False)

        @block.gpsimd
        def _(pool):
            def store(n, half):
                u = 2 * n + half
                for r in range(4):
                    pool.wait_ge(r_done, 4 * u + r + 5)
                    pool.wait_ge(i_done, 4 * u + r + 5)
                    pool.dma_start(t["RI"][4 * half + r, :, n], ri[:, r, :, :]).then_inc(ri_stored[r], 16)

            with pool.Fori(0, N) as n:
                store(n, 0)
                store(n, 1)
            for r in range(4):
                pool.wait_ge(ri_stored[r], 16 * 2 * N)

        @block.tensor
        def _(pe):
            bank = chip.psum

            def attn_products(n, half):
                u = 2 * n + half
                pe.wait_ge(o_loaded[half], 32 * (n + 1))
                for j in range(8):
                    e, dt = j // 4, j % 4
                    pe.wait_ge(r_done, 4 * u + 3 + j // 4)
                    pe.wait_ge(i_done, 4 * u + 3 + j // 4)
                    for kt in range(DT):
                        cols = slice(dt * P, (dt + 1) * P)
                        mm = mm3(pe, bank[:, j, :], wo[0][:, e, kt, cols], wo[1][:, e, kt, cols],
                                 o[half][0][:, :, e, kt, :], o[half][1][:, :, e, kt, :], kt == 0, kt == DT - 1)
                    mm.then_inc(attn_done, 1)

            def ri_products(n, half):
                u = 2 * n + half
                pe.wait_ge(attn_lo, 8 * (u + 1))
                pe.wait_ge(w_lo, 8 * (n + 1))
                for r in range(4):
                    if r >= 2:
                        pe.wait_ge(r_done, 4 * u + r - 2 + 5)
                        pe.wait_ge(i_done, 4 * u + r - 2 + 5)
                    rows = slice(r * P, (r + 1) * P)
                    first = 4 * (r % 2)
                    for j, terms in enumerate((((0, 0),), ((1, 1),), ((0, 1), (1, 0)))):
                        for a, (e, m) in enumerate(terms):
                            for kt in range(DT):
                                mm = mm3(pe, bank[:, first + j, :], attn[0][:, e, kt, rows], attn[1][:, e, kt, rows],
                                         w[0][:, m, kt, :], w[1][:, m, kt, :],
                                         (a, kt) == (0, 0), (a, kt) == (len(terms) - 1, DT - 1))
                        mm.then_inc(ri_done, 1)

            for e in range(2):
                for dt in range(DT):
                    for kt in range(DT):
                        cols = slice(dt * P, (dt + 1) * P)
                        mm = mm3(pe, bank[:, 3, (e * DT + dt) * 2:(e * DT + dt) * 2 + 2],
                                 wo[0][:, e, kt, cols], wo[1][:, e, kt, cols],
                                 bv[0][:, e, kt, :], bv[1][:, e, kt, :], kt == 0, kt == DT - 1)
            mm.then_inc(bias_done, 1)
            pe.wait_ge(bias_ready, 1)
            with pe.Fori(0, N) as n:
                for half in range(2):
                    attn_products(n, half)
                    ri_products(n, half)

        @block.scalar
        def _(act):
            bank = chip.psum

            def unit(n, half):
                u = 2 * n + half
                if half == 0:
                    act.wait_ge(w_loaded, 16 * (n + 1))
                for j in range(8):
                    e, dt = j // 4, j % 4
                    if half == 0:
                        act.activation(w[0][:, e, dt, :], w_raw[:, e, dt, :], ACT.Copy).then_inc(w_hi, 1)
                    act.wait_ge(attn_done, 8 * u + j + 1)
                    act.activation(attn[0][:, e, dt, :], bank[:, j, :], ACT.Identity,
                                   bias=bo[:, e, dt:dt + 1]).then_inc(attn_hi, 1)
                for r in range(4):
                    first = 4 * (r % 2)
                    act.wait_ge(ri_done, 12 * u + 3 * r + 1)
                    act.wait_ge(r_done, 4 * u + r + 3)
                    act.activation(rr[:, r % 2, :], bank[:, first, :], ACT.Copy).then_inc(rr_copied, 1)
                    if not (isinstance(u, int) and u == 0):
                        act.wait_ge(ri_stored[r], 16 * u)
                    act.wait_ge(ri_done, 12 * u + 3 * r + 3)
                    act.activation(ri[:, r, 1, :], bank[:, first + 2, :], ACT.Copy).then_inc(i_done, 1)

            act.sem_inc(i_done, 4)
            act.wait_ge(bias_ready, 1)
            unit(0, 0)
            unit(0, 1)
            with act.Fori(1, N) as n:
                unit(n, 0)
                unit(n, 1)

        @block.vector
        def _(dve):
            bank = chip.psum

            def unit(n, half):
                u = 2 * n + half
                for j in range(8):
                    e, dt = j // 4, j % 4
                    if half == 0:
                        dve.wait_ge(w_hi, 8 * n + j + 1)
                        dve.tensor_tensor(w[1][:, e, dt, :], w_raw[:, e, dt, :], w[0][:, e, dt, :].bitcast(F32),
                                          ALU.subtract).then_inc(w_lo, 1)
                    dve.wait_ge(attn_hi, 8 * u + j + 1)
                    dve.scalar_tensor_tensor(out=attn[1][:, e, dt, :], in0=bank[:, j, :],
                                             scalar=bo[:, e, dt:dt + 1], in1=attn[0][:, e, dt, :].bitcast(F32),
                                             op0=ALU.add, op1=ALU.subtract).then_inc(attn_lo, 1)
                for r in range(4):
                    first = 4 * (r % 2)
                    dve.wait_ge(rr_copied, 4 * u + r + 1)
                    if not (isinstance(u, int) and u == 0):
                        dve.wait_ge(ri_stored[r], 16 * u)
                    dve.wait_ge(ri_done, 12 * u + 3 * r + 2)
                    dve.tensor_tensor(ri[:, r, 0, :], rr[:, r % 2, :], bank[:, first + 1, :],
                                      ALU.subtract).then_inc(r_done, 1)

            dve.sem_inc(r_done, 4)
            dve.wait_ge(consts_loaded, 16)
            dve.wait_ge(bias_done, 1)
            dve.tensor_tensor(bo[:, :, :].rearrange("p e d -> p (e d)"), bo[:, :, :].rearrange("p e d -> p (e d)"),
                              bank[:, 3, 0:16:2], ALU.add).then_inc(bias_ready, 1)
            dve.wait_ge(bias_ready, 1)
            unit(0, 0)
            unit(0, 1)
            with dve.Fori(1, N) as n:
                unit(n, 0)
                unit(n, 1)


def interference_and_top(nc, chip, t, out):
    PAIRS = ((0, 1), (0, 2), (0, 3), (1, 2), (1, 3), (2, 3))
    OFF = [(i, j) for i in range(N) for j in range(N) if i != j]
    W = 2 * P
    with ExitStack() as mem:
        def sb(name, shape, dt=F32):
            return mem.enter_context(nc.sbuf_tensor(name, shape, dt))

        def parts(name, shape):
            return [sb(f"{name}_{part}", shape, F32R) for part in ("hi", "lo")]

        wm = parts("wm", [P, 2, DT, 512])
        wp = parts("wp", [P, DT, 512])
        w1 = parts("wt1", [P, DT, 512])
        w2 = parts("wt2", [P, DT, 256])
        pieces = []
        for m in range(2):
            for kt in (0, 2):
                pieces.append((t["wm"][m, :, kt:kt + 2, :], [x[:, m, kt:kt + 2, :] for x in wm]))
        for src, dst in ((t["wp"], wp), (t["wt1"], w1)):
            for kt in (0, 2):
                pieces.append((src[:, kt:kt + 2, :], [x[:, kt:kt + 2, :] for x in dst]))
        pieces.append((t["wt2"], [x[:, :, :] for x in w2]))
        split_weights(nc, chip, "e_w", [tuple(x.rearrange("p k f -> p (k f)") for x in (src, *dst)) + (1024,)
                                        for src, dst in pieces])

        ri = sb("ri_in", [P, 2, N, 2, 512])
        u = sb("u", [P, N, 2, 512])
        norm2, inv = u[:, :, 0, :], u[:, :, 1, :]
        pair = sb("pair", [P, 12, 512])
        zero = sb("zero", [P, N, 512])
        sup = [ri[:, par, 0, :, :] for par in range(2)]
        sumsq = sb("sumsq", [P, 2])
        inorm = sb("inorm", [P, 2])
        strength = sb("strength_now", [P, 2, N * N])
        diag = sb("diag", [P, 2, len(OFF), P])
        sup_t = [parts(f"sup_t{c}", [P, DT, W]) for c in ("r", "i", "n")]
        act_t = parts("act_t", [P, DT, W])
        raw_t = sb("raw_t", [P, DT, W])
        rows_x = sb("rows_x", [P, 2, 512])
        vstats = sb("vstats", [P, 2, 6])
        vmean = sb("vmean", [P, 2, 2])
        vstd = sb("vstd", [P, 2])
        y_row = raw_t[0:1, 2, :]
        post_b = sb("post_b", [P, 512])
        post_ln = sb("post_ln", [P, 2, DT])
        top_b2 = sb("top_b2", [P, 2])
        top_w3 = sb("top_w3", [P, 2])

        consts_loaded = chip.sem("e_consts_loaded")
        ri_loaded = [chip.sem(f"e_ri_loaded{i}") for i in range(2)]
        strength_ready = chip.sem("e_strength_ready")
        diag_ready = chip.sem("e_diag_ready")
        squared = chip.sem("e_squared")
        norm2_ready = chip.sem("e_norm2_ready")
        inv_guess = chip.sem("e_inv_guess")
        unit_ready = chip.sem("e_unit_ready")
        prod_ready = chip.sem("e_prod_ready")
        cos_ready = chip.sem("e_cos_ready")
        zero_used = chip.sem("e_zero_used")
        weight_done = chip.sem("e_weight_done")
        part_ready = chip.sem("e_part_ready")
        sup_step = chip.sem("e_sup_step")
        sup_turned = chip.sem("e_sup_turned")
        sumsq_ready = chip.sem("e_sumsq_ready")
        sup_hi = chip.sem("e_sup_hi")
        sup_lo = chip.sem("e_sup_lo")
        norm_step = chip.sem("e_norm_step")
        norm_root = chip.sem("e_norm_root")
        meas_done = chip.sem("e_meas_done")
        meas_sq = chip.sem("e_meas_sq")
        amp2_ready = chip.sem("e_amp2_ready")
        amp_ready = chip.sem("e_amp_ready")
        amp_hi = chip.sem("e_amp_hi")
        amp_lo = chip.sem("e_amp_lo")
        post_done = chip.sem("e_post_done")
        post_step = chip.sem("e_post_step")
        std_ready = chip.sem("e_std_ready")
        z_turned = chip.sem("e_z_turned")
        z_raw = chip.sem("e_z_raw")
        z_hi = chip.sem("e_z_hi")
        z_lo = chip.sem("e_z_lo")
        hx_loaded = chip.sem("e_hx_loaded")
        top1_done = chip.sem("e_top1_done")
        h_raw = chip.sem("e_h_raw")
        h_hi = chip.sem("e_h_hi")
        h_lo = chip.sem("e_h_lo")
        top2_done = chip.sem("e_top2_done")
        h2_ready = chip.sem("e_h2_ready")
        y_done = chip.sem("e_y_done")
        y_copied = chip.sem("e_y_copied")
        stored = chip.sem("e_stored")

        def flat(x):
            return x.rearrange("p a b -> p (a b)")

        block = mem.enter_context(nc.Block())

        @block.sync
        def _(sp):
            def load(r, par, is_first):
                if not is_first:
                    sp.wait_ge(sumsq_ready, r - 1)
                sp.dma_start(ri[:, par, :, :, :], t["RI"][r]).then_inc(ri_loaded[par], 16)

            load(0, 0, True)
            sp.dma_start(post_b[:, :], t["post_b"].partition_broadcast(P)).then_inc(consts_loaded, 16)
            sp.dma_start(top_b2[:, :], t["top_b2"]).then_inc(consts_loaded, 16)
            sp.dma_start(top_w3[:, :], t["top_w3"]).then_inc(consts_loaded, 16)
            sp.dma_start(post_ln[:, :, :], t["post_ln"]).then_inc(consts_loaded, 16)
            load(1, 1, True)
            with sp.Fori(1, RT // 2) as p:
                load(2 * p, 0, False)
                load(2 * p + 1, 1, False)

        @block.gpsimd
        def _(pool):
            with pool.Fori(0, RT // 2) as q:
                pool.wait_ge(z_turned, 2 * (q + 1))
                pool.dma_start(rows_x[:, :, :], t["y"][8, bass.ds(2 * q, 2)].rearrange("r p f -> p r f"))\
                    .then_inc(hx_loaded, 16)
                pool.wait_ge(y_copied, q + 1)
                pool.dma_start(out[bass.ds(W * q, W), :].rearrange("b c -> c b"), y_row).then_inc(stored, 16)
            pool.wait_ge(stored, 16 * (RT // 2))

        @block.tensor
        def _(pe):
            bank = chip.psum
            ident = t["ident"]

            def weigh(par, i, j, x, start, stop):
                return pe.matmul(bank[:, j, :], diag[:, par, OFF.index((i, j)), :], x,
                                 start=start, stop=stop, skip_group_check=True)

            def weights_zero(r, par, is_first):
                pe.wait_ge(diag_ready, r + 1)
                pe.wait_ge(norm2_ready, 3 * r + 2)
                for j in range(N):
                    if not is_first:
                        pe.wait_ge(part_ready, 4 * (r - 1) + j + 1)
                    others = [i for i in range(N) if i != j]
                    for i in others:
                        mm = weigh(par, i, j, zero[:, i, :], i == others[0], False)
                mm.then_inc(zero_used, 1)

            def weights_cos(r, par, i):
                pe.wait_ge(cos_ready, 3 * r + i + 1)
                for n, (a, b) in enumerate(PAIRS):
                    if a == i:
                        weigh(par, a, b, pair[:, n, :], False, False)
                        mm = weigh(par, b, a, pair[:, n, :], False, n == len(PAIRS) - 1)
                if i == 2:
                    mm.then_inc(weight_done, 1)

            def turn(dst, src, signal):
                for d in range(DT):
                    mm = pe.transpose(bank[:, dst, d * P:(d + 1) * P], src[:, d * P:(d + 1) * P], ident[:, :])
                mm.then_inc(signal, 1)

            def turn_sup(r, par, has_before):
                pe.wait_ge(sup_step, 2 * (r + 1))
                if has_before:
                    pe.wait_ge(sup_lo, 3 * r)
                turn(4, sup[par][:, 0, :], sup_turned)
                turn(5, sup[par][:, 1, :], sup_turned)

            def measure(q):
                pe.wait_ge(sup_lo, 6 * (q + 1))
                for d, b in enumerate((6, 7, 4, 5)):
                    cols = slice(d * P, (d + 1) * P)
                    for c, terms in enumerate((((0, 0), (1, 2)), ((1, 0), (0, 1)))):
                        for n, (m, x) in enumerate(terms):
                            for kt in range(DT):
                                mm = mm3(pe, bank[:, b, c * W:(c + 1) * W], wm[0][:, m, kt, cols], wm[1][:, m, kt, cols],
                                         sup_t[x][0][:, kt, :], sup_t[x][1][:, kt, :],
                                         (n, kt) == (0, 0), (n, kt) == (1, DT - 1))
                    mm.then_inc(meas_done, 1)

            def post(q):
                pe.wait_ge(amp_lo, 2 * (q + 1))
                for h in range(2):
                    rows = slice(h * P, (h + 1) * P)
                    for kt in range(DT):
                        mm = mm3(pe, bank[:, 6 + h, :], act_t[0][:, kt, rows], act_t[1][:, kt, rows],
                                 wp[0][:, kt, :], wp[1][:, kt, :], kt == 0, kt == DT - 1)
                    mm.then_inc(post_done, 1)

            def turn_z(q):
                pe.wait_ge(post_step, 10 * (q + 1))
                turn(6, rows_x[:, 0, :], z_turned)
                turn(7, rows_x[:, 1, :], z_turned)

            def top1(q, r):
                pe.wait_ge(z_lo, q + 1)
                if r is not None:
                    pe.wait_ge(sup_lo, 3 * (r + 1))
                for d in range(DT):
                    cols = slice(d * P, (d + 1) * P)
                    first = (d % 2) * W
                    for kt in range(DT):
                        if kt == DT - 1:
                            if d == 0:
                                pe.wait_ge(hx_loaded, 16 * (q + 1))
                            for h in range(2):
                                pe.matmul(bank[:, 4 + d // 2, first + h * P:first + (h + 1) * P],
                                          rows_x[:, h, d * P:(d + 1) * P], ident[:, :], start=False, stop=False,
                                          skip_group_check=True)
                        mm = mm3(pe, bank[:, 4 + d // 2, first:first + W], w1[0][:, kt, cols], w1[1][:, kt, cols],
                                 act_t[0][:, kt, :], act_t[1][:, kt, :], kt == 0, kt == DT - 1)
                mm.then_inc(top1_done, 1)

            def top2(q):
                pe.wait_ge(h_lo, q + 1)
                for m in range(2):
                    cols = slice(m * P, (m + 1) * P)
                    for kt in range(DT):
                        mm = mm3(pe, bank[:, 6, m * W:(m + 1) * W], w2[0][:, kt, cols], w2[1][:, kt, cols],
                                 act_t[0][:, kt, :], act_t[1][:, kt, :], kt == 0, kt == DT - 1)
                mm.then_inc(top2_done, 1)

            def top3(q):
                pe.wait_ge(h2_ready, q + 1)
                for m in range(2):
                    mm = pe.matmul(bank[0:1, 7, 0:W], top_w3[:, m:m + 1], raw_t[:, m, :], start=m == 0, stop=m == 1)
                mm.then_inc(y_done, 1)

            def step(p, has_tail):
                r = 2 * p
                weights_zero(r, 0, not has_tail)
                if has_tail:
                    turn_sup(r - 1, 1, True)
                    measure(p - 1)
                for i in range(3):
                    weights_cos(r, 0, i)
                if has_tail:
                    post(p - 1)
                weights_zero(r + 1, 1, False)
                turn_sup(r, 0, has_tail)
                if has_tail:
                    turn_z(p - 1)
                    top1(p - 1, r)
                weights_cos(r + 1, 1, 0)
                weights_cos(r + 1, 1, 1)
                if has_tail:
                    top2(p - 1)
                weights_cos(r + 1, 1, 2)
                if has_tail:
                    top3(p - 1)

            pe.wait_ge(consts_loaded, 64)
            step(0, False)
            with pe.Fori(1, RT // 2) as p:
                step(p, True)
            q = RT // 2 - 1
            turn_sup(RT - 1, 1, True)
            measure(q)
            post(q)
            turn_z(q)
            top1(q, None)
            top2(q)
            top3(q)

        @block.scalar
        def _(act):
            bank = chip.psum

            def make_diag(r, par, is_first):
                act.wait_ge(strength_ready, r + 1)
                if not is_first:
                    act.wait_ge(weight_done, r - 1)
                for n, (i, j) in enumerate(OFF):
                    a = act.activation(diag[:, par, n, :], t["ident"][:, :], ACT.Copy,
                                       scale=strength[:, par, i * N + j:i * N + j + 1])
                a.then_inc(diag_ready, 1)

            def square(r, par, is_first):
                act.wait_ge(ri_loaded[par], 16 * ((r - par) // 2 + 1) if isinstance(r, int) else 8 * (r - par) + 16)
                if not is_first:
                    act.wait_ge(prod_ready, 3 * r)
                act.activation(u[:, :, :, :], ri[:, par, :, :, :], ACT.Square).then_inc(squared, 1)

            def guess_inv(r):
                act.wait_ge(norm2_ready, 3 * (r + 1))
                act.activation(inv, norm2, ACT.Ln).then_inc(inv_guess, 1)
                act.wait_ge(inv_guess, 2 * r + 1)
                act.activation(inv, inv, ACT.Exp, scale=-0.5).then_inc(inv_guess, 1)

            def split_sup(r, par, has_before):
                cols = slice(par * P, (par + 1) * P)
                for n, (c, scale) in enumerate(((0, 1.0), (1, 1.0), (1, -1.0))):
                    act.wait_ge(sup_turned, 2 * r + c + 1)
                    if has_before and par == 0 and n == 0:
                        act.wait_ge(meas_done, 2 * r)
                    act.activation(sup_t[n][0][:, :, cols], bank[:, 4 + c, :].rearrange("p (d q) -> p d q", q=P),
                                   ACT.Copy, scale=scale).then_inc(sup_hi, 1)
                if has_before and par == 0:
                    act.wait_ge(norm_step, r)
                act.activation(flat(sup[par]), flat(sup[par]), ACT.Square,
                               accum_out=sumsq[:, par:par + 1]).then_inc(sumsq_ready, 1)

            def norm(q):
                act.wait_ge(norm_step, 2 * q + 1)
                act.activation(inorm[:, :], inorm[:, :], ACT.Sqrt).then_inc(norm_root, 1)

            def amp(q, h):
                b = (6, 4)[h]
                act.wait_ge(meas_done, 4 * q + 2 * h + 2)
                if h:
                    act.wait_ge(amp2_ready, 2 * q + 1)
                act.activation(rows_x[:, :, :], bank[:, b:b + 2, :], ACT.Square).then_inc(meas_sq, 1)
                act.wait_ge(amp2_ready, 2 * q + h + 1)
                act.activation(raw_t[:, 2 * h:2 * h + 2, :], raw_t[:, 2 * h:2 * h + 2, :], ACT.Sqrt).then_inc(amp_ready, 1)
                act.wait_ge(amp_ready, 2 * q + h + 1)
                act.activation(act_t[0][:, 2 * h:2 * h + 2, :], raw_t[:, 2 * h:2 * h + 2, :], ACT.Copy).then_inc(amp_hi, 1)

            def std(q):
                act.wait_ge(post_step, 10 * q + 7)
                act.activation(vstd[:, :], vstd[:, :], ACT.Sqrt).then_inc(std_ready, 1)

            def gelu(q):
                act.wait_ge(z_turned, 2 * (q + 1))
                for d in range(DT):
                    a = act.activation(raw_t[:, d, :].rearrange("p (h q) -> p h q", q=P),
                                       bank[:, 6:8, d * P:(d + 1) * P], ACT.Gelu,
                                       bias=post_ln[:, 1, d:d + 1], scale=post_ln[:, 0, d:d + 1])
                a.then_inc(z_raw, 1)
                act.wait_ge(z_raw, q + 1)
                act.activation(act_t[0][:, :, :], raw_t[:, :, :], ACT.Copy).then_inc(z_hi, 1)

            def relu1(q):
                act.wait_ge(top1_done, q + 1)
                act.activation(flat(raw_t[:, :, :]), flat(bank[:, 4:6, :]), ACT.Relu).then_inc(h_raw, 1)
                act.wait_ge(h_raw, q + 1)
                act.activation(act_t[0][:, :, :], raw_t[:, :, :], ACT.Copy).then_inc(h_hi, 1)

            def relu2(q):
                act.wait_ge(top2_done, q + 1)
                for m in range(2):
                    a = act.activation(raw_t[:, m, :], bank[:, 6, m * W:(m + 1) * W], ACT.Relu, bias=top_b2[:, m:m + 1])
                a.then_inc(h2_ready, 1)

            def copy_y(q):
                act.wait_ge(y_done, q + 1)
                act.activation(y_row, bank[0:1, 7, 0:W], ACT.Copy).then_inc(y_copied, 1)

            def step(p, has_tail, has_before, has_next):
                r, q = 2 * p, p - 1
                if has_tail:
                    split_sup(r - 1, 1, has_before)
                    norm(q)
                make_diag(r + 1, 1, not has_tail)
                if has_tail:
                    amp(q, 0)
                square(r + 1, 1, False)
                if has_tail:
                    amp(q, 1)
                guess_inv(r + 1)
                if has_tail:
                    std(q)
                split_sup(r, 0, has_tail)
                if has_tail:
                    gelu(q)
                if has_next:
                    make_diag(r + 2, 0, False)
                if has_tail:
                    relu1(q)
                if has_next:
                    square(r + 2, 0, False)
                if has_tail:
                    relu2(q)
                if has_next:
                    guess_inv(r + 2)
                if has_tail:
                    copy_y(q)

            act.wait_ge(consts_loaded, 64)
            make_diag(0, 0, True)
            square(0, 0, True)
            guess_inv(0)
            LAST = RT // 2 - 1
            step(0, False, False, True)
            step(1, True, False, True)
            with act.Fori(2, LAST) as p:
                step(p, True, True, True)
            step(LAST, True, True, False)
            split_sup(RT - 1, 1, True)
            norm(LAST)
            amp(LAST, 0)
            amp(LAST, 1)
            std(LAST)
            gelu(LAST)
            relu1(LAST)
            relu2(LAST)
            copy_y(LAST)

        @block.vector
        def _(dve):
            bank = chip.psum

            def copy_strength(r, par):
                dve.tensor_copy(strength[:, par, :], t["strength"][:, r, :]).then_inc(strength_ready, 1)

            def sum_squares(r, is_first):
                dve.wait_ge(squared, r + 1)
                dve.tensor_tensor(norm2, norm2, inv, ALU.add).then_inc(norm2_ready, 1)
                dve.wait_ge(norm2_ready, 3 * r + 1)
                if not is_first:
                    dve.wait_ge(zero_used, r)
                dve.tensor_scalar(zero[:, :, :], norm2, 0.0, None, ALU.is_equal).then_inc(norm2_ready, 1)
                dve.wait_ge(norm2_ready, 3 * r + 2)
                dve.tensor_scalar(norm2, norm2, 1e-37, None, ALU.max).then_inc(norm2_ready, 1)

            def newton(r):
                dve.wait_ge(inv_guess, 2 * (r + 1))
                dve.tensor_tensor(norm2, norm2, inv, ALU.mult).then_inc(unit_ready, 1)
                dve.wait_ge(unit_ready, 4 * r + 1)
                dve.scalar_tensor_tensor(out=norm2, in0=norm2, scalar=-0.5, in1=inv,
                                         op0=ALU.mult, op1=ALU.mult).then_inc(unit_ready, 1)
                dve.wait_ge(unit_ready, 4 * r + 2)
                dve.scalar_tensor_tensor(out=inv, in0=norm2, scalar=1.5, in1=inv,
                                         op0=ALU.add, op1=ALU.mult).then_inc(unit_ready, 1)

            def unit(r, par):
                dve.wait_ge(unit_ready, 4 * r + 3)
                dve.tensor_tensor(u[:, :, :, :], ri[:, par, :, :, :], inv.unsqueeze(2).broadcast_to((P, N, 2, 512)),
                                  ALU.mult).then_inc(unit_ready, 1)

            def cosines(r):
                dve.wait_ge(unit_ready, 4 * (r + 1))
                for i in range(3):
                    first, n = (0, 3, 5)[i], 3 - i
                    both = pair[:, :, :].rearrange("p (c j) f -> p j c f", c=2)[:, first:first + n]
                    dve.tensor_tensor(both, u[:, i + 1:N, :, :], u[:, i:i + 1, :, :].broadcast_to((P, n, 2, 512)),
                                      ALU.mult).then_inc(prod_ready, 1)
                    dve.wait_ge(prod_ready, 3 * r + i + 1)
                    dve.tensor_tensor(pair[:, first:first + n, :], pair[:, first:first + n, :],
                                      pair[:, 6 + first:6 + first + n, :], ALU.add).then_inc(cos_ready, 1)

            def shares(r, par):
                dve.wait_ge(weight_done, r + 1)
                for j in range(N):
                    for c in range(2):
                        a = dve.scalar_tensor_tensor(out=ri[:, par, j, c, :], in0=bank[:, j, :],
                                                     scalar=strength[:, par, j * N + j:j * N + j + 1],
                                                     in1=ri[:, par, j, c, :], op0=ALU.add, op1=ALU.mult)
                    a.then_inc(part_ready, 1)

            def superpose(r, par):
                dve.wait_ge(part_ready, 4 * (r + 1))
                dve.tensor_tensor(ri[:, par, 0:2, :, :], ri[:, par, 0:2, :, :], ri[:, par, 2:4, :, :], ALU.add).then_inc(sup_step, 1)
                dve.wait_ge(sup_step, 2 * r + 1)
                dve.tensor_tensor(sup[par], sup[par], ri[:, par, 1, :, :], ALU.add).then_inc(sup_step, 1)

            def split_sup(r, par):
                cols = slice(par * P, (par + 1) * P)
                for n, (c, scale) in enumerate(((0, 1.0), (1, 1.0), (1, -1.0))):
                    dve.wait_ge(sup_hi, 3 * r + (1 if n == 0 else 3))
                    dve.scalar_tensor_tensor(out=sup_t[n][1][:, :, cols],
                                             in0=bank[:, 4 + c, :].rearrange("p (d q) -> p d q", q=P), scalar=scale,
                                             in1=sup_t[n][0][:, :, cols].bitcast(F32),
                                             op0=ALU.mult, op1=ALU.subtract).then_inc(sup_lo, 1)

            def norm_eps(q, has_before):
                dve.wait_ge(sumsq_ready, 2 * (q + 1))
                if has_before:
                    dve.wait_ge(post_step, 10 * q)
                dve.tensor_scalar(inorm[:, :], sumsq[:, :], 1e-8, None, ALU.add).then_inc(norm_step, 1)

            def norm_inv(q):
                dve.wait_ge(norm_root, q + 1)
                dve.reciprocal(inorm[:, :], inorm[:, :]).then_inc(norm_step, 1)

            def amp(q, h, has_before):
                both = rows_x[:, :, :].rearrange("p d (c q) -> p d c q", c=2)
                part = slice(2 * h, 2 * h + 2)
                if h and has_before:
                    dve.wait_ge(stored, 16 * q)
                dve.wait_ge(meas_sq, 2 * q + h + 1)
                dve.tensor_tensor(raw_t[:, part, :], both[:, :, 0, :], both[:, :, 1, :], ALU.add).then_inc(amp2_ready, 1)

            def amp_low(q, h):
                part = slice(2 * h, 2 * h + 2)
                dve.wait_ge(amp_hi, 2 * q + h + 1)
                dve.tensor_tensor(act_t[1][:, part, :], raw_t[:, part, :], act_t[0][:, part, :].bitcast(F32),
                                  ALU.subtract).then_inc(amp_lo, 1)

            def post(q):
                dve.wait_ge(norm_step, 2 * (q + 1))
                for h in range(2):
                    dve.wait_ge(post_done, 2 * q + h + 1)
                    dve.scalar_tensor_tensor(out=rows_x[:, h, :], in0=bank[:, 6 + h, :], scalar=inorm[:, h:h + 1],
                                             in1=post_b[:, :], op0=ALU.mult, op1=ALU.add).then_inc(post_step, 1)
                for h in range(2):
                    dve.wait_ge(post_step, 10 * q + h + 1)
                    dve.bn_stats(vstats[:, h, :], rows_x[:, h, :]).then_inc(post_step, 1)
                dve.wait_ge(post_step, 10 * q + 4)
                for h in range(2):
                    dve.bn_aggr(vmean[:, h, :], vstats[:, h, :]).then_inc(post_step, 1)
                dve.wait_ge(post_step, 10 * q + 6)
                dve.tensor_scalar(vstd[:, :], vmean[:, :, 1], EPS, None, ALU.add).then_inc(post_step, 1)

            def z_rows(q):
                dve.wait_ge(std_ready, q + 1)
                dve.reciprocal(vstd[:, :], vstd[:, :]).then_inc(post_step, 1)
                dve.wait_ge(post_step, 10 * q + 8)
                for h in range(2):
                    dve.tensor_scalar(rows_x[:, h, :], rows_x[:, h, :], vmean[:, h, 0:1], vstd[:, h:h + 1],
                                      ALU.subtract, ALU.mult).then_inc(post_step, 1)

            def low(is_hi, is_lo, q):
                dve.wait_ge(is_hi, q + 1)
                dve.tensor_tensor(act_t[1][:, :, :], raw_t[:, :, :], act_t[0][:, :, :].bitcast(F32),
                                  ALU.subtract).then_inc(is_lo, 1)

            def step(p, has_tail, has_before, has_next):
                r, q = 2 * p, p - 1
                if has_tail:
                    split_sup(r - 1, 1)
                    norm_eps(q, has_before)
                newton(r)
                copy_strength(r + 1, 1)
                unit(r, 0)
                cosines(r)
                if has_tail:
                    norm_inv(q)
                    for h in range(2):
                        amp(q, h, has_before)
                        amp_low(q, h)
                sum_squares(r + 1, False)
                shares(r, 0)
                superpose(r, 0)
                if has_tail:
                    post(q)
                newton(r + 1)
                if has_tail:
                    z_rows(q)
                split_sup(r, 0)
                if has_next:
                    copy_strength(r + 2, 0)
                unit(r + 1, 1)
                if has_tail:
                    low(z_hi, z_lo, q)
                cosines(r + 1)
                if has_next:
                    sum_squares(r + 2, False)
                if has_tail:
                    low(h_hi, h_lo, q)
                shares(r + 1, 1)
                superpose(r + 1, 1)

            dve.wait_ge(consts_loaded, 64)
            copy_strength(0, 0)
            sum_squares(0, True)
            LAST = RT // 2 - 1
            step(0, False, False, True)
            step(1, True, False, True)
            with dve.Fori(2, LAST) as p:
                step(p, True, True, True)
            step(LAST, True, True, False)
            split_sup(RT - 1, 1)
            norm_eps(LAST, True)
            norm_inv(LAST)
            for h in range(2):
                amp(LAST, h, True)
                amp_low(LAST, h)
            post(LAST)
            z_rows(LAST)
            low(z_hi, z_lo, LAST)
            low(h_hi, h_lo, LAST)


def build(nc, d, outs, upto=9):
    with ExitStack() as ctx:
        chip = Chip(nc, ctx)
        t = dict(d)
        t["tables"] = [d["tbl_0"], d["tbl_1"], d["tbl_2"], d["tbl_3"]]
        t["ident"] = chip.keep("ident", [P, P])
        t["strength"] = chip.keep("strength", [P, RT, N * N])
        t["mean_var"] = chip.keep("mean_var", [P, 2 * RT, 2])
        t["rstd"] = chip.keep("rstd", [P, 2 * RT])
        t["y"] = chip.scratch("y_scratch", (9, RT, P, 512))
        t["sT"] = chip.scratch("sT_scratch", (2, 2, NBLK, P, DT, N, BLK))
        encoder_first_layer(nc, chip, t)
        if upto >= 2:
            encoder_second_layer(nc, chip, t)
        t["oT"] = chip.scratch("oT_scratch", (2, NBLK, P, N, 2, DT, BLK))
        if upto >= 3:
            attention(nc, chip, t)
        t["RI"] = chip.scratch("RI_scratch", (RT, P, N, 2, 512))
        if upto >= 4:
            interaction_products(nc, chip, t)
        if upto >= 5:
            interference_and_top(nc, chip, t, outs)
        return t


def host_layout(x):
    import numpy as np

    def tiles(w):
        return w.reshape(w.shape[0] // 128, 128, w.shape[1])

    def chunks(w):
        return w.reshape(w.shape[0] // 128, 128, w.shape[1] // 512, 512).transpose(2, 0, 1, 3)

    def column(v):
        return v.reshape(-1, 128).T

    L = {k[7:]: np.asarray(v) for k, v in x.items() if k.startswith("L0_rec_")}
    d = {"ids": np.asarray(x["ids"])}
    for i in range(4):
        d[f"tbl_{i}"] = np.asarray(x[f"tbl_{i}"])
    d["xT"] = tiles(np.asarray(x["r_x"]).T)
    top1 = np.asarray(x["W_top1"])
    d["w1"] = np.concatenate([chunks(L["er_W1"].T), chunks(L["ei_W1"].T), chunks(top1[512:])])
    d["b1"] = np.concatenate([L["er_b1"], L["ei_b1"], np.asarray(x["b_top1"])]).reshape(9, 512)
    d["ln1"] = np.stack([np.stack([column(L[e + "_g1"]), column(L[e + "_be1"])], 1) for e in ("er", "ei")], 1)
    d["w2"] = np.concatenate([chunks(L["er_W2"].T), chunks(L["ei_W2"].T)])
    d["b2"] = np.concatenate([column(L["er_b2"]), column(L["ei_b2"])], 1)

    def rows(w):
        return w.reshape(w.shape[0] // 128, 128, w.shape[1]).transpose(1, 0, 2)

    names = ("q_r", "k_r", "q_i", "k_i", "v_r", "v_i")
    d["wqkv"] = np.stack([rows(L["W" + m].T) for m in names])
    d["bqk"] = np.stack([column(L["b" + m]) for m in names[:4]], 1)


    def crossed(w):
        return w.reshape(4, 2, 64, -1)[:, ::-1].reshape(w.shape)

    d["wo"] = np.stack([rows(L["Wo_r"].T), rows(crossed(L["Wo_i"].T))])
    bv = np.stack([column(L["bv_r"]), column(crossed(L["bv_i"]))], 1)
    d["bv"] = np.repeat(bv[..., None], 2, -1)
    d["bo"] = np.stack([column(L["bo_r"]), column(L["bo_i"])], 1)
    wint = np.stack([L["int_Wr"], L["int_Wi"]], 1).transpose(0, 1, 3, 2)
    d["wint"] = wint.reshape(4, 2, 4, 128, 512).transpose(0, 3, 1, 2, 4)
    d["wm"] = np.stack([rows(L["meas_Mr"].T), rows(L["meas_Mi"].T)])
    d["wp"] = rows(L["post_W"].T)
    d["wt1"] = rows(top1[:512])
    d["wt2"] = rows(np.asarray(x["W_top2"]))
    d["post_b"] = L["post_b"]
    d["post_ln"] = np.stack([column(L["post_g"]), column(L["post_be"])], 1)
    d["top_b2"] = column(np.asarray(x["b_top2"]))
    d["top_w3"] = column(np.asarray(x["W_top3"]))
    return {k: np.ascontiguousarray(v) for k, v in d.items()}


def kernel(**inputs):
    import concourse.bacc as bacc
    from concourse.bass_utils import run_bass_kernel_spmd

    arrays = host_layout(inputs)
    nc = bacc.Bacc("TRN2", target_bir_lowering=False, num_devices=1)
    d = {n: nc.dram_tensor("in_" + n, a.shape, mybir.dt.from_np(a.dtype), kind="ExternalInput").ap()
         for n, a in arrays.items()}
    out = nc.dram_tensor("out_0_dram", (B, 1), F32, kind="ExternalOutput").ap()
    build(nc, d, out)
    r = run_bass_kernel_spmd(nc, [{"in_" + n: a for n, a in arrays.items()}], core_ids=[0])
    return r.results[0]["out_0_dram"]
```

```python
import concourse.bass as bass
from concourse import mybir
from contextlib import ExitStack

F32 = mybir.dt.float32
F32R = mybir.dt.float32r
U32 = mybir.dt.uint32
I32 = mybir.dt.int32
ALU = mybir.AluOpType
ACT = mybir.ActivationFunctionType
AX = mybir.AxisListType.X

P = 128
B = 1024
IN = 2048
HID = 2048
D = 512
N = 4
H = 8
HD = D // H
RT = B // P
KT = IN // P
DT = D // P
NB = 8
BLK = 64
NBLK = B // BLK
EPS = 1e-5


def mm3(pe, out, a_hi, a_lo, b_hi, b_lo, start, stop):
    pe.matmul(out, a_hi, b_hi, start=start, stop=False)
    pe.matmul(out, a_hi, b_lo, start=False, stop=False)
    return pe.matmul(out, a_lo, b_hi, start=False, stop=stop)


class Chip:

    def __init__(self, nc, ctx):
        self.nc = nc
        self.ctx = ctx
        self.psum = ctx.enter_context(nc.psum_tensor("psum", [P, NB, 512], F32))

    def sem(self, name):
        return self.ctx.enter_context(self.nc.semaphore(name))

    def keep(self, name, shape, dt=F32):
        return self.ctx.enter_context(self.nc.sbuf_tensor(name, shape, dt))

    def scratch(self, name, shape, dt=F32):
        return self.nc.dram_tensor(name, shape, dt, kind="Internal").ap()


def encoder_first_layer(nc, chip, t):
    CH = 9
    RING = 4
    with ExitStack() as mem:
        def sb(name, shape, dt=F32):
            return mem.enter_context(nc.sbuf_tensor(name, shape, dt))

        x_raw = sb("x_raw", [P, 2, B])
        x_hi = sb("x_hi", [P, KT, B], F32R)
        x_lo = sb("x_lo", [P, KT, B], F32R)
        w_raw = sb("w1_raw", [P, RING, 512])
        w_hi = sb("w1_hi", [P, RING, 512], F32R)
        w_lo = sb("w1_lo", [P, RING, 512], F32R)
        y = sb("y_rows", [P, RT, 512])
        bias = sb("bias1", [P, 512])
        stats = sb("stats", [P, RT, CH - 1, 6])
        ids = sb("ids_sb", [P, RT, N], I32)

        x_loaded = [chip.sem(f"a_x_loaded{i}") for i in range(2)]
        x_hi_done = chip.sem("a_x_hi_done")
        x_lo_done = chip.sem("a_x_lo_done")
        w_loaded = [chip.sem(f"a_w_loaded{i}") for i in range(RING)]
        w_hi_done = chip.sem("a_w_hi_done")
        w_lo_done = chip.sem("a_w_lo_done")
        w_used = chip.sem("a_w_used")
        acc_done = chip.sem("a_acc_done")
        y_copied = chip.sem("a_y_copied")
        y_biased = chip.sem("a_y_biased")
        y_stored = t["y_stored"]
        stats_done = chip.sem("a_stats_done")
        var_ready = chip.sem("a_var_ready")
        std_ready = chip.sem("a_std_ready")
        bias_loaded = chip.sem("a_bias_loaded")
        ids_loaded = chip.sem("a_ids_loaded")
        gathered = chip.sem("a_gathered")
        ident_step = chip.sem("a_ident_step")

        block = mem.enter_context(nc.Block())

        @block.sync
        def _(sp):
            def load_w(c, k):
                if not (isinstance(c, int) and c == 0 and k < RING):
                    sp.wait_ge(w_lo_done, KT * c + k - RING + 1)
                sp.dma_start(w_raw[:, k % RING, :], t["w1"][c, k]).then_inc(w_loaded[k % RING], 16)

            def load_x(k):
                if k >= 2:
                    sp.wait_ge(x_lo_done, k - 1)
                sp.dma_start(x_raw[:, k % 2, :], t["xT"][k]).then_inc(x_loaded[k % 2], 16)

            for k in range(KT):
                load_x(k)
                load_w(0, k)
            sp.dma_start(bias[:, :], t["b1"][0].partition_broadcast(P)).then_inc(bias_loaded, 16)
            with sp.Fori(1, CH) as c:
                for k in range(KT):
                    load_w(c, k)
                    if k == KT // 2:
                        sp.wait_ge(y_biased, RT * c)
                        sp.dma_start(bias[:, :], t["b1"][c].partition_broadcast(P)).then_inc(bias_loaded, 16)
            sp.wait_ge(gathered, 16 * RT * N)
            for r in range(RT):
                sp.wait_ge(y_biased, RT * (CH - 1) + r + 1)
                sp.dma_start(t["y"][CH - 1, r], y[:, r, :]).then_inc(t["y_last_stored"], 16)

        @block.gpsimd
        def _(pool):
            pool.memset(t["ident"][:, :], 0.0).then_inc(ident_step, 1)
            pool.wait_ge(ident_step, 1)
            pool.affine_select(out=t["ident"][:, :], in_=t["ident"][:, :], compare_op=ALU.not_equal,
                               fill=1.0, base=0, pattern=[[-1, P]], channel_multiplier=1)\
                .then_inc(ident_step, 1)
            pool.dma_start(ids[:, :, :], t["ids"].rearrange("(r p) i -> p r i", p=P)).then_inc(ids_loaded, 16)
            pool.wait_ge(ids_loaded, 16)
            for r in range(RT):
                for i in range(N):
                    pool.indirect_dma_start(
                        out=t["strength"][:, r, i * N:(i + 1) * N], out_offset=None,
                        in_=t["tables"][i],
                        in_offset=bass.IndirectOffsetOnAxis(ap=ids[:, r, i:i + 1].bitcast(U32), axis=0),
                    ).then_inc(gathered, 16)

            def store(c):
                for r in range(RT):
                    pool.wait_ge(y_biased, RT * c + r + 1)
                    pool.dma_start(t["y"][c, r], y[:, r, :]).then_inc(y_stored, 16)

            with pool.Fori(0, CH - 1) as c:
                store(c)
            pool.wait_ge(y_stored, 16 * RT * (CH - 1))
            for u in range(2):
                load_y_unit(pool, t, 0, u)

        @block.scalar
        def _(act):
            def hi(c, k):
                act.wait_ge(w_loaded[k % RING], 16 * (KT // RING * c + k // RING + 1))
                if not (isinstance(c, int) and c == 0 and k < RING):
                    act.wait_ge(w_used, KT * c + k - RING + 1)
                act.activation(w_hi[:, k % RING, :], w_raw[:, k % RING, :], ACT.Copy).then_inc(w_hi_done, 1)

            def evacuate(c):
                if not (isinstance(c, int) and c == 0):
                    act.wait_ge(y_stored, 16 * RT * c)
                for r in range(RT):
                    if r < RT - 1:
                        act.wait_ge(acc_done, (RT - 1) * c + r + 1)
                    else:
                        act.wait_ge(w_used, KT * (c + 1))
                    act.activation(y[:, r, :], chip.psum[:, r, :], ACT.Copy).then_inc(y_copied, 1)

            def chunk(c, is_first, is_last):
                for k in range(0 if is_first else 3, KT):
                    if is_first:
                        act.wait_ge(x_loaded[k % 2], 16 * (k // 2 + 1))
                        act.activation(x_hi[:, k, :], x_raw[:, k % 2, :], ACT.Copy).then_inc(x_hi_done, 1)
                    hi(c, k)
                if not is_last:
                    for k in range(3):
                        hi(c + 1, k)
                evacuate(c)

            chunk(0, True, False)
            with act.Fori(1, CH - 1) as c:
                chunk(c, False, False)
            act.wait_ge(var_ready, 2)
            act.activation(t["rstd"][:, :], t["rstd"][:, :], ACT.Sqrt).then_inc(std_ready, 1)
            chunk(CH - 1, False, True)

        @block.vector
        def _(dve):
            def lo(c, k):
                dve.wait_ge(w_hi_done, KT * c + k + 1)
                dve.tensor_tensor(w_lo[:, k % RING, :], w_raw[:, k % RING, :],
                                  w_hi[:, k % RING, :].bitcast(F32), ALU.subtract).then_inc(w_lo_done, 1)

            def add_bias(c, r):
                dve.wait_ge(y_copied, RT * c + r + 1)
                dve.tensor_tensor(y[:, r, :], y[:, r, :], bias[:, :], ALU.add).then_inc(y_biased, 1)

            def row_stats(c, r):
                dve.wait_ge(y_biased, RT * c + r + 1)
                dve.bn_stats(stats[:, r, c, :], y[:, r, :]).then_inc(stats_done, 1)

            def chunk(c, is_first, is_last):
                for k in range(0 if is_first else 3, KT):
                    if is_first:
                        dve.wait_ge(x_hi_done, k + 1)
                        dve.tensor_tensor(x_lo[:, k, :], x_raw[:, k % 2, :],
                                          x_hi[:, k, :].bitcast(F32), ALU.subtract).then_inc(x_lo_done, 1)
                    lo(c, k)
                if not is_last:
                    for k in range(3):
                        lo(c + 1, k)
                dve.wait_ge(bias_loaded, 16 * (c + 1))
                for r in range(RT):
                    add_bias(c, r)
                    if r and not is_last:
                        row_stats(c, r - 1)
                if not is_last:
                    row_stats(c, RT - 1)
                    dve.wait_ge(stats_done, RT * (c + 1))

            chunk(0, True, False)
            with dve.Fori(1, CH - 1) as c:
                chunk(c, False, False)
            for e in range(2):
                for r in range(RT):
                    a = dve.bn_aggr(t["mean_var"][:, e * RT + r, :], stats[:, r, 4 * e:4 * e + 4, :])
            a.then_inc(var_ready, 1)
            dve.wait_ge(var_ready, 1)
            dve.tensor_scalar(t["rstd"][:, :], t["mean_var"][:, :, 1], EPS, None, ALU.add).then_inc(var_ready, 1)
            dve.wait_ge(std_ready, 1)
            dve.reciprocal(t["rstd"][:, :], t["rstd"][:, :]).then_inc(var_ready, 1)
            chunk(CH - 1, False, True)
            dve.wait_ge(var_ready, 3)

        @block.tensor
        def _(pe):
            def chunk(c, is_first):
                for k in range(KT):
                    if is_first:
                        pe.wait_ge(x_lo_done, k + 1)
                    pe.wait_ge(w_lo_done, KT * c + k + 1)
                    for r in range(RT):
                        if k == 0 and not is_first:
                            pe.wait_ge(y_copied, RT * (c - 1) + r + 1)
                        rows = slice(r * P, (r + 1) * P)
                        mm = mm3(pe, chip.psum[:, r, :], x_hi[:, k, rows], x_lo[:, k, rows],
                                 w_hi[:, k % RING, :], w_lo[:, k % RING, :], k == 0, k == KT - 1)
                        if r == RT - 1:
                            mm.then_inc(w_used, 1)
                        elif k == KT - 1:
                            mm.then_inc(acc_done, 1)

            chunk(0, True)
            with pe.Fori(1, CH) as c:
                chunk(c, False)


def load_y_unit(pool, t, e, u):
    pool.dma_start(t["z"][:, u % 2, :, :], t["y"][4 * e + u % 4, 4 * (u // 4):4 * (u // 4) + 4]
                   .rearrange("r p f -> p r f")).then_inc(t["y_loaded"][u % 2], 16)


def encoder_second_layer(nc, chip, t):
    RING = 4
    UNITS = 8
    PASSES = N + 1
    ACCS = 3 + 3 + 7 * (N - 1)
    with ExitStack() as mem:
        def sb(name, shape, dt=F32):
            return mem.enter_context(nc.sbuf_tensor(name, shape, dt))

        z = t["z"]
        h_raw = sb("h_raw", [P, 2, 512])
        h_hi = sb("h_hi", [P, KT, B], F32R)
        h_lo = sb("h_lo", [P, KT, B], F32R)
        w_raw = sb("w2_raw", [P, RING, 512])
        w_hi = sb("w2_hi", [P, RING, 512], F32R)
        w_lo = sb("w2_lo", [P, RING, 512], F32R)
        s_hi = sb("s_hi", [P, NB, 512], F32R)
        s_lo = sb("s_lo", [P, NB, 512], F32R)
        ln = sb("ln", [P, 2, 2, KT])
        b2 = sb("b2", [P, 2 * N * DT])
        b2_now = sb("b2_now", [P, DT])

        y_loaded = t["y_loaded"]
        z_ready = chip.sem("b_z_ready")
        turned = chip.sem("b_turned")
        h_raw_done = chip.sem("b_h_raw_done")
        h_hi_done = chip.sem("b_h_hi_done")
        h_lo_done = chip.sem("b_h_lo_done")
        w_loaded = [chip.sem(f"b_w_loaded{i}") for i in range(RING)]
        w_hi_done = chip.sem("b_w_hi_done")
        w_lo_done = chip.sem("b_w_lo_done")
        w_used = chip.sem("b_w_used")
        acc_done = chip.sem("b_acc_done")
        s_hi_done = chip.sem("b_s_hi_done")
        s_lo_done = chip.sem("b_s_lo_done")
        s_stored = t["s_stored"]
        consts_loaded = chip.sem("b_consts_loaded")
        b2_ready = chip.sem("b_b2_ready")

        def half_piece(h, dt):
            return 4 * h + dt, dt, dt, h

        def last_piece(h, dt):
            return 4 * h + dt, dt if h else 4 + dt, dt, h

        def full_piece(i):
            return i, (i + 4) % NB, i // 2, i % 2

        def half_pieces(h):
            return [half_piece(h, dt) for dt in range(DT)]

        def last_pieces(h):
            return [last_piece(h, dt) for dt in range(DT)]

        FULL = [full_piece(i) for i in range(NB)]

        block = mem.enter_context(nc.Block())

        @block.sync
        def _(sp):
            sp.dma_start(ln[:, :, :, :], t["ln1"]).then_inc(consts_loaded, 16)
            sp.dma_start(b2[:, :], t["b2"]).then_inc(consts_loaded, 16)

            def load_w(e, a, en, k):
                if not (isinstance(a, int) and (e, a) == (0, 0) and k < RING):
                    sp.wait_ge(w_lo_done, KT * (PASSES * e + a) + k - RING + 1)
                sp.dma_start(w_raw[:, k % RING, :], t["w2"][en, k]).then_inc(w_loaded[k % RING], 16)

            for e in range(2):
                for a in range(2):
                    for k in range(KT):
                        load_w(e, a, N * e, k)
                with sp.Fori(1, N - e) as n:
                    for k in range(KT):
                        load_w(e, n + 1, N * e + n, k)
            for a in (N, N + 1):
                for k in range(KT):
                    load_w(1, a, 2 * N - 1, k)
            for i, _, dt, half in last_pieces(1):
                for part, src, done in ((0, s_hi, s_hi_done), (1, s_lo, s_lo_done)):
                    sp.wait_ge(done, NB * (2 * N - 1) + i + 1)
                    sp.dma_start(
                        t["sT"][part, 1, half * 8:half * 8 + 8, :, dt, N - 1, :].rearrange("b p q -> p b q"),
                        src[:, i, :].rearrange("p (b q) -> p b q", q=BLK).bitcast(F32)).then_inc(t["s_last_stored"], 16)

        @block.gpsimd
        def _(pool):
            def load_y(e, u):
                pool.wait_ge(turned, 4 * (UNITS * e + u - 2) + 4)
                load_y_unit(pool, t, e, u)

            def store(e, n, pieces):
                for i, _, dt, half in pieces:
                    pool.wait_ge(s_lo_done, NB * (N * e + n) + i + 1)
                    for part, src in enumerate((s_hi, s_lo)):
                        pool.dma_start(
                            t["sT"][part, e, half * 8:half * 8 + 8, :, dt, n, :].rearrange("b p q -> p b q"),
                            src[:, i, :].rearrange("p (b q) -> p b q", q=BLK).bitcast(F32),
                        ).then_inc(s_stored[i], 16)

            for e in range(2):
                for u in range(4 if e else 2, UNITS):
                    load_y(e, u)
                    if u == 6:
                        store(e, 0, half_pieces(0))
                if e == 0:
                    load_y(1, 0)
                    load_y(1, 1)
                store(e, 0, half_pieces(1))
                with pool.Fori(1, N - 1) as n:
                    store(e, n, FULL)
                if e == 0:
                    store(0, N - 1, FULL[:2])
                    load_y(1, 2)
                    store(0, N - 1, FULL[2:5])
                    load_y(1, 3)
                    store(0, N - 1, FULL[5:])
            store(1, N - 1, last_pieces(0))
        @block.scalar
        def _(act):
            def hi(e, a, k):
                tile = KT * (PASSES * e + a) + k
                act.wait_ge(w_loaded[k % RING], 4 * (tile - k % RING) + 16)
                if not (isinstance(a, int) and tile < RING):
                    act.wait_ge(w_used, tile - RING + 2)
                act.activation(w_hi[:, k % RING, :], w_raw[:, k % RING, :], ACT.Copy).then_inc(w_hi_done, 1)

            def gelu(e, u, j):
                n = 4 * (UNITS * e + u) + j
                k, half = 4 * (u % 4) + j, u // 4
                act.wait_ge(turned, n + 1)
                if n >= 2:
                    act.wait_ge(h_lo_done, n - 1)
                act.activation(h_raw[:, n % 2, :], chip.psum[:, 4 + n % 4, :], ACT.Gelu,
                               bias=ln[:, e, 1, k:k + 1], scale=ln[:, e, 0, k:k + 1]).then_inc(h_raw_done, 1)
                act.wait_ge(h_raw_done, n + 1)
                act.activation(h_hi[:, k, half * 512:(half + 1) * 512], h_raw[:, n % 2, :], ACT.Copy)\
                    .then_inc(h_hi_done, 1)

            def evacuate(e, a, en, pieces, accs):
                act.wait_ge(b2_ready, en + 1)
                for x, (i, b, dt, _) in enumerate(pieces):
                    if x < len(pieces) - 1:
                        act.wait_ge(acc_done, accs + x + 1)
                    else:
                        act.wait_ge(w_used, KT * (PASSES * e + a + 1) + 1)
                    if not (isinstance(en, int) and en == 0):
                        act.wait_ge(s_stored[i], 32 * en)
                    act.activation(s_hi[:, i, :], chip.psum[:, b, :], ACT.Identity,
                                   bias=b2_now[:, dt:dt + 1]).then_inc(s_hi_done, 1)

            def token(e, n):
                for k in range(3, KT + 3):
                    hi(e, n + 1, k)
                evacuate(e, n + 1, N * e + n, FULL, ACCS * e + 7 * (n - 1) + 6)

            for k in range(3):
                hi(0, 0, k)
            act.wait_ge(consts_loaded, 32)
            for e in range(2):
                for j in range(4):
                    gelu(e, 0, j)
                for u in range(UNITS):
                    if u == 4:
                        evacuate(e, 0, N * e, half_pieces(0), ACCS * e)
                    for j in range(4):
                        if u + 1 < UNITS:
                            gelu(e, u + 1, j)
                        hi(e, 0, 4 * u + j + 3)
                evacuate(e, 1, N * e, half_pieces(1), ACCS * e + 3)
                with act.Fori(1, N - e) as n:
                    token(e, n)
            for h in range(2):
                for k in range(3, KT if h else KT + 3):
                    hi(1, N + h, k)
                evacuate(1, N + h, 2 * N - 1, last_pieces(h), ACCS + 7 * (N - 2) + 6 + 3 * h)

        @block.vector
        def _(dve):
            def lo(tile, k):
                dve.wait_ge(w_hi_done, tile + 1)
                dve.tensor_tensor(w_lo[:, k % RING, :], w_raw[:, k % RING, :],
                                  w_hi[:, k % RING, :].bitcast(F32), ALU.subtract).then_inc(w_lo_done, 1)

            def normalise(e, u):
                n = UNITS * e + u
                dve.wait_ge(y_loaded[u % 2], 16 * (n // 2 + 1))
                for r in range(4):
                    row = e * RT + 4 * (u // 4) + r
                    v = dve.tensor_scalar(z[:, u % 2, r, :], z[:, u % 2, r, :], t["mean_var"][:, row, 0:1],
                                          t["rstd"][:, row:row + 1], ALU.subtract, ALU.mult)
                v.then_inc(z_ready, 1)

            def h_low(e, u, j):
                n = 4 * (UNITS * e + u) + j
                k, half = 4 * (u % 4) + j, u // 4
                cols = slice(half * 512, (half + 1) * 512)
                dve.wait_ge(h_hi_done, n + 1)
                dve.tensor_tensor(h_lo[:, k, cols], h_raw[:, n % 2, :],
                                  h_hi[:, k, cols].bitcast(F32), ALU.subtract).then_inc(h_lo_done, 1)

            def take_bias(en):
                dve.tensor_copy(b2_now[:, :], b2[:, bass.ds(DT * en, DT)]).then_inc(b2_ready, 1)
                dve.wait_ge(b2_ready, en + 1)

            def evacuate(en, pieces):
                for i, b, dt, _ in pieces:
                    dve.wait_ge(s_hi_done, NB * en + i + 1)
                    dve.scalar_tensor_tensor(
                        out=s_lo[:, i, :], in0=chip.psum[:, b, :],
                        scalar=b2_now[:, dt:dt + 1],
                        in1=s_hi[:, i, :].bitcast(F32), op0=ALU.add, op1=ALU.subtract).then_inc(s_lo_done, 1)

            def token(e, n):
                en = N * e + n
                take_bias(en)
                for k in range(3, KT + 3):
                    lo(KT * (PASSES * e + n + 1) + k, k)
                evacuate(en, FULL)
                dve.wait_ge(s_lo_done, NB * (en + 1))

            for k in range(3):
                lo(k, k)
            dve.wait_ge(consts_loaded, 32)
            normalise(0, 0)
            normalise(0, 1)
            for e in range(2):
                take_bias(N * e)
                for j in range(4):
                    h_low(e, 0, j)
                normalise(e, 2)
                for u in range(UNITS):
                    if u == 4:
                        evacuate(N * e, half_pieces(0))
                    for j in range(4):
                        if u + 1 < UNITS:
                            h_low(e, u + 1, j)
                        lo(KT * PASSES * e + 4 * u + j + 3, 4 * u + j + 3)
                    if u + 3 < UNITS:
                        normalise(e, u + 3)
                evacuate(N * e, half_pieces(1))
                dve.wait_ge(s_lo_done, NB * (N * e + 1))
                if e == 0:
                    normalise(1, 0)
                    normalise(1, 1)
                with dve.Fori(1, N - e) as n:
                    token(e, n)
            take_bias(2 * N - 1)
            for h in range(2):
                for k in range(3, KT if h else KT + 3):
                    lo(KT * (PASSES + N + h) + k, k)
                evacuate(2 * N - 1, last_pieces(h))

        @block.tensor
        def _(pe):
            def turn(e, u):
                pe.wait_ge(z_ready, UNITS * e + u + 1)
                for j in range(4):
                    n = 4 * (UNITS * e + u) + j
                    if u:
                        pe.wait_ge(h_raw_done, n - 4 + 1)
                    elif e:
                        pe.wait_ge(s_lo_done, NB * N * e - NB + j + 1)
                    for r in range(4):
                        mm = pe.transpose(chip.psum[:, 4 + j, r * P:(r + 1) * P],
                                          z[:, u % 2, r, j * P:(j + 1) * P], t["ident"][:, :])
                    mm.then_inc(turned, 1)

            def products(k, pieces, wait_for_bank=None):
                for x, (i, b, dt, half) in enumerate(pieces):
                    if k == 0 and wait_for_bank:
                        wait_for_bank(i, b)
                    cols = slice(dt * P, (dt + 1) * P)
                    rows = slice(half * 512, (half + 1) * 512)
                    mm = mm3(pe, chip.psum[:, b, :], w_hi[:, k % RING, cols], w_lo[:, k % RING, cols],
                             h_hi[:, k, rows], h_lo[:, k, rows], k == 0, k == KT - 1)
                    if x == len(pieces) - 1:
                        mm.then_inc(w_used, 1)
                    elif k == KT - 1:
                        mm.then_inc(acc_done, 1)

            def half_products(e, u):
                h = u // 4
                for j in range(4):
                    k = 4 * (u % 4) + j
                    pe.wait_ge(w_lo_done, KT * (PASSES * e + h) + k + 1)
                    pe.wait_ge(h_lo_done, 4 * (UNITS * e + u) + j + 1)
                    if k == 0 and (e or h):
                        pe.wait_ge(s_lo_done, NB * N * e + 4 * h)
                    products(k, half_pieces(h))

            def token(e, n, is_first):
                def bank_free(i, b):
                    if not is_first:
                        pe.wait_ge(s_lo_done, NB * (N * e + n - 1) + i + 1)
                    elif b < 4:
                        pe.wait_ge(s_lo_done, NB * N * e + 4 + b + 1)
                    else:
                        pe.wait_ge(h_raw_done, 4 * UNITS * (e + 1))

                for k in range(KT):
                    pe.wait_ge(w_lo_done, KT * (PASSES * e + n + 1) + k + 1)
                    products(k, FULL, bank_free)

            pe.sem_inc(w_used, 1)
            for e in range(2):
                turn(e, 0)
                for u in range(UNITS):
                    if u + 1 < UNITS:
                        turn(e, u + 1)
                    half_products(e, u)
                token(e, 1, True)
                with pe.Fori(2, N - e) as n:
                    token(e, n, False)
            for h in range(2):
                for k in range(KT):
                    pe.wait_ge(w_lo_done, KT * (PASSES + N + h) + k + 1)
                    products(k, last_pieces(h), lambda i, b: pe.wait_ge(s_lo_done, NB * (2 * N - 2) + i + 1))


class WeightSplit:

    def __init__(self, chip, tag, raw, sources):
        self.raw, self.sources = raw, sources
        self.loaded = [chip.sem(f"{tag}_loaded{i}") for i in range(len(raw))]
        self.hi_done = chip.sem(tag + "_hi_done")
        self.lo_done = chip.sem(tag + "_lo_done")

    def into(self, parts):
        self.parts = parts

    def slot(self, j):
        return self.raw[j % len(self.raw)][:, 0:self.sources[j][1]]

    def load(self, sp, j):
        if j >= len(self.raw):
            sp.wait_ge(self.lo_done, j - len(self.raw) + 1)
        sp.dma_start(self.slot(j), self.sources[j][0]).then_inc(self.loaded[j % len(self.raw)], 16)

    def hi(self, act, j):
        act.wait_ge(self.loaded[j % len(self.raw)], 16 * (j // len(self.raw) + 1))
        act.activation(self.parts[j][0], self.slot(j), ACT.Copy).then_inc(self.hi_done, 1)

    def lo(self, dve, j):
        dve.wait_ge(self.hi_done, j + 1)
        dve.tensor_tensor(self.parts[j][1], self.slot(j), self.parts[j][0].bitcast(F32), ALU.subtract)\
            .then_inc(self.lo_done, 1)


def group(x, g):
    return x.rearrange("p n q -> p (n q)")[:, g::2]


def sum_pieces(psum, o, j):
    g, odd = j // 2, j % 2
    for half in range(2):
        lanes = slice(half * HD, (half + 1) * HD)
        src = psum[lanes, j, :].rearrange("p (d n q) -> p d n q", n=N, q=32)
        yield o[lanes, :, half ^ odd, :, g:BLK:2].rearrange("p n d q -> p d n q"), src


def attention(nc, chip, t):
    G = BLK // 32
    NV = 32
    QK = ("q_r", "k_r", "q_i", "k_i")
    with ExitStack() as mem:
        def sb(name, shape, dt=F32):
            return mem.enter_context(nc.sbuf_tensor(name, shape, dt))

        w_hi = sb("wc_hi", [P, 6, DT, 512], F32R)
        w_lo = sb("wc_lo", [P, 6, DT, 512], F32R)
        split = WeightSplit(chip, "c_w", [t["ri"][:, i, :, :].rearrange("p c f -> p (c f)") for i in range(4)], [
            (t["wqkv"][m, :, kt:kt + 2, :].rearrange("p k f -> p (k f)"), 1024)
            for m in range(6) for kt in (0, 2)])
        split.into([(w_hi[:, m, kt:kt + 2, :].rearrange("p k f -> p (k f)"),
                     w_lo[:, m, kt:kt + 2, :].rearrange("p k f -> p (k f)")) for m in range(6) for kt in (0, 2)])

        s = [[sb(f"s_{e}{part}", [P, DT, N, BLK], F32R) for part in ("hi", "lo")] for e in "ri"]
        q_r = [sb(f"q_r_{part}", [P, DT, N, BLK], F32R) for part in ("hi", "lo")]
        q_i = [sb(f"q_i_{part}", [P, DT, N, BLK], F32R) for part in ("hi", "lo")]
        k3 = [sb(f"k3_{part}", [P, DT, 3, N, BLK], F32R) for part in ("hi", "lo")]
        v = sb("v", [P, G, DT, 4, HD])
        wt = sb("wt", [P, 2 * G, DT, N * NV])
        o = [sb(f"o_{part}", [P, N, 2, DT, BLK], F32R) for part in ("hi", "lo")]
        picked = sb("picked", [P, 2, 16, NV])
        mask = sb("mask", [P, NV])
        A = G * H
        sc = sb("sc", [P, 2, A, N])
        sq = sb("sq", [P, 2, A * N])
        mag = sb("mag", [P, A, N])
        top = sb("top", [P, A])
        ex = sb("ex", [P, A, N])
        total = sb("total", [P, A])
        wgt = sb("wgt", [P, A, N])
        wgt_t = sb("wgt_t", [P, A, N])
        bqk = sb("bqk", [P, 4, DT])

        def dest(x, m, dt):
            return (q_r[x][:, dt], k3[x][:, dt, 1], q_i[x][:, dt], k3[x][:, dt, 0])[m].rearrange("p n q -> p (n q)")

        consts_loaded = chip.sem("c_consts_loaded")
        mask_done = chip.sem("c_mask_done")
        s_loaded = [chip.sem(f"c_s_loaded{e}") for e in "ri"]
        proj_done = chip.sem("c_proj_done")
        proj_hi = chip.sem("c_proj_hi")
        proj_lo = chip.sem("c_proj_lo")
        neg_done = chip.sem("c_neg_done")
        score_done = chip.sem("c_score_done")
        score_free = chip.sem("c_score_free")
        score_sum = chip.sem("c_score_sum")
        soft = chip.sem("c_soft")
        mag_ready = chip.sem("c_mag_ready")
        ex_ready = chip.sem("c_ex_ready")
        swapped = chip.sem("c_swapped")
        wt_ready = chip.sem("c_wt_ready")
        val_done = chip.sem("c_val_done")
        val_copied = chip.sem("c_val_copied")
        sum_done = chip.sem("c_sum_done")
        sum_hi = chip.sem("c_sum_hi")
        sum_lo = chip.sem("c_sum_lo")
        o_stored = t["o_stored"]
        SOFT = 7

        block = mem.enter_context(nc.Block())

        @block.sync
        def _(sp):
            sp.dma_start(bqk[:, :, :], t["bqk"]).then_inc(consts_loaded, 16)

            def load_s(b):
                for e in range(2):
                    if not (isinstance(b, int) and b == 0):
                        sp.wait_ge(val_done, 4 * b)
                    for part in range(2):
                        sp.dma_start(s[e][part][:, :, :, :].rearrange("p d n q -> p (d n q)").bitcast(F32),
                                     t["sT"][part, e, b].rearrange("p d n q -> p (d n q)"))\
                            .then_inc(s_loaded[e], 16)

            def store_o(i):
                sp.wait_ge(sum_lo, 4 + 4 * (i + 1))
                for part in range(2):
                    sp.dma_start(t["oT"][part, i].rearrange("p n e d q -> p (n e d q)"),
                                 o[part][:, :, :, :, :].rearrange("p n e d q -> p (n e d q)").bitcast(F32))\
                        .then_inc(o_stored, 16)

            sp.sem_inc(o_stored, 32)
            split.load(sp, 0)
            split.load(sp, 1)
            for slot in range(4):
                sp.wait_ge(t["s_stored"][slot], 32 * 2 * N)
            load_s(0)
            for j in range(2, 12):
                split.load(sp, j)
            for slot in range(4, NB):
                sp.wait_ge(t["s_stored"][slot], 32 * (2 * N - 1))
            sp.wait_ge(t["s_last_stored"], 32 * DT)
            with sp.Fori(0, NBLK - 1) as i:
                load_s(i + 1)
                store_o(i)
            sp.wait_ge(split.lo_done, 12)
            for j in range(4):
                t["d_split"].load(sp, j)
            store_o(NBLK - 1)

        @block.tensor
        def _(pe):
            bank = chip.psum

            def projections(b, is_first):
                for j in range(8):
                    m, pair = j // 2, j % 2
                    e = m // 2
                    if j % 4 == 0:
                        pe.wait_ge(s_loaded[e], 32 * (b + 1))
                    if is_first:
                        pe.wait_ge(split.lo_done, 2 * m + 2)
                    if not is_first:
                        pe.wait_ge(score_free, 8 * (b - 1) + j + 1)
                    for d in range(2):
                        dt = 2 * pair + d
                        cols = slice(dt * P, (dt + 1) * P)
                        for kt in range(DT):
                            mm = mm3(pe, bank[:, j, d * 256:(d + 1) * 256],
                                     w_hi[:, m, kt, cols], w_lo[:, m, kt, cols],
                                     s[e][0][:, kt, :, :].rearrange("p n q -> p (n q)"),
                                     s[e][1][:, kt, :, :].rearrange("p n q -> p (n q)"), kt == 0, kt == DT - 1)
                    mm.then_inc(proj_done, 1)

            def values(b):
                for j in range(4):
                    e, g = j // 2, j % 2
                    pe.wait_ge(proj_lo, 8 * b + 4 + j + 1)
                    for kt in range(DT):
                        mm = mm3(pe, bank[:, 4 + j, :], group(s[e][0][:, kt, :, :], g), group(s[e][1][:, kt, :, :], g),
                                 w_hi[:, 4 + e, kt, :], w_lo[:, 4 + e, kt, :], kt == 0, kt == DT - 1)
                    mm.then_inc(val_done, 1)

            def scores(i):
                pe.wait_ge(neg_done, 4 * (i + 1))
                for jj in range(4):
                    g, dtp = jj // 2, jj % 2
                    for j in (2 * jj, 2 * jj + 1):
                        if j < 4:
                            pe.wait_ge(sum_lo, 4 * i + j + 1)
                        else:
                            pe.wait_ge(val_copied, 4 * i + j - 4 + 1)
                    for d in range(2):
                        dt = 2 * dtp + d
                        for n, (q, first) in enumerate(((q_r, 1), (q_i, 0))):
                            for x, y in ((0, 0), (0, 1), (1, 0)):
                                for odd in range(2):
                                    lanes = slice(odd * HD, (odd + 1) * HD)
                                    ks = k3[y][lanes, dt, first:first + 2].rearrange("p c n q -> p c (n q)")[:, :, g::2]
                                    mm = pe.matmul(bank[:, 2 * jj + odd, 256 * d:256 * d + 256],
                                                   group(q[x][lanes, dt], g), ks,
                                                   start=(n, x, y) == (0, 0, 0), stop=(n, x) == (1, 1))
                                    if (d, n, x) == (1, 1, 1):
                                        mm.then_inc(score_done, 1)

            def sums(i, has_next):
                pe.wait_ge(val_copied, 4 * (i + 1))
                for j in range(4):
                    g, odd = j // 2, j % 2
                    pe.wait_ge(wt_ready, 4 * i + j + 1)
                    if has_next:
                        pe.wait_ge(proj_lo, 8 * (i + 1) + j + 1)
                    for dt in range(DT):
                        mm = pe.matmul(bank[:, j, dt * P:(dt + 1) * P],
                                       v[:, g, dt, 2 * odd:2 * odd + 2, :].rearrange("p a d -> p (a d)"),
                                       wt[:, j, dt, :], start=True, stop=True)
                    mm.then_inc(sum_done, 1)

            projections(0, True)
            pe.wait_ge(split.lo_done, 12)
            values(0)
            with pe.Fori(0, NBLK - 1) as i:
                scores(i)
                projections(i + 1, False)
                sums(i, True)
                values(i + 1)
            scores(NBLK - 1)
            sums(NBLK - 1, False)

        @block.scalar
        def _(act):
            bank = chip.psum

            def projections_hi(b):
                for j in range(8):
                    m, pair = j // 2, j % 2
                    act.wait_ge(proj_done, 8 * b + j + 1)
                    for d in range(2):
                        dt = 2 * pair + d
                        a = act.activation(dest(0, m, dt), bank[:, j, d * 256:(d + 1) * 256], ACT.Identity,
                                           bias=bqk[:, m, dt:dt + 1])
                    a.then_inc(proj_hi, 1)

            def values_copy(b):
                for j in range(4):
                    e, g = j // 2, j % 2
                    act.wait_ge(val_done, 4 * b + j + 1)
                    dst = v[:, g, :, 0:4:3, :] if e == 0 else v[:, g, :, 1:3, :]
                    act.activation(dst, bank[:, 4 + j, :].rearrange("p (h a d) -> p h a d", a=2, d=HD), ACT.Copy)\
                        .then_inc(val_copied, 1)

            def sums_hi(i):
                act.wait_ge(o_stored, 32 * (i + 1))
                for j in range(4):
                    act.wait_ge(sum_done, 4 * i + j + 1)
                    for dst, src in sum_pieces(bank, o[0], j):
                        a = act.activation(dst, src, ACT.Copy)
                    a.then_inc(sum_hi, 1)

            def softmax(i):
                act.wait_ge(soft, SOFT * i + 2)
                act.activation(mag[:, :, :], mag[:, :, :], ACT.Sqrt).then_inc(mag_ready, 1)
                act.wait_ge(soft, SOFT * i + 4)
                act.activation(ex[:, :, :], mag[:, :, :], ACT.Exp, scale=HD ** -0.5).then_inc(ex_ready, 1)

            for j in range(12):
                split.hi(act, j)
            act.wait_ge(consts_loaded, 16)
            projections_hi(0)
            values_copy(0)
            with act.Fori(0, NBLK - 1) as i:
                softmax(i)
                projections_hi(i + 1)
                sums_hi(i)
                values_copy(i + 1)
            softmax(NBLK - 1)
            sums_hi(NBLK - 1)

        @block.vector
        def _(dve):
            bank = chip.psum

            def projections_lo(b):
                for j in range(8):
                    m, pair = j // 2, j % 2
                    dve.wait_ge(proj_hi, 8 * b + j + 1)
                    for d in range(2):
                        dt = 2 * pair + d
                        a = dve.scalar_tensor_tensor(out=dest(1, m, dt), in0=bank[:, j, d * 256:(d + 1) * 256],
                                                     scalar=bqk[:, m, dt:dt + 1], in1=dest(0, m, dt).bitcast(F32),
                                                     op0=ALU.add, op1=ALU.subtract)
                    a.then_inc(proj_lo, 1)
                    if m == 3:
                        dve.wait_ge(proj_lo, 8 * b + j + 1)
                        for x in range(2):
                            k_i, k_n = (k3[x][:, 2 * pair:2 * pair + 2, c].rearrange("p d n q -> p d (n q)") for c in (0, 2))
                            dve.tensor_scalar(k_n, k_i.bitcast(F32), -1.0, None, ALU.mult).then_inc(neg_done, 1)

            def pick_scores(i):
                for j in range(9):
                    if j < 8:
                        dve.wait_ge(score_done, 8 * i + j + 1)
                        if j >= 2:
                            dve.wait_ge(score_sum, 8 * i + j - 1)
                        dve.tensor_tensor(picked[:, j % 2, :, :],
                                          bank[:, j, :].rearrange("p (m b) -> p m b", b=NV),
                                          mask[:, :].unsqueeze(1).broadcast_to((P, 16, NV)), ALU.mult)\
                            .then_inc(score_free, 1)
                    if j >= 1:
                        g, dtp, odd = (j - 1) // 4, ((j - 1) // 2) % 2, (j - 1) % 2
                        first = (g * 2 + odd) * DT + 2 * dtp
                        dve.wait_ge(score_free, 8 * i + j)
                        dve.tensor_reduce(sc[:, :, first:first + 2, :].rearrange("p c a m -> p a c m"),
                                          picked[:, (j - 1) % 2, :, :].rearrange("p (a c m) b -> p a c m b", a=2, c=2),
                                          AX, ALU.add).then_inc(score_sum, 1)

            def softmax(i):
                def flat(x):
                    return x.rearrange("p a m -> p (a m)")

                wide = (P, A, N)
                dve.wait_ge(score_sum, 8 * (i + 1))
                dve.tensor_tensor(sq[:, :, :], sc[:, :, :, :].rearrange("p c a m -> p c (a m)"),
                                  sc[:, :, :, :].rearrange("p c a m -> p c (a m)"), ALU.mult).then_inc(soft, 1)
                dve.wait_ge(soft, SOFT * i + 1)
                dve.scalar_tensor_tensor(out=flat(mag[:, :, :]), in0=sq[:, 0, :], scalar=1e-8, in1=sq[:, 1, :],
                                         op0=ALU.add, op1=ALU.add).then_inc(soft, 1)
                dve.wait_ge(mag_ready, i + 1)
                dve.tensor_reduce(top[:, :], mag[:, :, :], AX, ALU.max).then_inc(soft, 1)
                dve.wait_ge(soft, SOFT * i + 3)
                dve.tensor_tensor(mag[:, :, :], mag[:, :, :], top[:, :].unsqueeze(2).broadcast_to(wide),
                                  ALU.subtract).then_inc(soft, 1)
                dve.wait_ge(ex_ready, i + 1)
                dve.tensor_reduce(total[:, :], ex[:, :, :], AX, ALU.add).then_inc(soft, 1)
                dve.wait_ge(soft, SOFT * i + 5)
                dve.reciprocal(total[:, :], total[:, :]).then_inc(soft, 1)
                dve.wait_ge(soft, SOFT * i + 6)
                dve.tensor_tensor(wgt[:, :, :], ex[:, :, :], total[:, :].unsqueeze(2).broadcast_to(wide),
                                  ALU.mult).then_inc(soft, 1)
                dve.wait_ge(soft, SOFT * i + 7)

            def spread_weights(i):
                for n in range(N):
                    for m in range(N):
                        c = dve.tensor_copy(wgt_t[m * NV:(m + 1) * NV, :, n], wgt[n * NV:(n + 1) * NV, :, m])
                c.then_inc(swapped, 1)
                dve.wait_ge(swapped, i + 1)
                for j in range(4):
                    dve.tensor_tensor(wt[:, j, :, :].rearrange("p d (n b) -> p (d n) b", b=NV),
                                      wgt_t[:, 4 * j:4 * j + 4, :].rearrange("p a n -> p (a n)").unsqueeze(2)
                                      .broadcast_to((P, 16, NV)),
                                      mask[:, :].unsqueeze(1).broadcast_to((P, 16, NV)), ALU.mult)\
                        .then_inc(wt_ready, 1)

            def sums_lo(i):
                for j in range(4):
                    dve.wait_ge(sum_hi, 4 * i + j + 1)
                    for (lo, src), (hi, _) in zip(sum_pieces(bank, o[1], j), sum_pieces(bank, o[0], j)):
                        a = dve.tensor_tensor(lo, src, hi.bitcast(F32), ALU.subtract)
                    a.then_inc(sum_lo, 1)

            dve.sem_inc(sum_lo, 4)
            dve.tensor_reduce(mask[:, :], t["ident"][:, :].rearrange("p (m b) -> p b m", b=NV), AX, ALU.add)\
                .then_inc(mask_done, 1)
            for j in range(12):
                split.lo(dve, j)
            dve.wait_ge(mask_done, 1)
            dve.wait_ge(consts_loaded, 16)
            projections_lo(0)
            with dve.Fori(0, NBLK - 1) as i:
                pick_scores(i)
                softmax(i)
                spread_weights(i)
                projections_lo(i + 1)
                sums_lo(i)
            pick_scores(NBLK - 1)
            softmax(NBLK - 1)
            spread_weights(NBLK - 1)
            sums_lo(NBLK - 1)


def interaction_products(nc, chip, t):
    HALF = B // 2
    with ExitStack() as mem:
        def sb(name, shape, dt=F32):
            return mem.enter_context(nc.sbuf_tensor(name, shape, dt))

        wo = [sb(f"wo_{part}", [P, 2, DT, 512], F32R) for part in ("hi", "lo")]
        bv = [sb(f"bv_{part}", [P, 2, DT, 2], F32R) for part in ("hi", "lo")]
        ri = t["ri"]
        split = t["d_split"]
        split.into([(bv[0][:, :, :, :].rearrange("p e d c -> p (e d c)"), bv[1][:, :, :, :].rearrange("p e d c -> p (e d c)"))] +
                   [(wo[0][:, e, kt:kt + 2, :].rearrange("p k f -> p (k f)"),
                     wo[1][:, e, kt:kt + 2, :].rearrange("p k f -> p (k f)")) for e in range(2) for kt in (0, 2)])

        o = [[sb(f"oT_{half}{part}", [P, HALF // BLK, 2, DT, BLK], F32R) for part in ("hi", "lo")] for half in range(2)]
        attn = [sb(f"attn_{part}", [P, 2, DT, HALF], F32R) for part in ("hi", "lo")]
        w_raw = sb("wi_raw", [P, 2, DT, 512])
        w = [sb(f"wi_{part}", [P, 2, DT, 512], F32R) for part in ("hi", "lo")]
        rr = sb("rr", [P, 2, 512])
        bo = sb("bo", [P, 2, DT])

        consts_loaded = chip.sem("d_consts_loaded")
        bias_done = chip.sem("d_bias_done")
        bias_ready = chip.sem("d_bias_ready")
        o_loaded = [chip.sem(f"d_o_loaded{half}") for half in range(2)]
        w_loaded = chip.sem("d_w_loaded")
        w_hi = chip.sem("d_w_hi")
        w_lo = chip.sem("d_w_lo")
        attn_done = chip.sem("d_attn_done")
        attn_hi = chip.sem("d_attn_hi")
        attn_lo = chip.sem("d_attn_lo")
        ri_done = chip.sem("d_ri_done")
        rr_copied = chip.sem("d_rr_copied")
        r_done = chip.sem("d_r_done")
        i_done = chip.sem("d_i_done")
        ri_stored = t["ri_stored"]

        block = mem.enter_context(nc.Block())

        @block.sync
        def _(sp):
            sp.dma_start(bo[:, :, :], t["bo"]).then_inc(consts_loaded, 16)

            def load_w(n):
                if not (isinstance(n, int) and n == 0):
                    sp.wait_ge(w_lo, 8 * n)
                sp.dma_start(w_raw[:, :, :, :].rearrange("p m k f -> p (m k f)"),
                             t["wint"][n].rearrange("p m k f -> p (m k f)")).then_inc(w_loaded, 16)

            def load_o(n, half, is_first):
                if not is_first:
                    sp.wait_ge(attn_done, 8 * (2 * n + half - 1))
                for part in range(2):
                    sp.dma_start(o[half][part][:, :, :, :, :].rearrange("p b e d q -> p b (e d q)").bitcast(F32),
                                 t["oT"][part, half * 8:half * 8 + 8, :, n].rearrange("b p e d q -> p b (e d q)"))\
                        .then_inc(o_loaded[half], 16)

            split.load(sp, 4)
            sp.wait_ge(t["o_stored"], 32 * (NBLK // 2 + 1))
            load_o(0, 0, True)
            load_w(0)
            sp.wait_ge(t["o_stored"], 32 * (NBLK + 1))
            load_o(0, 1, True)
            with sp.Fori(1, N) as n:
                load_o(n, 0, False)
                load_w(n)
                load_o(n, 1, False)
            for r in range(4):
                sp.wait_ge(r_done, 4 * (2 * N - 1) + r + 5)
                sp.wait_ge(i_done, 4 * (2 * N - 1) + r + 5)
                sp.dma_start(t["RI"][4 + r, :, N - 1], ri[:, r, :, :]).then_inc(t["ri_last_stored"], 16)

        @block.gpsimd
        def _(pool):
            def store(n, half):
                u = 2 * n + half
                for r in range(4):
                    pool.wait_ge(r_done, 4 * u + r + 5)
                    pool.wait_ge(i_done, 4 * u + r + 5)
                    pool.dma_start(t["RI"][4 * half + r, :, n], ri[:, r, :, :]).then_inc(ri_stored[r], 16)

            with pool.Fori(0, N - 1) as n:
                store(n, 0)
                store(n, 1)
            store(N - 1, 0)

        @block.tensor
        def _(pe):
            bank = chip.psum

            def attn_products(n, half):
                u = 2 * n + half
                pe.wait_ge(o_loaded[half], 32 * (n + 1))
                for j in range(8):
                    e, dt = j // 4, j % 4
                    pe.wait_ge(r_done, 4 * u + 3 + j // 4)
                    pe.wait_ge(i_done, 4 * u + 3 + j // 4)
                    for kt in range(DT):
                        cols = slice(dt * P, (dt + 1) * P)
                        mm = mm3(pe, bank[:, j, :], wo[0][:, e, kt, cols], wo[1][:, e, kt, cols],
                                 o[half][0][:, :, e, kt, :], o[half][1][:, :, e, kt, :], kt == 0, kt == DT - 1)
                    mm.then_inc(attn_done, 1)

            def ri_products(n, half):
                u = 2 * n + half
                pe.wait_ge(attn_lo, 8 * (u + 1))
                pe.wait_ge(w_lo, 8 * (n + 1))
                for r in range(4):
                    if r >= 2:
                        pe.wait_ge(r_done, 4 * u + r - 2 + 5)
                        pe.wait_ge(i_done, 4 * u + r - 2 + 5)
                    rows = slice(r * P, (r + 1) * P)
                    first = 4 * (r % 2)
                    for j, terms in enumerate((((0, 0),), ((1, 1),), ((0, 1), (1, 0)))):
                        for a, (e, m) in enumerate(terms):
                            for kt in range(DT):
                                mm = mm3(pe, bank[:, first + j, :], attn[0][:, e, kt, rows], attn[1][:, e, kt, rows],
                                         w[0][:, m, kt, :], w[1][:, m, kt, :],
                                         (a, kt) == (0, 0), (a, kt) == (len(terms) - 1, DT - 1))
                        mm.then_inc(ri_done, 1)

            for e in range(2):
                pe.wait_ge(split.lo_done, 2 * e + 3)
                for dt in range(DT):
                    for kt in range(DT):
                        cols = slice(dt * P, (dt + 1) * P)
                        mm = mm3(pe, bank[:, 3, (e * DT + dt) * 2:(e * DT + dt) * 2 + 2],
                                 wo[0][:, e, kt, cols], wo[1][:, e, kt, cols],
                                 bv[0][:, e, kt, :], bv[1][:, e, kt, :], kt == 0, kt == DT - 1)
            mm.then_inc(bias_done, 1)
            pe.wait_ge(bias_ready, 1)
            with pe.Fori(0, N) as n:
                for half in range(2):
                    attn_products(n, half)
                    ri_products(n, half)

        @block.scalar
        def _(act):
            bank = chip.psum

            def unit(n, half):
                u = 2 * n + half
                if half == 0:
                    act.wait_ge(w_loaded, 16 * (n + 1))
                for j in range(8):
                    e, dt = j // 4, j % 4
                    if half == 0:
                        act.activation(w[0][:, e, dt, :], w_raw[:, e, dt, :], ACT.Copy).then_inc(w_hi, 1)
                    act.wait_ge(attn_done, 8 * u + j + 1)
                    act.activation(attn[0][:, e, dt, :], bank[:, j, :], ACT.Identity,
                                   bias=bo[:, e, dt:dt + 1]).then_inc(attn_hi, 1)
                for r in range(4):
                    first = 4 * (r % 2)
                    act.wait_ge(ri_done, 12 * u + 3 * r + 1)
                    act.wait_ge(r_done, 4 * u + r + 3)
                    act.activation(rr[:, r % 2, :], bank[:, first, :], ACT.Copy).then_inc(rr_copied, 1)
                    if not (isinstance(u, int) and u == 0):
                        act.wait_ge(ri_stored[r], 16 * u)
                    act.wait_ge(ri_done, 12 * u + 3 * r + 3)
                    act.activation(ri[:, r, 1, :], bank[:, first + 2, :], ACT.Copy).then_inc(i_done, 1)

            for j in range(5):
                split.hi(act, j)
            act.sem_inc(i_done, 4)
            act.wait_ge(bias_ready, 1)
            unit(0, 0)
            unit(0, 1)
            with act.Fori(1, N) as n:
                unit(n, 0)
                unit(n, 1)

        @block.vector
        def _(dve):
            bank = chip.psum

            def unit(n, half):
                u = 2 * n + half
                for j in range(8):
                    e, dt = j // 4, j % 4
                    if half == 0:
                        dve.wait_ge(w_hi, 8 * n + j + 1)
                        dve.tensor_tensor(w[1][:, e, dt, :], w_raw[:, e, dt, :], w[0][:, e, dt, :].bitcast(F32),
                                          ALU.subtract).then_inc(w_lo, 1)
                    dve.wait_ge(attn_hi, 8 * u + j + 1)
                    dve.scalar_tensor_tensor(out=attn[1][:, e, dt, :], in0=bank[:, j, :],
                                             scalar=bo[:, e, dt:dt + 1], in1=attn[0][:, e, dt, :].bitcast(F32),
                                             op0=ALU.add, op1=ALU.subtract).then_inc(attn_lo, 1)
                for r in range(4):
                    first = 4 * (r % 2)
                    dve.wait_ge(rr_copied, 4 * u + r + 1)
                    if not (isinstance(u, int) and u == 0):
                        dve.wait_ge(ri_stored[r], 16 * u)
                    dve.wait_ge(ri_done, 12 * u + 3 * r + 2)
                    dve.tensor_tensor(ri[:, r, 0, :], rr[:, r % 2, :], bank[:, first + 1, :],
                                      ALU.subtract).then_inc(r_done, 1)

            for j in range(5):
                split.lo(dve, j)
            dve.sem_inc(r_done, 4)
            dve.wait_ge(consts_loaded, 16)
            dve.wait_ge(bias_done, 1)
            dve.tensor_tensor(bo[:, :, :].rearrange("p e d -> p (e d)"), bo[:, :, :].rearrange("p e d -> p (e d)"),
                              bank[:, 3, 0:16:2], ALU.add).then_inc(bias_ready, 1)
            dve.wait_ge(bias_ready, 1)
            unit(0, 0)
            unit(0, 1)
            with dve.Fori(1, N) as n:
                unit(n, 0)
                unit(n, 1)


def interference_and_top(nc, chip, t, out):
    PAIRS = ((0, 1), (0, 2), (0, 3), (1, 2), (1, 3), (2, 3))
    OFF = [(i, j) for i in range(N) for j in range(N) if i != j]
    W = 2 * P
    with ExitStack() as mem:
        def sb(name, shape, dt=F32):
            return mem.enter_context(nc.sbuf_tensor(name, shape, dt))

        def parts(name, shape):
            return [sb(f"{name}_{part}", shape, F32R) for part in ("hi", "lo")]

        wm = parts("wm", [P, 2, DT, 512])
        wp = parts("wp", [P, DT, 512])
        w1 = parts("wt1", [P, DT, 512])
        w2 = parts("wt2", [P, DT, 256])
        pieces = []
        for m in range(2):
            for kt in (0, 2):
                pieces.append((t["wm"][m, :, kt:kt + 2, :], [x[:, m, kt:kt + 2, :] for x in wm]))
        for src, dst in ((t["wp"], wp), (t["wt1"], w1)):
            for kt in (0, 2):
                pieces.append((src[:, kt:kt + 2, :], [x[:, kt:kt + 2, :] for x in dst]))
        pieces.append((t["wt2"], [x[:, :, :] for x in w2]))
        ri = sb("ri_in", [P, 2, N, 2, 512])
        u = sb("u", [P, N, 2, 512])
        norm2, inv = u[:, :, 0, :], u[:, :, 1, :]
        pair = sb("pair", [P, 12, 512])
        zero = sb("zero", [P, N, 512])
        sup = [ri[:, par, 0, :, :] for par in range(2)]
        sumsq = sb("sumsq", [P, 2])
        inorm = sb("inorm", [P, 2])
        strength = sb("strength_now", [P, 2, N * N])
        diag = sb("diag", [P, 2, len(OFF), P])
        sup_t = [parts(f"sup_t{c}", [P, DT, W]) for c in ("r", "i", "n")]
        act_t = parts("act_t", [P, DT, W])
        raw_t = sb("raw_t", [P, DT, W])
        rows_x = sb("rows_x", [P, 2, 512])
        vstats = sb("vstats", [P, 2, 6])
        vmean = sb("vmean", [P, 2, 2])
        vstd = sb("vstd", [P, 2])
        split = WeightSplit(chip, "e_w", [raw_t[:, :, :].rearrange("p d q -> p (d q)"),
                                          rows_x[:, :, :].rearrange("p c f -> p (c f)")],
                            [(src.rearrange("p k f -> p (k f)"), 1024) for src, _ in pieces])
        split.into([tuple(x.rearrange("p k f -> p (k f)") for x in dst) for _, dst in pieces])
        PIECES = len(pieces)
        y_row = raw_t[0:1, 2, :]
        post_b = sb("post_b", [P, 512])
        post_ln = sb("post_ln", [P, 2, DT])
        top_b2 = sb("top_b2", [P, 2])
        top_w3 = sb("top_w3", [P, 2])

        consts_loaded = chip.sem("e_consts_loaded")
        ri_loaded = [chip.sem(f"e_ri_loaded{i}") for i in range(2)]
        strength_ready = chip.sem("e_strength_ready")
        diag_ready = chip.sem("e_diag_ready")
        squared = chip.sem("e_squared")
        norm2_ready = chip.sem("e_norm2_ready")
        inv_guess = chip.sem("e_inv_guess")
        unit_ready = chip.sem("e_unit_ready")
        prod_ready = chip.sem("e_prod_ready")
        cos_ready = chip.sem("e_cos_ready")
        zero_used = chip.sem("e_zero_used")
        weight_done = chip.sem("e_weight_done")
        part_ready = chip.sem("e_part_ready")
        sup_step = chip.sem("e_sup_step")
        sup_turned = chip.sem("e_sup_turned")
        sumsq_ready = chip.sem("e_sumsq_ready")
        sup_hi = chip.sem("e_sup_hi")
        sup_lo = chip.sem("e_sup_lo")
        norm_step = chip.sem("e_norm_step")
        norm_root = chip.sem("e_norm_root")
        meas_done = chip.sem("e_meas_done")
        meas_sq = chip.sem("e_meas_sq")
        amp2_ready = chip.sem("e_amp2_ready")
        amp_ready = chip.sem("e_amp_ready")
        amp_hi = chip.sem("e_amp_hi")
        amp_lo = chip.sem("e_amp_lo")
        post_done = chip.sem("e_post_done")
        post_step = chip.sem("e_post_step")
        std_ready = chip.sem("e_std_ready")
        z_turned = chip.sem("e_z_turned")
        z_raw = chip.sem("e_z_raw")
        z_hi = chip.sem("e_z_hi")
        z_lo = chip.sem("e_z_lo")
        hx_loaded = chip.sem("e_hx_loaded")
        top1_done = chip.sem("e_top1_done")
        h_raw = chip.sem("e_h_raw")
        h_hi = chip.sem("e_h_hi")
        h_lo = chip.sem("e_h_lo")
        top2_done = chip.sem("e_top2_done")
        h2_ready = chip.sem("e_h2_ready")
        y_done = chip.sem("e_y_done")
        y_copied = chip.sem("e_y_copied")
        stored = chip.sem("e_stored")

        def flat(x):
            return x.rearrange("p a b -> p (a b)")

        block = mem.enter_context(nc.Block())

        @block.sync
        def _(sp):
            def load(r, par, is_first):
                if not is_first:
                    sp.wait_ge(sumsq_ready, r - 1)
                sp.dma_start(ri[:, par, :, :, :], t["RI"][r]).then_inc(ri_loaded[par], 16)

            for r in range(4):
                sp.wait_ge(t["ri_stored"][r], 16 * (2 * N - 1))
            load(0, 0, True)
            split.load(sp, 0)
            split.load(sp, 1)
            load(1, 1, True)
            sp.dma_start(post_b[:, :], t["post_b"].partition_broadcast(P)).then_inc(consts_loaded, 16)
            sp.dma_start(top_b2[:, :], t["top_b2"]).then_inc(consts_loaded, 16)
            sp.dma_start(top_w3[:, :], t["top_w3"]).then_inc(consts_loaded, 16)
            sp.dma_start(post_ln[:, :, :], t["post_ln"]).then_inc(consts_loaded, 16)
            for j in range(2, PIECES):
                split.load(sp, j)
            sp.wait_ge(t["ri_last_stored"], 16 * 4)
            with sp.Fori(1, RT // 2) as p:
                load(2 * p, 0, False)
                load(2 * p + 1, 1, False)

        @block.gpsimd
        def _(pool):
            pool.wait_ge(t["y_last_stored"], 16 * RT)
            with pool.Fori(0, RT // 2) as q:
                pool.wait_ge(z_turned, 2 * (q + 1))
                pool.dma_start(rows_x[:, :, :], t["y"][8, bass.ds(2 * q, 2)].rearrange("r p f -> p r f"))\
                    .then_inc(hx_loaded, 16)
                pool.wait_ge(y_copied, q + 1)
                pool.dma_start(out[bass.ds(W * q, W), :].rearrange("b c -> c b"), y_row).then_inc(stored, 16)
            pool.wait_ge(stored, 16 * (RT // 2))

        @block.tensor
        def _(pe):
            bank = chip.psum
            ident = t["ident"]

            def weigh(par, i, j, x, start, stop):
                return pe.matmul(bank[:, j, :], diag[:, par, OFF.index((i, j)), :], x,
                                 start=start, stop=stop, skip_group_check=True)

            def weights_zero(r, par, is_first):
                pe.wait_ge(diag_ready, r + 1)
                pe.wait_ge(norm2_ready, 3 * r + 2)
                for j in range(N):
                    if not is_first:
                        pe.wait_ge(part_ready, 4 * (r - 1) + j + 1)
                    others = [i for i in range(N) if i != j]
                    for i in others:
                        mm = weigh(par, i, j, zero[:, i, :], i == others[0], False)
                mm.then_inc(zero_used, 1)

            def weights_cos(r, par, i):
                pe.wait_ge(cos_ready, 3 * r + i + 1)
                for n, (a, b) in enumerate(PAIRS):
                    if a == i:
                        weigh(par, a, b, pair[:, n, :], False, False)
                        mm = weigh(par, b, a, pair[:, n, :], False, n == len(PAIRS) - 1)
                if i == 2:
                    mm.then_inc(weight_done, 1)

            def turn(dst, src, signal):
                for d in range(DT):
                    mm = pe.transpose(bank[:, dst, d * P:(d + 1) * P], src[:, d * P:(d + 1) * P], ident[:, :])
                mm.then_inc(signal, 1)

            def turn_sup(r, par, has_before):
                pe.wait_ge(sup_step, 2 * (r + 1))
                if has_before:
                    pe.wait_ge(sup_lo, 3 * r)
                turn(4, sup[par][:, 0, :], sup_turned)
                turn(5, sup[par][:, 1, :], sup_turned)

            def measure(q):
                pe.wait_ge(split.lo_done, PIECES)
                pe.wait_ge(sup_lo, 6 * (q + 1))
                for d, b in enumerate((6, 7, 4, 5)):
                    cols = slice(d * P, (d + 1) * P)
                    for c, terms in enumerate((((0, 0), (1, 2)), ((1, 0), (0, 1)))):
                        for n, (m, x) in enumerate(terms):
                            for kt in range(DT):
                                mm = mm3(pe, bank[:, b, c * W:(c + 1) * W], wm[0][:, m, kt, cols], wm[1][:, m, kt, cols],
                                         sup_t[x][0][:, kt, :], sup_t[x][1][:, kt, :],
                                         (n, kt) == (0, 0), (n, kt) == (1, DT - 1))
                    mm.then_inc(meas_done, 1)

            def post(q):
                pe.wait_ge(amp_lo, 2 * (q + 1))
                for h in range(2):
                    rows = slice(h * P, (h + 1) * P)
                    for kt in range(DT):
                        mm = mm3(pe, bank[:, 6 + h, :], act_t[0][:, kt, rows], act_t[1][:, kt, rows],
                                 wp[0][:, kt, :], wp[1][:, kt, :], kt == 0, kt == DT - 1)
                    mm.then_inc(post_done, 1)

            def turn_z(q):
                pe.wait_ge(post_step, 10 * (q + 1))
                turn(6, rows_x[:, 0, :], z_turned)
                turn(7, rows_x[:, 1, :], z_turned)

            def top1(q):
                pe.wait_ge(z_lo, q + 1)
                for d in range(DT):
                    cols = slice(d * P, (d + 1) * P)
                    first = (d % 2) * W
                    for kt in range(DT):
                        if kt == DT - 1:
                            if d == 0:
                                pe.wait_ge(hx_loaded, 16 * (q + 1))
                            for h in range(2):
                                pe.matmul(bank[:, 6 + d // 2, first + h * P:first + (h + 1) * P],
                                          rows_x[:, h, d * P:(d + 1) * P], ident[:, :], start=False, stop=False,
                                          skip_group_check=True)
                        mm = mm3(pe, bank[:, 6 + d // 2, first:first + W], w1[0][:, kt, cols], w1[1][:, kt, cols],
                                 act_t[0][:, kt, :], act_t[1][:, kt, :], kt == 0, kt == DT - 1)
                mm.then_inc(top1_done, 1)

            def top2(q, r):
                pe.wait_ge(h_lo, q + 1)
                pe.wait_ge(sup_lo, 3 * (r + 1))
                for m in range(2):
                    cols = slice(m * P, (m + 1) * P)
                    for kt in range(DT):
                        mm = mm3(pe, bank[:, 4, m * W:(m + 1) * W], w2[0][:, kt, cols], w2[1][:, kt, cols],
                                 act_t[0][:, kt, :], act_t[1][:, kt, :], kt == 0, kt == DT - 1)
                mm.then_inc(top2_done, 1)

            def top3(q):
                pe.wait_ge(consts_loaded, 64)
                pe.wait_ge(h2_ready, q + 1)
                for m in range(2):
                    mm = pe.matmul(bank[0:1, 7, 0:W], top_w3[:, m:m + 1], raw_t[:, m, :], start=m == 0, stop=m == 1)
                mm.then_inc(y_done, 1)

            def step(p, has_tail):
                r = 2 * p
                weights_zero(r, 0, not has_tail)
                if has_tail:
                    turn_sup(r - 1, 1, True)
                    measure(p - 1)
                weights_cos(r, 0, 0)
                weights_cos(r, 0, 1)
                if has_tail:
                    post(p - 1)
                weights_cos(r, 0, 2)
                if has_tail:
                    turn_z(p - 1)
                weights_zero(r + 1, 1, False)
                turn_sup(r, 0, has_tail)
                if has_tail:
                    top1(p - 1)
                weights_cos(r + 1, 1, 0)
                weights_cos(r + 1, 1, 1)
                if has_tail:
                    top2(p - 1, r)
                weights_cos(r + 1, 1, 2)
                if has_tail:
                    top3(p - 1)

            step(0, False)
            with pe.Fori(1, RT // 2) as p:
                step(p, True)
            q = RT // 2 - 1
            turn_sup(RT - 1, 1, True)
            measure(q)
            post(q)
            turn_z(q)
            top1(q)
            top2(q, RT - 1)
            top3(q)

        @block.scalar
        def _(act):
            bank = chip.psum

            def make_diag(r, par, is_first):
                act.wait_ge(strength_ready, r + 1)
                if not is_first:
                    act.wait_ge(weight_done, r - 1)
                for n, (i, j) in enumerate(OFF):
                    a = act.activation(diag[:, par, n, :], t["ident"][:, :], ACT.Copy,
                                       scale=strength[:, par, i * N + j:i * N + j + 1])
                a.then_inc(diag_ready, 1)

            def square(r, par, is_first):
                act.wait_ge(ri_loaded[par], 16 * ((r - par) // 2 + 1) if isinstance(r, int) else 8 * (r - par) + 16)
                if not is_first:
                    act.wait_ge(prod_ready, 3 * r)
                act.activation(u[:, :, :, :], ri[:, par, :, :, :], ACT.Square).then_inc(squared, 1)

            def guess_inv(r):
                act.wait_ge(norm2_ready, 3 * (r + 1))
                act.activation(inv, norm2, ACT.Ln).then_inc(inv_guess, 1)
                act.wait_ge(inv_guess, 2 * r + 1)
                act.activation(inv, inv, ACT.Exp, scale=-0.5).then_inc(inv_guess, 1)

            def split_sup(r, par, has_before):
                cols = slice(par * P, (par + 1) * P)
                for n, (c, scale) in enumerate(((0, 1.0), (1, 1.0), (1, -1.0))):
                    act.wait_ge(sup_turned, 2 * r + c + 1)
                    if has_before and par == 0 and n == 0:
                        act.wait_ge(meas_done, 2 * r)
                    act.activation(sup_t[n][0][:, :, cols], bank[:, 4 + c, :].rearrange("p (d q) -> p d q", q=P),
                                   ACT.Copy, scale=scale).then_inc(sup_hi, 1)
                if has_before and par == 0:
                    act.wait_ge(norm_step, r)
                act.activation(flat(sup[par]), flat(sup[par]), ACT.Square,
                               accum_out=sumsq[:, par:par + 1]).then_inc(sumsq_ready, 1)

            def norm(q):
                act.wait_ge(norm_step, 2 * q + 1)
                act.activation(inorm[:, :], inorm[:, :], ACT.Sqrt).then_inc(norm_root, 1)

            def amp(q, h):
                b = (6, 4)[h]
                act.wait_ge(meas_done, 4 * q + 2 * h + 2)
                if h:
                    act.wait_ge(amp2_ready, 2 * q + 1)
                act.activation(rows_x[:, :, :], bank[:, b:b + 2, :], ACT.Square).then_inc(meas_sq, 1)
                act.wait_ge(amp2_ready, 2 * q + h + 1)
                act.activation(raw_t[:, 2 * h:2 * h + 2, :], raw_t[:, 2 * h:2 * h + 2, :], ACT.Sqrt).then_inc(amp_ready, 1)
                act.wait_ge(amp_ready, 2 * q + h + 1)
                act.activation(act_t[0][:, 2 * h:2 * h + 2, :], raw_t[:, 2 * h:2 * h + 2, :], ACT.Copy).then_inc(amp_hi, 1)

            def std(q):
                act.wait_ge(post_step, 10 * q + 7)
                act.activation(vstd[:, :], vstd[:, :], ACT.Sqrt).then_inc(std_ready, 1)

            def gelu(q):
                act.wait_ge(consts_loaded, 64)
                act.wait_ge(z_turned, 2 * (q + 1))
                for d in range(DT):
                    a = act.activation(raw_t[:, d, :].rearrange("p (h q) -> p h q", q=P),
                                       bank[:, 6:8, d * P:(d + 1) * P], ACT.Gelu,
                                       bias=post_ln[:, 1, d:d + 1], scale=post_ln[:, 0, d:d + 1])
                a.then_inc(z_raw, 1)
                act.wait_ge(z_raw, q + 1)
                act.activation(act_t[0][:, :, :], raw_t[:, :, :], ACT.Copy).then_inc(z_hi, 1)

            def relu1(q):
                act.wait_ge(top1_done, q + 1)
                act.activation(flat(raw_t[:, :, :]), flat(bank[:, 6:8, :]), ACT.Relu).then_inc(h_raw, 1)
                act.wait_ge(h_raw, q + 1)
                act.activation(act_t[0][:, :, :], raw_t[:, :, :], ACT.Copy).then_inc(h_hi, 1)

            def relu2(q):
                act.wait_ge(top2_done, q + 1)
                for m in range(2):
                    a = act.activation(raw_t[:, m, :], bank[:, 4, m * W:(m + 1) * W], ACT.Relu, bias=top_b2[:, m:m + 1])
                a.then_inc(h2_ready, 1)

            def copy_y(q):
                act.wait_ge(y_done, q + 1)
                act.activation(y_row, bank[0:1, 7, 0:W], ACT.Copy).then_inc(y_copied, 1)

            def step(p, has_tail, has_before, has_next):
                r, q = 2 * p, p - 1
                if not has_tail:
                    split.hi(act, 2)
                    split.hi(act, 3)
                if has_tail:
                    split_sup(r - 1, 1, has_before)
                    norm(q)
                make_diag(r + 1, 1, not has_tail)
                if has_tail:
                    amp(q, 0)
                square(r + 1, 1, False)
                if has_tail:
                    amp(q, 1)
                else:
                    split.hi(act, 4)
                    split.hi(act, 5)
                if has_tail:
                    std(q)
                guess_inv(r + 1)
                if has_tail:
                    gelu(q)
                else:
                    split.hi(act, 6)
                    split.hi(act, 7)
                split_sup(r, 0, has_tail)
                if not has_tail:
                    split.hi(act, 8)
                if has_next:
                    make_diag(r + 2, 0, False)
                if has_tail:
                    relu1(q)
                if has_next:
                    square(r + 2, 0, False)
                if has_tail:
                    relu2(q)
                if has_next:
                    guess_inv(r + 2)
                if has_tail:
                    copy_y(q)

            make_diag(0, 0, True)
            square(0, 0, True)
            split.hi(act, 0)
            split.hi(act, 1)
            guess_inv(0)
            LAST = RT // 2 - 1
            step(0, False, False, True)
            step(1, True, False, True)
            with act.Fori(2, LAST) as p:
                step(p, True, True, True)
            step(LAST, True, True, False)
            split_sup(RT - 1, 1, True)
            norm(LAST)
            amp(LAST, 0)
            amp(LAST, 1)
            std(LAST)
            gelu(LAST)
            relu1(LAST)
            relu2(LAST)
            copy_y(LAST)

        @block.vector
        def _(dve):
            bank = chip.psum

            def copy_strength(r, par):
                dve.tensor_copy(strength[:, par, :], t["strength"][:, r, :]).then_inc(strength_ready, 1)

            def sum_squares(r, is_first):
                dve.wait_ge(squared, r + 1)
                dve.tensor_tensor(norm2, norm2, inv, ALU.add).then_inc(norm2_ready, 1)
                dve.wait_ge(norm2_ready, 3 * r + 1)
                if not is_first:
                    dve.wait_ge(zero_used, r)
                dve.tensor_scalar(zero[:, :, :], norm2, 0.0, None, ALU.is_equal).then_inc(norm2_ready, 1)
                dve.wait_ge(norm2_ready, 3 * r + 2)
                dve.tensor_scalar(norm2, norm2, 1e-37, None, ALU.max).then_inc(norm2_ready, 1)

            def newton(r):
                dve.wait_ge(inv_guess, 2 * (r + 1))
                dve.tensor_tensor(norm2, norm2, inv, ALU.mult).then_inc(unit_ready, 1)
                dve.wait_ge(unit_ready, 4 * r + 1)
                dve.scalar_tensor_tensor(out=norm2, in0=norm2, scalar=-0.5, in1=inv,
                                         op0=ALU.mult, op1=ALU.mult).then_inc(unit_ready, 1)
                dve.wait_ge(unit_ready, 4 * r + 2)
                dve.scalar_tensor_tensor(out=inv, in0=norm2, scalar=1.5, in1=inv,
                                         op0=ALU.add, op1=ALU.mult).then_inc(unit_ready, 1)

            def unit(r, par):
                dve.wait_ge(unit_ready, 4 * r + 3)
                dve.tensor_tensor(u[:, :, :, :], ri[:, par, :, :, :], inv.unsqueeze(2).broadcast_to((P, N, 2, 512)),
                                  ALU.mult).then_inc(unit_ready, 1)

            def cosines(r):
                dve.wait_ge(unit_ready, 4 * (r + 1))
                for i in range(3):
                    first, n = (0, 3, 5)[i], 3 - i
                    both = pair[:, :, :].rearrange("p (c j) f -> p j c f", c=2)[:, first:first + n]
                    dve.tensor_tensor(both, u[:, i + 1:N, :, :], u[:, i:i + 1, :, :].broadcast_to((P, n, 2, 512)),
                                      ALU.mult).then_inc(prod_ready, 1)
                    dve.wait_ge(prod_ready, 3 * r + i + 1)
                    dve.tensor_tensor(pair[:, first:first + n, :], pair[:, first:first + n, :],
                                      pair[:, 6 + first:6 + first + n, :], ALU.add).then_inc(cos_ready, 1)

            def shares(r, par):
                dve.wait_ge(weight_done, r + 1)
                for j in range(N):
                    for c in range(2):
                        a = dve.scalar_tensor_tensor(out=ri[:, par, j, c, :], in0=bank[:, j, :],
                                                     scalar=strength[:, par, j * N + j:j * N + j + 1],
                                                     in1=ri[:, par, j, c, :], op0=ALU.add, op1=ALU.mult)
                    a.then_inc(part_ready, 1)

            def superpose(r, par):
                dve.wait_ge(part_ready, 4 * (r + 1))
                dve.tensor_tensor(ri[:, par, 0:2, :, :], ri[:, par, 0:2, :, :], ri[:, par, 2:4, :, :], ALU.add).then_inc(sup_step, 1)
                dve.wait_ge(sup_step, 2 * r + 1)
                dve.tensor_tensor(sup[par], sup[par], ri[:, par, 1, :, :], ALU.add).then_inc(sup_step, 1)

            def split_sup(r, par):
                cols = slice(par * P, (par + 1) * P)
                for n, (c, scale) in enumerate(((0, 1.0), (1, 1.0), (1, -1.0))):
                    dve.wait_ge(sup_hi, 3 * r + (1 if n == 0 else 3))
                    dve.scalar_tensor_tensor(out=sup_t[n][1][:, :, cols],
                                             in0=bank[:, 4 + c, :].rearrange("p (d q) -> p d q", q=P), scalar=scale,
                                             in1=sup_t[n][0][:, :, cols].bitcast(F32),
                                             op0=ALU.mult, op1=ALU.subtract).then_inc(sup_lo, 1)

            def norm_eps(q, has_before):
                dve.wait_ge(sumsq_ready, 2 * (q + 1))
                if has_before:
                    dve.wait_ge(post_step, 10 * q)
                dve.tensor_scalar(inorm[:, :], sumsq[:, :], 1e-8, None, ALU.add).then_inc(norm_step, 1)

            def norm_inv(q):
                dve.wait_ge(norm_root, q + 1)
                dve.reciprocal(inorm[:, :], inorm[:, :]).then_inc(norm_step, 1)

            def amp(q, h, has_before):
                both = rows_x[:, :, :].rearrange("p d (c q) -> p d c q", c=2)
                part = slice(2 * h, 2 * h + 2)
                if h and has_before:
                    dve.wait_ge(stored, 16 * q)
                dve.wait_ge(meas_sq, 2 * q + h + 1)
                dve.tensor_tensor(raw_t[:, part, :], both[:, :, 0, :], both[:, :, 1, :], ALU.add).then_inc(amp2_ready, 1)

            def amp_low(q, h):
                part = slice(2 * h, 2 * h + 2)
                dve.wait_ge(amp_hi, 2 * q + h + 1)
                dve.tensor_tensor(act_t[1][:, part, :], raw_t[:, part, :], act_t[0][:, part, :].bitcast(F32),
                                  ALU.subtract).then_inc(amp_lo, 1)

            def post(q):
                dve.wait_ge(consts_loaded, 64)
                dve.wait_ge(norm_step, 2 * (q + 1))
                for h in range(2):
                    dve.wait_ge(post_done, 2 * q + h + 1)
                    dve.scalar_tensor_tensor(out=rows_x[:, h, :], in0=bank[:, 6 + h, :], scalar=inorm[:, h:h + 1],
                                             in1=post_b[:, :], op0=ALU.mult, op1=ALU.add).then_inc(post_step, 1)
                for h in range(2):
                    dve.wait_ge(post_step, 10 * q + h + 1)
                    dve.bn_stats(vstats[:, h, :], rows_x[:, h, :]).then_inc(post_step, 1)
                dve.wait_ge(post_step, 10 * q + 4)
                for h in range(2):
                    dve.bn_aggr(vmean[:, h, :], vstats[:, h, :]).then_inc(post_step, 1)
                dve.wait_ge(post_step, 10 * q + 6)
                dve.tensor_scalar(vstd[:, :], vmean[:, :, 1], EPS, None, ALU.add).then_inc(post_step, 1)

            def z_rows(q):
                dve.wait_ge(std_ready, q + 1)
                dve.reciprocal(vstd[:, :], vstd[:, :]).then_inc(post_step, 1)
                dve.wait_ge(post_step, 10 * q + 8)
                for h in range(2):
                    dve.tensor_scalar(rows_x[:, h, :], rows_x[:, h, :], vmean[:, h, 0:1], vstd[:, h:h + 1],
                                      ALU.subtract, ALU.mult).then_inc(post_step, 1)

            def low(is_hi, is_lo, q):
                dve.wait_ge(is_hi, q + 1)
                dve.tensor_tensor(act_t[1][:, :, :], raw_t[:, :, :], act_t[0][:, :, :].bitcast(F32),
                                  ALU.subtract).then_inc(is_lo, 1)

            def step(p, has_tail, has_before, has_next):
                r, q = 2 * p, p - 1
                if has_tail:
                    split_sup(r - 1, 1)
                    norm_eps(q, has_before)
                newton(r)
                copy_strength(r + 1, 1)
                unit(r, 0)
                cosines(r)
                if not has_tail:
                    split.lo(dve, 2)
                    split.lo(dve, 3)
                if has_tail:
                    norm_inv(q)
                    for h in range(2):
                        amp(q, h, has_before)
                        amp_low(q, h)
                sum_squares(r + 1, False)
                if has_tail:
                    post(q)
                    z_rows(q)
                shares(r, 0)
                superpose(r, 0)
                if not has_tail:
                    split.lo(dve, 4)
                    split.lo(dve, 5)
                newton(r + 1)
                if has_tail:
                    low(z_hi, z_lo, q)
                else:
                    split.lo(dve, 6)
                    split.lo(dve, 7)
                split_sup(r, 0)
                if has_next:
                    copy_strength(r + 2, 0)
                unit(r + 1, 1)
                cosines(r + 1)
                if has_tail:
                    low(h_hi, h_lo, q)
                else:
                    split.lo(dve, 8)
                if has_next:
                    sum_squares(r + 2, False)
                shares(r + 1, 1)
                superpose(r + 1, 1)

            copy_strength(0, 0)
            sum_squares(0, True)
            split.lo(dve, 0)
            split.lo(dve, 1)
            LAST = RT // 2 - 1
            step(0, False, False, True)
            step(1, True, False, True)
            with dve.Fori(2, LAST) as p:
                step(p, True, True, True)
            step(LAST, True, True, False)
            split_sup(RT - 1, 1)
            norm_eps(LAST, True)
            norm_inv(LAST)
            for h in range(2):
                amp(LAST, h, True)
                amp_low(LAST, h)
            post(LAST)
            z_rows(LAST)
            low(z_hi, z_lo, LAST)
            low(h_hi, h_lo, LAST)


def build(nc, d, outs, upto=9):
    with ExitStack() as ctx:
        chip = Chip(nc, ctx)
        t = dict(d)
        t["tables"] = [d["tbl_0"], d["tbl_1"], d["tbl_2"], d["tbl_3"]]
        t["ident"] = chip.keep("ident", [P, P])
        t["strength"] = chip.keep("strength", [P, RT, N * N])
        t["mean_var"] = chip.keep("mean_var", [P, 2 * RT, 2])
        t["rstd"] = chip.keep("rstd", [P, 2 * RT])
        t["y"] = chip.scratch("y_scratch", (9, RT, P, 512))
        t["sT"] = chip.scratch("sT_scratch", (2, 2, NBLK, P, DT, N, BLK))
        t["y_stored"] = chip.sem("a_y_stored")
        t["y_last_stored"] = chip.sem("a_y_last_stored")
        t["y_loaded"] = [chip.sem(f"b_y_loaded{i}") for i in range(2)]
        t["s_stored"] = [chip.sem(f"b_s_stored{i}") for i in range(NB)]
        t["s_last_stored"] = chip.sem("b_s_last_stored")
        t["o_stored"] = chip.sem("c_o_stored")
        t["ri_last_stored"] = chip.sem("d_ri_last_stored")
        t["ri_stored"] = [chip.sem(f"d_ri_stored{i}") for i in range(4)]
        t["oT"] = chip.scratch("oT_scratch", (2, NBLK, P, N, 2, DT, BLK))
        t["RI"] = chip.scratch("RI_scratch", (RT, P, N, 2, 512))
        with nc.sbuf_tensor("z", [P, 2, 4, 512], F32) as z:
            t["z"] = z
            encoder_first_layer(nc, chip, t)
            encoder_second_layer(nc, chip, t)
        with nc.sbuf_tensor("ri", [P, 4, 2, 512], F32) as ri:
            t["ri"] = ri
            t["d_split"] = WeightSplit(
                chip, "d_wo", [ri[:, i, :, :].rearrange("p c f -> p (c f)") for i in range(4)],
                [(d["bv"].rearrange("p e d c -> p (e d c)"), 16)] +
                [(d["wo"][e, :, kt:kt + 2, :].rearrange("p k f -> p (k f)"), 1024)
                 for e in range(2) for kt in (0, 2)])
            attention(nc, chip, t)
            interaction_products(nc, chip, t)
        interference_and_top(nc, chip, t, outs)
        return t


def host_layout(x):
    import numpy as np

    def tiles(w):
        return w.reshape(w.shape[0] // 128, 128, w.shape[1])

    def chunks(w):
        return w.reshape(w.shape[0] // 128, 128, w.shape[1] // 512, 512).transpose(2, 0, 1, 3)

    def column(v):
        return v.reshape(-1, 128).T

    L = {k[7:]: np.asarray(v) for k, v in x.items() if k.startswith("L0_rec_")}
    d = {"ids": np.asarray(x["ids"])}
    for i in range(4):
        d[f"tbl_{i}"] = np.asarray(x[f"tbl_{i}"])
    d["xT"] = tiles(np.asarray(x["r_x"]).T)
    top1 = np.asarray(x["W_top1"])
    d["w1"] = np.concatenate([chunks(L["er_W1"].T), chunks(L["ei_W1"].T), chunks(top1[512:])])
    d["b1"] = np.concatenate([L["er_b1"], L["ei_b1"], np.asarray(x["b_top1"])]).reshape(9, 512)
    d["ln1"] = np.stack([np.stack([column(L[e + "_g1"]), column(L[e + "_be1"])], 1) for e in ("er", "ei")], 1)
    d["w2"] = np.concatenate([chunks(L["er_W2"].T), chunks(L["ei_W2"].T)])
    d["b2"] = np.concatenate([column(L["er_b2"]), column(L["ei_b2"])], 1)

    def rows(w):
        return w.reshape(w.shape[0] // 128, 128, w.shape[1]).transpose(1, 0, 2)

    names = ("q_r", "k_r", "q_i", "k_i", "v_r", "v_i")
    d["wqkv"] = np.stack([rows(L["W" + m].T) for m in names])
    d["bqk"] = np.stack([column(L["b" + m]) for m in names[:4]], 1)


    def crossed(w):
        return w.reshape(4, 2, 64, -1)[:, ::-1].reshape(w.shape)

    d["wo"] = np.stack([rows(L["Wo_r"].T), rows(crossed(L["Wo_i"].T))])
    bv = np.stack([column(L["bv_r"]), column(crossed(L["bv_i"]))], 1)
    d["bv"] = np.repeat(bv[..., None], 2, -1)
    d["bo"] = np.stack([column(L["bo_r"]), column(L["bo_i"])], 1)
    wint = np.stack([L["int_Wr"], L["int_Wi"]], 1).transpose(0, 1, 3, 2)
    d["wint"] = wint.reshape(4, 2, 4, 128, 512).transpose(0, 3, 1, 2, 4)
    d["wm"] = np.stack([rows(L["meas_Mr"].T), rows(L["meas_Mi"].T)])
    d["wp"] = rows(L["post_W"].T)
    d["wt1"] = rows(top1[:512])
    d["wt2"] = rows(np.asarray(x["W_top2"]))
    d["post_b"] = L["post_b"]
    d["post_ln"] = np.stack([column(L["post_g"]), column(L["post_be"])], 1)
    d["top_b2"] = column(np.asarray(x["b_top2"]))
    d["top_w3"] = column(np.asarray(x["W_top3"]))
    return {k: np.ascontiguousarray(v) for k, v in d.items()}


def kernel(**inputs):
    import concourse.bacc as bacc
    from concourse.bass_utils import run_bass_kernel_spmd

    arrays = host_layout(inputs)
    nc = bacc.Bacc("TRN2", target_bir_lowering=False, num_devices=1)
    d = {n: nc.dram_tensor("in_" + n, a.shape, mybir.dt.from_np(a.dtype), kind="ExternalInput").ap()
         for n, a in arrays.items()}
    out = nc.dram_tensor("out_0_dram", (B, 1), F32, kind="ExternalOutput").ap()
    build(nc, d, out)
    r = run_bass_kernel_spmd(nc, [{"in_" + n: a for n, a in arrays.items()}], core_ids=[0])
    return r.results[0]["out_0_dram"]
```
